# Optimizing a Trainium2 kernel written in Bass

```python
import numpy as np
import jax
import jax.numpy as jnp

def _softmax(x, axis=-1):
    return jax.nn.softmax(x, axis=axis)

def _gelu(x):
    return jax.nn.gelu(x, approximate=True)

def _silu(x):
    return jax.nn.silu(x)

def _sigmoid(x):
    return jax.nn.sigmoid(x)

def _layernorm(x, axis=-1, eps=1e-05):
    m = jnp.mean(x, axis=axis, keepdims=True)
    v = jnp.var(x, axis=axis, keepdims=True)
    return (x - m) / jnp.sqrt(v + eps)

def _scatter_add(tgt, idx, src, axis=0):
    return tgt.at[idx].add(src)

def _segment_sum(src, seg, n):
    return jax.ops.segment_sum(src, seg, n)
kernel_name = 'mk_perceiver_d1_seqx_r4_0a1b65'

def setup_inputs(seed: int=0):
    np.random.seed(seed)
    _w = jnp.asarray

    def _rec_inputs():
        import jax
        import jax.numpy as jnp
        _rk = jax.random.key(seed)
        x = -9.806e-05 + 1 * jax.random.normal(jax.random.fold_in(_rk, 1), (8, 64, 256), jnp.float32)
        _lenS = 64 - jax.random.randint(jax.random.fold_in(_rk, 7), (8,), 0, max(1, 64 // 4) + 1, jnp.int32)
        _lenS2 = 1601 - jax.random.randint(jax.random.fold_in(_rk, 8), (8,), 0, max(1, 1601 // 4) + 1, jnp.int32)
        _ctx_1024P = jax.random.normal(jax.random.fold_in(_rk, 11), (8, 16, 256), jnp.float32)
        _ctx_1024c = jax.random.dirichlet(jax.random.fold_in(_rk, 511), 0.3 * jnp.ones((16,), jnp.float32), (8, 1601))
        _ctx_1024t = jnp.einsum('bsk,bkd->bsd', _ctx_1024c, _ctx_1024P)
        _ctx_1024t = _ctx_1024t * jax.lax.rsqrt(jnp.mean(jnp.square(_ctx_1024t)) + 1e-12) * 0.953939
        ctx_1024 = -1.52775e-05 + 0.999936 * (_ctx_1024t + 0.3 * jax.random.normal(jax.random.fold_in(_rk, 611), (8, 1601, 256), jnp.float32))
        return (x, ctx_1024)
    x, ctx_1024 = _rec_inputs()

    def _L0_xattn_setup():
        import jax, jax.numpy as jnp
        import numpy as np
        D = 256
        NUM_ITERS = 3
        EPS = 1e-06
        SCALE = D ** (-0.5)

        def rmsnorm(x, w, eps=EPS):
            return x * jax.lax.rsqrt(jnp.mean(x * x, axis=-1, keepdims=True) + eps) * w

        def gru_cell(x, h, wih, whh, bih, bhh):
            gx = x @ wih.T + bih
            gh = h @ whh.T + bhh
            xr, xz, xn = jnp.split(gx, 3, axis=-1)
            hr, hz, hn = jnp.split(gh, 3, axis=-1)
            r = jax.nn.sigmoid(xr + hr)
            z = jax.nn.sigmoid(xz + hz)
            n = jnp.tanh(xn + r * hn)
            return (1.0 - z) * n + z * h
        key = jax.random.key(seed)
        ks = jax.random.split(key, 8)
        B, K, M, d = (8, 64, 1024, D)
        w_std = d ** (-0.5)
        return {'slots': jax.random.normal(ks[0], (B, K, d), jnp.float32), 'P': jax.random.normal(ks[1], (B, M, d), jnp.float32), 'Wq': jax.random.normal(ks[2], (d, d), jnp.float32) * w_std, 'Wk': jax.random.normal(ks[3], (d, d), jnp.float32) * w_std, 'Wv': jax.random.normal(ks[4], (d, d), jnp.float32) * w_std, 'gru_wih': jax.random.normal(ks[5], (3 * d, d), jnp.float32) * w_std, 'gru_whh': jax.random.normal(ks[6], (3 * d, d), jnp.float32) * w_std, 'gru_bih': jnp.zeros((3 * d,), jnp.float32), 'gru_bhh': jnp.zeros((3 * d,), jnp.float32), 'slot_norm_w': jnp.ones((d,), jnp.float32), 'input_norm_w': jnp.ones((d,), jnp.float32)}
    _L0_xattn_all = _L0_xattn_setup()
    _L0_xattn_in = {k: v for k, v in _L0_xattn_all.items() if k in ('Wq', 'Wk', 'Wv', 'gru_wih', 'gru_whh', 'gru_bih', 'gru_bhh', 'slot_norm_w', 'input_norm_w')}
    del _L0_xattn_all

    def _L0_attn_setup():
        import jax, jax.numpy as jnp
        import numpy as np
        HEADS = 16
        DIM_HEAD = 64
        T_MAX = DIM_HEAD

        def _cope(q, sim, pos_emb):
            G = jax.nn.sigmoid(sim)
            P = jnp.flip(jnp.cumsum(jnp.flip(G, axis=-1), axis=-1), axis=-1)
            P = jnp.minimum(P, T_MAX - 1)
            P_floor = jnp.floor(P)
            P_ceil_i = jnp.ceil(P).astype(jnp.int32)
            P_floor_i = P_floor.astype(jnp.int32)
            E = jnp.einsum('bnc,ct->bnt', q, pos_emb)
            E_ceil = jnp.take_along_axis(E, P_ceil_i, axis=-1)
            E_floor = jnp.take_along_axis(E, P_floor_i, axis=-1)
            w = P - P_floor
            return w * E_ceil + (1.0 - w) * E_floor
        key = jax.random.key(seed)
        ks = jax.random.split(key, 6)
        B, N, D = (1, 512, 256)
        inner = HEADS * DIM_HEAD
        return {'x': jax.random.normal(ks[0], (B, N, D), dtype=jnp.float32), 'Wq': jax.random.normal(ks[1], (D, inner), dtype=jnp.float32) * 0.02, 'Wkv': jax.random.normal(ks[2], (D, 2 * inner), dtype=jnp.float32) * 0.02, 'Wout': jax.random.normal(ks[3], (inner, D), dtype=jnp.float32) * 0.02, 'b_out': jnp.zeros((D,), dtype=jnp.float32), 'pos_emb': jax.random.normal(ks[4], (DIM_HEAD, T_MAX), dtype=jnp.float32) * 0.02}
    _L0_attn_all = _L0_attn_setup()
    _L0_attn_in = {k: v for k, v in _L0_attn_all.items() if k in ('Wq', 'Wkv', 'Wout', 'b_out', 'pos_emb')}
    del _L0_attn_all

    def _L0_ffn_setup():
        import jax, jax.numpy as jnp
        import numpy as np
        FF_DIM = 512
        TOP_K = 2
        key = jax.random.key(seed)
        k1, k2, k3, k4 = jax.random.split(key, 4)
        B, S, D, E, F = (2, 512, 256, 8, FF_DIM)
        std = 0.006
        return {'x': jax.random.normal(k1, (B, S, D), dtype=jnp.float32), 'gate_w': jax.random.normal(k2, (D, E), dtype=jnp.float32) * 0.02, 'gate_up_w': jax.random.normal(k3, (E, D, 2 * F), dtype=jnp.float32) * std, 'down_w': jax.random.normal(k4, (E, F, D), dtype=jnp.float32) * std}
    _L0_ffn_all = _L0_ffn_setup()
    _L0_ffn_in = {k: v for k, v in _L0_ffn_all.items() if k in ('gate_w', 'gate_up_w', 'down_w')}
    del _L0_ffn_all
    return {'x': x, 'ctx_1024': ctx_1024, 'L0_xattn_Wq': _L0_xattn_in['Wq'], 'L0_xattn_Wk': _L0_xattn_in['Wk'], 'L0_xattn_Wv': _L0_xattn_in['Wv'], 'L0_xattn_gru_wih': _L0_xattn_in['gru_wih'], 'L0_xattn_gru_whh': _L0_xattn_in['gru_whh'], 'L0_xattn_gru_bih': _L0_xattn_in['gru_bih'], 'L0_xattn_gru_bhh': _L0_xattn_in['gru_bhh'], 'L0_xattn_slot_norm_w': _L0_xattn_in['slot_norm_w'], 'L0_xattn_input_norm_w': _L0_xattn_in['input_norm_w'], 'L0_attn_Wq': _L0_attn_in['Wq'], 'L0_attn_Wkv': _L0_attn_in['Wkv'], 'L0_attn_Wout': _L0_attn_in['Wout'], 'L0_attn_b_out': _L0_attn_in['b_out'], 'L0_attn_pos_emb': _L0_attn_in['pos_emb'], 'L0_ffn_gate_w': _L0_ffn_in['gate_w'], 'L0_ffn_gate_up_w': _L0_ffn_in['gate_up_w'], 'L0_ffn_down_w': _L0_ffn_in['down_w']}

def reference(x, ctx_1024, L0_xattn_Wq, L0_xattn_Wk, L0_xattn_Wv, L0_xattn_gru_wih, L0_xattn_gru_whh, L0_xattn_gru_bih, L0_xattn_gru_bhh, L0_xattn_slot_norm_w, L0_xattn_input_norm_w, L0_attn_Wq, L0_attn_Wkv, L0_attn_Wout, L0_attn_b_out, L0_attn_pos_emb, L0_ffn_gate_w, L0_ffn_gate_up_w, L0_ffn_down_w):
    import jax
    import jax.numpy as jnp

    def _L0_xattn_ref(slots, P, Wq, Wk, Wv, gru_wih, gru_whh, gru_bih, gru_bhh, slot_norm_w, input_norm_w):
        import jax, jax.numpy as jnp
        import numpy as np
        D = 256
        NUM_ITERS = 3
        EPS = 1e-06
        SCALE = D ** (-0.5)

        def rmsnorm(x, w, eps=EPS):
            return x * jax.lax.rsqrt(jnp.mean(x * x, axis=-1, keepdims=True) + eps) * w

        def gru_cell(x, h, wih, whh, bih, bhh):
            gx = x @ wih.T + bih
            gh = h @ whh.T + bhh
            xr, xz, xn = jnp.split(gx, 3, axis=-1)
            hr, hz, hn = jnp.split(gh, 3, axis=-1)
            r = jax.nn.sigmoid(xr + hr)
            z = jax.nn.sigmoid(xz + hz)
            n = jnp.tanh(xn + r * hn)
            return (1.0 - z) * n + z * h
        Pn = rmsnorm(P, input_norm_w)
        k_proj = Pn @ Wk.T
        v_proj = Pn @ Wv.T
        for _ in range(NUM_ITERS):
            sn = rmsnorm(slots, slot_norm_w)
            q_proj = sn @ Wq.T
            scores = jnp.einsum('bkd,bmd->bkm', q_proj, k_proj) * SCALE
            attn = jax.nn.softmax(scores, axis=-2)
            attn = attn / (jnp.sum(attn, axis=-1, keepdims=True) + EPS)
            updates = jnp.einsum('bkm,bmd->bkd', attn, v_proj)
            slots = gru_cell(updates, slots, gru_wih, gru_whh, gru_bih, gru_bhh)
        return slots

    def _L0_attn_ref(x, Wq, Wkv, Wout, b_out, pos_emb):
        import jax, jax.numpy as jnp
        import numpy as np
        HEADS = 16
        DIM_HEAD = 64
        T_MAX = DIM_HEAD

        def _cope(q, sim, pos_emb):
            G = jax.nn.sigmoid(sim)
            P = jnp.flip(jnp.cumsum(jnp.flip(G, axis=-1), axis=-1), axis=-1)
            P = jnp.minimum(P, T_MAX - 1)
            P_floor = jnp.floor(P)
            P_ceil_i = jnp.ceil(P).astype(jnp.int32)
            P_floor_i = P_floor.astype(jnp.int32)
            E = jnp.einsum('bnc,ct->bnt', q, pos_emb)
            E_ceil = jnp.take_along_axis(E, P_ceil_i, axis=-1)
            E_floor = jnp.take_along_axis(E, P_floor_i, axis=-1)
            w = P - P_floor
            return w * E_ceil + (1.0 - w) * E_floor
        B, N, D = x.shape
        h, d = (HEADS, DIM_HEAD)
        scale = d ** (-0.5)
        q = x @ Wq
        kv = x @ Wkv
        k, v = jnp.split(kv, 2, axis=-1)

        def to_heads(t):
            return t.reshape(B, N, h, d).transpose(0, 2, 1, 3).reshape(B * h, N, d)
        q, k, v = (to_heads(q), to_heads(k), to_heads(v))
        sim = jnp.einsum('bid,bjd->bij', q, k) * scale
        sim = sim + _cope(q, sim, pos_emb)
        attn = jax.nn.softmax(sim, axis=-1)
        out = jnp.einsum('bij,bjd->bid', attn, v)
        out = out.reshape(B, h, N, d).transpose(0, 2, 1, 3).reshape(B, N, h * d)
        return out @ Wout + b_out

    def _L0_ffn_ref(x, gate_w, gate_up_w, down_w):
        import jax, jax.numpy as jnp
        import numpy as np
        FF_DIM = 512
        TOP_K = 2
        B, S, D = x.shape
        E = gate_up_w.shape[0]
        F = down_w.shape[1]
        x_flat = x.reshape(B * S, D)
        router_logits = x_flat @ gate_w
        router_probs = jax.nn.softmax(router_logits, axis=-1)
        top_k_probs, top_k_idx = jax.lax.top_k(router_probs, TOP_K)
        top_k_probs = top_k_probs / jnp.sum(top_k_probs, axis=-1, keepdims=True)
        gate_up = jnp.einsum('nd,edh->enh', x_flat, gate_up_w)
        gate_out = gate_up[..., :F]
        up_out = gate_up[..., F:]
        hidden = jax.nn.silu(gate_out) * up_out
        expert_out = jnp.einsum('enf,efd->end', hidden, down_w)
        out_t = jnp.transpose(expert_out, (1, 0, 2))
        sel = jnp.take_along_axis(out_t, top_k_idx[:, :, None], axis=1)
        output = jnp.sum(sel * top_k_probs[:, :, None], axis=1)
        return output.reshape(B, S, D)
    x = x + _L0_xattn_ref(_layernorm(x, axis=-1), ctx_1024, L0_xattn_Wq, L0_xattn_Wk, L0_xattn_Wv, L0_xattn_gru_wih, L0_xattn_gru_whh, L0_xattn_gru_bih, L0_xattn_gru_bhh, L0_xattn_slot_norm_w, L0_xattn_input_norm_w)
    x = x + _L0_attn_ref(_layernorm(x, axis=-1), L0_attn_Wq, L0_attn_Wkv, L0_attn_Wout, L0_attn_b_out, L0_attn_pos_emb)
    x = x + _L0_ffn_ref(_layernorm(x, axis=-1), L0_ffn_gate_w, L0_ffn_gate_up_w, L0_ffn_down_w)
    return x

_drawn_inputs = setup_inputs


def setup_inputs(seed=0):
    import zlib

    import numpy as np

    out = dict(_drawn_inputs(seed))
    spreads = {'L0_xattn_gru_bih': (0.0, 0.1),
     'L0_xattn_gru_bhh': (0.0, 0.1),
     'L0_xattn_slot_norm_w': (1.0, 0.6),
     'L0_xattn_input_norm_w': (1.0, 0.2),
     'L0_attn_b_out': (0.0, 0.1)}
    factors = {'L0_attn_Wq': 8.0,
     'L0_attn_pos_emb': 8.0,
     'L0_ffn_gate_w': 8.0,
     'L0_ffn_gate_up_w': 8.0,
     'L0_ffn_down_w': 8.0}
    for name, (base, spread) in spreads.items():
        noise = np.random.default_rng([zlib.crc32(name.encode()), seed]).standard_normal(out[name].shape)
        drawn = base * np.exp(spread * noise) if base else spread * noise
        out[name] = jnp.asarray(drawn.astype(out[name].dtype))
    for name, factor in factors.items():
        out[name] = (out[name] * factor).astype(out[name].dtype)
    return out
```

```python
from contextlib import ExitStack

import concourse.bass as bass
from concourse import mybir

ALU = mybir.AluOpType
ACT = mybir.ActivationFunctionType
AX_X = mybir.AxisListType.X
F32 = mybir.dt.float32
F16 = mybir.dt.float16
I32 = mybir.dt.int32

P = 128
WS = 64.0
AS = 1024.0
MAGIC = 12582912.0
PASSES = ((0, 0), (1, 0), (0, 1))


ONE = 1


def credit(eng, *sems):
    for s in sems:
        eng.sem_inc(s, ONE)


class Count:

    def __init__(self, base, per):
        self.base, self.per, self.n = base * per if per else 0, per, 0

    def next(self, by=1):
        self.n += by
        return self.base + self.n

    def done(self):
        assert self.n == self.per, (self.n, self.per)


def perceiver_kernel(nc, x, ctx_1024, xWq, xWk, xWv, wih, whh, bih, bhh, slot_w, input_w,
                     aWq, aWkv, aWout, ab_out, pos_emb, gate_w, gate_up_w, down_w, out):
    B, N, D = x.shape
    M = ctx_1024.shape[1]
    C = D // P
    PAIRS = B * N // P
    MR = M // P
    MT = MR + 1
    TAIL = M - MR * P
    G = 3 * D
    XW = D + 2
    GROUPS = PAIRS // 2
    H = aWq.shape[1] // N
    DH = pos_emb.shape[0]
    HP = H // 2
    V1 = N + 1
    E = gate_up_w.shape[0]
    F = down_w.shape[1]
    FC = F // P
    TOK = B * N

    with ExitStack() as ctx:
        def sb(name, shape, dt, on=ctx):
            return on.enter_context(nc.sbuf_tensor(name, shape, dt))

        def sem(name):
            return ctx.enter_context(nc.semaphore(name))

        bank = ctx.enter_context(nc.psum_tensor("bank", [P, 8, 512], F32))
        bank16 = bank[:].bitcast(F16)
        x_sb = sb("x_sb", [P, PAIRS, D], F32)
        ident = sb("ident", [P, P], F32)
        ident16 = sb("ident16", [P, P], F16)
        flip16 = sb("flip16", [P, P], F16)
        stats = sb("stats", [P, PAIRS, 6], F32)
        mv = sb("mv", [P, PAIRS, 2], F32)
        half = sb("half", [P, 16], F32)
        lnr = sb("lnr", [P, PAIRS], F32)
        deps = sb("deps", [P, 16], F32)

        phase1 = ctx.enter_context(ExitStack())
        s0 = sb("s0", [P, PAIRS, D], F32, phase1)
        A16 = sb("A16", [P, 2, C, D], F16, phase1)
        wihT16 = sb("wihT16", [P, 2, C, G], F16, phase1)
        whhT16 = sb("whhT16", [P, 2, C, G], F16, phase1)
        brz = sb("brz", [P, 2 * D], F32, phase1)
        bxn = sb("bxn", [P, D], F32, phase1)
        bhn = sb("bhn", [P, D], F32, phase1)

        load = sem("load")
        made = sem("made")
        folded = sem("folded")
        lv = sem("lv")
        lp = sem("lp")
        la = sem("la")
        pe0 = sem("pe0")
        ev0 = sem("ev0")
        rs0 = sem("rs0")
        mv0 = sem("mv0")
        hi0 = sem("hi0")
        with ExitStack() as p0:
            w3 = sb("w3", [P, 3, C, D], F32, p0)
            wg = sb("wg", [P, 2, G // P, D], F32, p0)
            wgT = sb("wgT", [P, 2, C, G], F32, p0)
            fold = sb("fold", [P, C, G], F32, p0)
            A32 = sb("A32", [P, C, D], F32, p0)
            swc = sb("swc", [P, C], F32, p0)
            iwc = sb("iwc", [P, C], F32, p0)
            iwb = sb("iwb", [P, D], F32, p0)
            bb = sb("bb", [P, 2, G], F32, p0)
            block = p0.enter_context(nc.Block())
            LOADS = 0

            @block.sync
            def _(sp):
                sp.dma_start(x_sb[:], x.rearrange("b k d -> (b k) d").rearrange("(q p) d -> p q d", p=P)).then_inc(load, 16)
                for i, w in enumerate((xWq, xWk, xWv)):
                    sp.dma_start(w3[:, i], w.rearrange("(c p) n -> p c n", p=P)).then_inc(load, 16)
                for i, w in enumerate((wih, whh)):
                    sp.dma_start(wg[:, i], w.rearrange("(c p) n -> p c n", p=P)).then_inc(load, 16)
                    b = (bih, bhh)[i]
                    sp.dma_start(bb[:, i], b.rearrange("(a n) -> a n", a=1).broadcast_to([P, G])).then_inc(load, 16)
                sp.dma_start(swc[:], slot_w.rearrange("(c p) -> p c", p=P),
                             allow_slow_non_contiguous=True).then_inc(load, 16)
                sp.dma_start(iwc[:], input_w.rearrange("(c p) -> p c", p=P),
                             allow_slow_non_contiguous=True).then_inc(load, 16)
                sp.dma_start(iwb[:], input_w.rearrange("(a n) -> a n", a=1).broadcast_to([P, D])).then_inc(load, 16)

            ALL = 11 * 16

            @block.gpsimd
            def _(pool):
                pool.memset(deps[:], D * 1e-6)
                pool.memset(half[:], -0.5).then_inc(made, 1)
                pool.memset(ident[:], 0.0).then_inc(made, 1)
                pool.memset(flip16[:], 0.0).then_inc(made, 1)
                pool.wait_ge(made, 3)
                pool.affine_select(out=ident[:], in_=ident[:], compare_op=ALU.not_equal, fill=1.0,
                                   base=0, pattern=[[-1, P]], channel_multiplier=1).then_inc(made, 1)
                for b in range(2):
                    part = flip16[:, b * N:(b + 1) * N]
                    pool.affine_select(out=part, in_=part, compare_op=ALU.not_equal, fill=1.0,
                                       base=-(N - 1) - b * N, pattern=[[1, N]],
                                       channel_multiplier=1).then_inc(made, 1)
                pool.wait_ge(made, 4)
                pool.tensor_copy(ident16[:], ident[:]).then_inc(made, 1)
                pool.wait_ge(mv0, 1)
                pool.tensor_scalar(lnr[:], mv[:, :, 1], 1.0, 1e-5, ALU.mult, ALU.add).then_inc(lp, 1)
                pool.wait_ge(lp, 1)
                pool.tensor_tensor(lnr[:], lnr[:], half[:, 0:PAIRS], ALU.pow).then_inc(rs0, 1)

            @block.tensor
            def _(pe):
                pe.wait_ge(load, ALL)
                pe.wait_ge(made, 7)
                for d in range(C):
                    for o in range(C):
                        last = pe.matmul(bank[:, d, 0:D], w3[:, 0, o, d * P:(d + 1) * P], w3[:, 1, o, :],
                                         start=(o == 0), stop=(o == C - 1))
                last.then_inc(pe0, 1)
                for i in range(2):
                    for c in range(C):
                        for half_ in range(2):
                            b = 2 + (i * C + c) * 2 + half_
                            if b >= 8:
                                b -= 6
                                pe.wait_ge(ev0, b)
                            for t in range(3):
                                g = half_ * 3 + t
                                last = pe.transpose(bank[:, b, t * P:(t + 1) * P],
                                                    wg[:, i, g, c * P:(c + 1) * P], ident[:])
                            last.then_inc(pe0, 1)
                pe.wait_ge(ev0, 9)
                for e in range(C):
                    for n0, n1 in ((0, 512), (512, G)):
                        for o in range(C):
                            last = pe.matmul(bank[:, 4 + 2 * e + n0 // 512, 0:n1 - n0],
                                             w3[:, 2, o, e * P:(e + 1) * P], wgT[:, 0, o, n0:n1],
                                             start=(o == 0), stop=(o == C - 1))
                last.then_inc(pe0, 1)

            @block.scalar
            def _(act):
                act.wait_ge(ev0, 1)
                act.activation(A16[:, 0], A32[:], ACT.Copy).then_inc(hi0, 1)
                act.wait_ge(ev0, 9)
                act.activation(whhT16[:, 0], wgT[:, 1], ACT.Copy, scale=WS).then_inc(hi0, 1)
                act.wait_ge(ev0, 10)
                act.activation(wihT16[:, 0], fold[:], ACT.Copy).then_inc(hi0, 1)

            @block.vector
            def _(dve):
                dve.wait_ge(load, ALL)
                for q in range(PAIRS):
                    dve.bn_stats(stats[:, q, :], x_sb[:, q, :]).then_inc(lv, 1)
                for q in range(PAIRS):
                    dve.wait_ge(lv, q + 1)
                    ins = dve.bn_aggr(mv[:, q, :], stats[:, q, :])
                    ins.then_inc(la, 1)
                dve.wait_ge(la, PAIRS)
                dve.tensor_copy(stats[:, :, 0:2], mv[:]).then_inc(mv0, 1)
                dve.tensor_tensor(brz[:], bb[:, 0, 0:2 * D], bb[:, 1, 0:2 * D], ALU.add).then_inc(folded, 1)
                dve.tensor_copy(bxn[:], bb[:, 0, 2 * D:G]).then_inc(folded, 1)
                dve.tensor_copy(bhn[:], bb[:, 1, 2 * D:G]).then_inc(folded, 1)
                dve.wait_ge(pe0, 1)
                for d in range(C):
                    ins = dve.scalar_tensor_tensor(A32[:, d], bank[:, d, 0:D], swc[:, d:d + 1], iwb[:],
                                                   ALU.mult, ALU.mult)
                ins.then_inc(lv, 1)
                dve.wait_ge(lv, PAIRS + 1)
                dve.tensor_scalar(A32[:], A32[:], WS, None, ALU.mult).then_inc(ev0, 1)
                for i in range(2):
                    for c in range(C):
                        for half_ in range(2):
                            k = (i * C + c) * 2 + half_
                            b = 2 + k if k < 6 else 2 + k - 6
                            dve.wait_ge(pe0, 2 + k)
                            dve.tensor_copy(wgT[:, i, c, half_ * 3 * P:(half_ + 1) * 3 * P],
                                            bank[:, b, 0:3 * P]).then_inc(ev0, 1)
                dve.wait_ge(pe0, 10)
                for e in range(C):
                    for n0, n1 in ((0, 512), (512, G)):
                        ins = dve.tensor_scalar(fold[:, e, n0:n1], bank[:, 4 + 2 * e + n0 // 512, 0:n1 - n0],
                                                iwc[:, e:e + 1], WS, ALU.mult, ALU.mult)
                ins.then_inc(ev0, 1)
                dve.wait_ge(hi0, 1)
                dve.tensor_tensor(A16[:, 1], A32[:], A16[:, 0], ALU.subtract).then_inc(folded, 1)
                dve.wait_ge(hi0, 2)
                dve.scalar_tensor_tensor(whhT16[:, 1].rearrange("p c n -> p (c n)"),
                                         wgT[:, 1].rearrange("p c n -> p (c n)"), WS,
                                         whhT16[:, 0].rearrange("p c n -> p (c n)"),
                                         ALU.mult, ALU.subtract).then_inc(folded, 1)
                dve.wait_ge(hi0, 3)
                dve.wait_ge(ev0, 10)
                dve.tensor_tensor(wihT16[:, 1], fold[:], wihT16[:, 0], ALU.subtract).then_inc(folded, 1)
                dve.wait_ge(rs0, 1)
                dve.wait_ge(mv0, 1)
                for q in range(PAIRS):
                    dve.tensor_scalar(s0[:, q], x_sb[:, q], mv[:, q, 0:1], lnr[:, q:q + 1],
                                      ALU.subtract, ALU.mult).then_inc(folded, 1)

        from_stage = phase1
        X32 = sb("X32", [P, 2, MT, D], F32, from_stage)
        XN = sb("XN", [P, 2, 2, MT, 2, XW], F16, from_stage)
        XT = sb("XT", [P, 2, 2, MT, 4, P], F16, from_stage)
        ssq = sb("ssq", [P, 2, MT], F32, from_stage)
        rinv = sb("rinv", [P, 2, MT], F32, from_stage)
        junk = sb("junk", [P, MT, D], F16, from_stage)
        mx = sb("mx", [P, 2, MT], F32, from_stage)
        sm = sb("sm", [P, 2, MT], F32, from_stage)
        e32 = sb("e32", [P, 2, MT, N], F32, from_stage)
        at16 = sb("at16", [P, 2, 2, MT, N], F16, from_stage)
        h32 = sb("h32", [P, 2, D], F32, from_stage)
        hT16 = sb("hT16", [P, 2, 8, P], F16, from_stage)
        hs16 = sb("hs16", [P, 2, 2, D], F16, from_stage)
        sn32 = sb("sn32", [P, D], F32, from_stage)
        qT16 = sb("qT16", [P, 2, 2, C, P], F16, from_stage)
        ssq1 = sb("ssq1", [P, 2], F32, from_stage)
        r1 = sb("r1", [P, 2], F32, from_stage)
        urs = sb("urs", [P, 2], F32, from_stage)
        upd = sb("upd", [P, D], F32, from_stage)
        upd16 = sb("upd16", [P, 2, D], F16, from_stage)
        uT16 = sb("uT16", [P, 4, P], F16, from_stage)
        rz = sb("rz", [P, 2 * D], F32, from_stage)
        cand = sb("cand", [P, D], F32, from_stage)
        xn_ = sb("xn_", [P, D], F32, from_stage)

        SC = [bank[:, 2 * k:2 * k + 2, :].rearrange("p b n -> p (b n)") for k in range(2)]
        SC16 = [bank16[:, 2 * k:2 * k + 2, :].rearrange("p b n -> p (b n)") for k in range(2)]
        U = bank[:, 4, :]
        T16, TQ = bank16[:, 5, :], bank[:, 5, :]
        RZ, NB = bank[:, 6, :], bank[:, 7, :]

        loaded = [sem(f"loaded{i}") for i in range(2)]
        stage_read = sem("stage_read")
        sq_done = sem("sq_done")
        rinv_ready = sem("rinv_ready")
        scaled = sem("scaled")
        xhi_done = sem("xhi_done")
        slot_full = sem("slot_full")
        slot_free = sem("slot_free")
        q_full = sem("q_full")
        exp_done = sem("exp_done")
        at32_done = sem("at32_done")
        athi_done = sem("athi_done")
        atlo_done = sem("atlo_done")
        u_done = sem("u_done")
        u_free = sem("u_free")
        updhi_done = sem("updhi_done")
        updlo_done = sem("updlo_done")
        t_full = sem("t_full")
        t_free = sem("t_free")
        gates_done = sem("gates_done")
        gates_free = sem("gates_free")
        rz_sum = sem("rz_sum")
        rz_tanh = sem("rz_tanh")
        n_sum = sem("n_sum")
        n_tanh = sem("n_tanh")
        h_ready = sem("h_ready")
        ssq1_done = sem("ssq1_done")
        hhi_done = sem("hhi_done")
        r1_ready = sem("r1_ready")
        sn_ready = sem("sn_ready")
        snhi_done = sem("snhi_done")
        hslo_done = sem("hslo_done")
        qhi_done = sem("qhi_done")
        q_ready = sem("q_ready")
        pool_step = sem("pool_step")
        dve_step = sem("dve_step")

        HS = 6
        TUSES = 2 * HS
        SLOTS = 4 * 4 + 2 * HS
        ctx_main = ctx_1024[:, 0:MR * P, :].rearrange("b (p t) d -> b p t d", t=MR)
        ctx_tail = ctx_1024[:, MR * P:M, :]

        def order(prep, fin, gru, att):
            for q in (0, 1):
                prep(q)
            fin(0)
            att(0, None)
            for q in (2, 3):
                prep(q)
            fin(1)
            for h in range(1, HS):
                att(h, h - 1)
                if h + 1 < HS:
                    fin(h + 1)
            gru(HS - 1)

        with ExitStack() as p1:
            block = p1.enter_context(nc.Block())

            @block.sync
            def _(sp):
                with sp.Fori(0, GROUPS) as g:
                    for q in range(4):
                        sp.wait_ge(stage_read, g * 4 + q + 1)
                        sp.dma_start(X32[:, q % 2, 0:MR, :], ctx_main[g * 4 + q]).then_inc(loaded[q % 2], 16)
                        sp.dma_start(X32[0:TAIL, q % 2, MR, :], ctx_tail[g * 4 + q]).then_inc(loaded[q % 2], 16)

            @block.gpsimd
            def _(pool):
                credit(pool, rinv_ready, atlo_done)
                for q in range(2):
                    pool.memset(X32[:, q, MR, :], 0.0).then_inc(stage_read, 1)
                with pool.Fori(0, GROUPS) as g:
                    step = Count(g, 4 + HS)
                    prepped = Count(g, 4)
                    lo = Count(g, 2 * HS)
                    fins = Count(g, HS)

                    def prep(q):
                        n = prepped.next()
                        pool.wait_ge(sq_done, n + ONE)
                        pool.tensor_tensor(rinv[:, q % 2], ssq[:, q % 2], deps[:, 0:MT],
                                           ALU.add).then_inc(pool_step, 1)
                        pool.wait_ge(pool_step, step.next())
                        pool.tensor_tensor(rinv[:, q % 2], rinv[:, q % 2], half[:, 0:MT],
                                           ALU.pow).then_inc(rinv_ready, 1)

                    def att(h, prev):
                        for j in range(2):
                            n = lo.next()
                            pool.wait_ge(at32_done, n)
                            pool.wait_ge(athi_done, n)
                            if h > 0:
                                pool.wait_ge(u_done, n - 2)
                            pool.tensor_tensor(at16[:, j, 1], e32[:, j], at16[:, j, 0],
                                               ALU.subtract).then_inc(atlo_done, 1)

                    def fin(f):
                        pool.wait_ge(ssq1_done, fins.next())
                        pool.tensor_tensor(r1[:, f % 2:f % 2 + 1], ssq1[:, f % 2:f % 2 + 1], deps[:, 0:1],
                                           ALU.add).then_inc(pool_step, 1)
                        pool.wait_ge(pool_step, step.next())
                        pool.tensor_tensor(r1[:, f % 2:f % 2 + 1], r1[:, f % 2:f % 2 + 1], half[:, 0:1],
                                           ALU.pow).then_inc(r1_ready, 1)

                    order(prep, fin, lambda h: None, att)
                    for c in (step, prepped, lo, fins):
                        c.done()

            @block.scalar
            def _(act):
                credit(act, sq_done)
                with act.Fori(0, GROUPS) as g:
                    prepped = Count(g, 4)
                    slots = Count(g, SLOTS)
                    exps = Count(g, 2 * HS)
                    his = Count(g, 2 * HS)
                    grus = Count(g, HS)
                    fins = Count(g, HS)

                    def prep(q):
                        n = prepped.next()
                        slots.next(4)
                        act.wait_ge(loaded[q % 2], (g * 2 + q // 2) * 32 + 32)
                        if q >= 2:
                            act.wait_ge(rinv_ready, n - 2 + ONE)
                        else:
                            act.wait_ge(rinv_ready, g * 4 + ONE)
                        act.wait_ge(sq_done, n - 1 + ONE)
                        for t in range(MT):
                            ins = act.activation(junk[:, t, :], X32[:, q % 2, t, :], ACT.Square,
                                                 accum_out=ssq[:, q % 2, t:t + 1])
                        ins.then_inc(sq_done, 1)
                        act.wait_ge(scaled, n)
                        act.wait_ge(h_ready, g * 8 + ONE)
                        act.activation(XN[:, q // 2, q % 2, :, 0, 0:D], X32[:, q % 2],
                                       ACT.Copy).then_inc(xhi_done, 1)

                    def att(h, prev):
                        if prev is not None:
                            n = grus.next()
                            act.wait_ge(u_free, n + ONE)
                            act.activation(upd16[:, 0], upd[:], ACT.Copy).then_inc(updhi_done, 1)
                        for j in range(2):
                            exps.next()
                            act.wait_ge(slot_free, slots.next() + 2)
                            act.activation(e32[:, j], e32[:, j], ACT.Exp, scale=float(D) ** -0.5).then_inc(exp_done, 1)
                        for j in range(2):
                            n = his.next()
                            act.wait_ge(at32_done, n)
                            if h > 0:
                                act.wait_ge(u_done, n - 2)
                            act.activation(at16[:, j, 0], e32[:, j], ACT.Copy).then_inc(athi_done, 1)
                        if prev is not None:
                            gates(n_=grus.base + grus.n)

                    def gates(n_):
                        act.wait_ge(rz_sum, n_)
                        act.activation(rz[:], rz[:], ACT.Tanh, scale=0.5).then_inc(rz_tanh, 1)
                        act.wait_ge(n_sum, n_)
                        act.activation(cand[:], cand[:], ACT.Tanh).then_inc(n_tanh, 1)

                    def gru(h):
                        n = grus.next()
                        act.wait_ge(u_free, n + ONE)
                        act.activation(upd16[:, 0], upd[:], ACT.Copy).then_inc(updhi_done, 1)
                        gates(n)

                    def fin(f):
                        n = fins.next()
                        act.wait_ge(h_ready, g * 8 + f + 1 + ONE)
                        act.activation(hs16[:, 1, 0], h32[:, f % 2], ACT.Square,
                                       accum_out=ssq1[:, f % 2:f % 2 + 1]).then_inc(ssq1_done, 1)
                        act.activation(hs16[:, 0, 0], h32[:, f % 2], ACT.Copy).then_inc(hhi_done, 1)
                        act.wait_ge(sn_ready, n)
                        act.activation(hs16[:, 1, 0], sn32[:], ACT.Copy).then_inc(snhi_done, 1)
                        act.wait_ge(q_full, n)
                        act.activation(qT16[:, f % 2, 0].rearrange("p c n -> p (c n)"), TQ[:, 0:D],
                                       ACT.Copy, scale=1.0 / WS).then_inc(qhi_done, 1)

                    order(prep, fin, gru, att)
                    for c in (prepped, slots, exps, his, grus, fins):
                        c.done()

            @block.tensor
            def _(pe):
                with pe.Fori(0, GROUPS) as g:
                    prepped = Count(g, 4)
                    slots = Count(g, SLOTS)
                    uses = Count(g, TUSES)
                    fins = Count(g, HS)
                    grus = Count(g, HS)
                    us = Count(g, 2 * HS)

                    def prep(q):
                        pe.wait_ge(stage_read, prepped.next() + 2)
                        for t0 in range(0, MT, 4):
                            k = slots.n % 2
                            pe.wait_ge(slot_free, slots.next())
                            for t in range(t0, min(t0 + 4, MT)):
                                for part in range(2):
                                    for c in range(C):
                                        o = ((t - t0) * 4 + part * C + c) * P
                                        last = pe.transpose(SC16[k][:, o:o + P],
                                                            XN[:, q // 2, q % 2, t, part, c * P:(c + 1) * P],
                                                            ident16[:])
                            last.then_inc(slot_full, 1)

                    def split_matmul(out_, stat, mov, cs, first, lastg):
                        todo = [(c, a, b) for c in cs for a, b in PASSES]
                        for i, (c, a, b) in enumerate(todo):
                            ins = pe.matmul(out_, stat(a, c), mov(b, c), start=(first and i == 0),
                                            stop=(lastg and i == len(todo) - 1))
                        return ins

                    def gates(h):
                        X = h % 2
                        n = grus.next()
                        pe.wait_ge(updlo_done, n)
                        pe.wait_ge(t_free, uses.next() - 1 + ONE)
                        for part in range(2):
                            for c in range(C):
                                o = (part * C + c) * P
                                last = pe.transpose(T16[:, o:o + P], upd16[:, part, c * P:(c + 1) * P], ident16[:])
                        last.then_inc(t_full, 1)
                        pe.wait_ge(gates_free, n - 1 + ONE)
                        hp = lambda a, c: hT16[:, X, a * C + c, :]
                        up = lambda a, c: uT16[:, a * C + c, :]
                        split_matmul(RZ, hp, lambda b, c: whhT16[:, b, c, 0:2 * D], range(C), True, False)
                        split_matmul(NB[:, D:2 * D], hp, lambda b, c: whhT16[:, b, c, 2 * D:G], range(C), True, True)
                        pe.wait_ge(t_free, uses.base + uses.n + ONE)
                        split_matmul(NB[:, 0:D], up, lambda b, c: wihT16[:, b, c, 2 * D:G], range(C), True, True)
                        last = split_matmul(RZ, up, lambda b, c: wihT16[:, b, c, 0:2 * D], range(C), False, True)
                        last.then_inc(gates_done, 1)

                    def att(h, prev):
                        X = h % 2
                        pe.wait_ge(q_ready, g * HS + h + 1)
                        for j in range(2):
                            k = slots.n % 2
                            pe.wait_ge(slot_free, slots.next())
                            for t in range(MT):
                                last = split_matmul(SC[k][:, t * N:(t + 1) * N],
                                                    lambda a, c: XT[:, X, j, t, a * C + c, :],
                                                    lambda b, c: qT16[:, X, b, c, j * N:(j + 1) * N],
                                                    range(C), True, True)
                            last.then_inc(slot_full, 1)
                        if prev is not None:
                            gates(prev)
                        pe.wait_ge(u_free, g * HS + h + ONE)
                        for j in range(2):
                            n = us.next()
                            pe.wait_ge(athi_done, n)
                            pe.wait_ge(atlo_done, n + ONE)
                            for t in range(MT):
                                for i, (a, b) in enumerate(PASSES):
                                    w = D + 1 if b == 0 else D
                                    last = pe.matmul(U[j * N:(j + 1) * N, 0:w], at16[:, j, a, t, :],
                                                     XN[:, X, j, t, b, 0:w], start=(t == 0 and i == 0),
                                                     stop=(t == MT - 1 and i == 2))
                            last.then_inc(u_done, 1)

                    def fin(f):
                        n = fins.next()
                        pe.wait_ge(hslo_done, n)
                        pe.wait_ge(t_free, uses.next() - 1 + ONE)
                        for i in range(2):
                            for part in range(2):
                                for c in range(C):
                                    o = ((i * 2 + part) * C + c) * P
                                    last = pe.transpose(T16[:, o:o + P], hs16[:, i, part, c * P:(c + 1) * P], ident16[:])
                        last.then_inc(t_full, 1)
                        pe.wait_ge(t_free, uses.base + uses.n + ONE)
                        for e in range(C):
                            last = split_matmul(TQ[:, e * P:(e + 1) * P],
                                                lambda a, c: A16[:, a, c, e * P:(e + 1) * P],
                                                lambda b, c: hT16[:, f % 2, 4 + b * C + c, :], range(C), True, True)
                        last.then_inc(q_full, 1)

                    order(prep, fin, gates, att)
                    for c in (prepped, slots, uses, fins, grus, us):
                        c.done()

            @block.vector
            def _(dve):
                credit(dve, h_ready, gates_free, t_free, u_free)
                for q in range(4):
                    dve.memset(XN[:, q // 2, q % 2, 0:MR, 0, D:XW], 1.0)
                    dve.memset(XN[:, q // 2, q % 2, :, 1, D:XW], 0.0)
                    dve.memset(XN[:, q // 2, q % 2, MR, 0, D:XW], 0.0)
                dve.memset(ssq1[:], 0.0).then_inc(dve_step, 1)
                dve.wait_ge(dve_step, 1)
                for q in range(4):
                    dve.memset(XN[0:TAIL, q // 2, q % 2, MR, 0, D:XW], 1.0)
                dve.memset(urs[:], 0.0).then_inc(slot_free, 2)
                STEPS = 3 * 2 * HS + 6 * HS + 2
                with dve.Fori(0, GROUPS) as g:
                    step = Count(g, STEPS)
                    prepped = Count(g, 4)
                    slots = Count(g, SLOTS)
                    uses = Count(g, TUSES)
                    fins = Count(g, HS)
                    grus = Count(g, HS)
                    exps = Count(g, 2 * HS)

                    def link(ins):
                        ins.then_inc(dve_step, 1)
                        dve.wait_ge(dve_step, step.next() + 1)

                    def prep(q):
                        n = prepped.next()
                        dve.wait_ge(rinv_ready, n + ONE)
                        dve.scalar_tensor_tensor(X32[:, q % 2], X32[:, q % 2], float(D) ** 0.5,
                                                 rinv[:, q % 2].unsqueeze(2).broadcast_to([P, MT, D]),
                                                 ALU.mult, ALU.mult).then_inc(scaled, 1)
                        dve.wait_ge(scaled, n)
                        dve.wait_ge(xhi_done, n)
                        dve.tensor_tensor(XN[:, q // 2, q % 2, :, 1, 0:D], X32[:, q % 2],
                                          XN[:, q // 2, q % 2, :, 0, 0:D], ALU.subtract).then_inc(stage_read, 1)
                        for t0 in range(0, MT, 4):
                            k = slots.n % 2
                            w = min(4, MT - t0)
                            dve.wait_ge(slot_full, slots.next())
                            dve.tensor_copy(XT[:, q // 2, q % 2, t0:t0 + w].rearrange("p t a n -> p (t a n)"),
                                            SC16[k][:, 0:w * 4 * P]).then_inc(slot_free, 1)

                    def shift(h, j):
                        k = slots.n % 2
                        dve.wait_ge(slot_full, slots.next())
                        s = SC[k][:, 0:MT * N].rearrange("p (t n) -> p t n", n=N)
                        link(dve.reduce_max(mx[:, j], s, AX_X))
                        if h > 0:
                            dve.wait_ge(atlo_done, g * 2 * HS + 2 * (h - 1) + j + 1 + ONE)
                        else:
                            dve.wait_ge(atlo_done, g * 2 * HS + ONE)
                        dve.tensor_tensor(e32[:, j], s, mx[:, j].unsqueeze(2).broadcast_to([P, MT, N]),
                                          ALU.subtract).then_inc(slot_free, 1)

                    def norm(h, j):
                        dve.wait_ge(exp_done, exps.next())
                        link(dve.reduce_sum(sm[:, j], e32[:, j], AX_X))
                        link(dve.reciprocal(sm[:, j], sm[:, j]))
                        dve.scalar_tensor_tensor(e32[:, j], e32[:, j], AS,
                                                 sm[:, j].unsqueeze(2).broadcast_to([P, MT, N]),
                                                 ALU.mult, ALU.mult).then_inc(at32_done, 1)

                    def take_update(h):
                        n = grus.next()
                        dve.wait_ge(u_done, g * 2 * HS + 2 * h + 2)
                        link(dve.tensor_scalar(urs[:, 0:1], U[:, D:D + 1], AS * 1e-6, None, ALU.add))
                        link(dve.reciprocal(urs[:, 0:1], urs[:, 0:1]))
                        dve.tensor_scalar(upd[:], U[:, 0:D], urs[:, 0:1], None, ALU.mult).then_inc(u_free, 1)
                        dve.wait_ge(u_free, n + ONE)
                        dve.wait_ge(updhi_done, n)
                        dve.tensor_tensor(upd16[:, 1], upd[:], upd16[:, 0], ALU.subtract).then_inc(updlo_done, 1)

                    def take_update_T():
                        dve.wait_ge(t_full, uses.next())
                        dve.tensor_copy(uT16[:].rearrange("p a n -> p (a n)"), T16[:, 0:4 * P]).then_inc(t_free, 1)

                    def gate(h):
                        X = h % 2
                        n = grus.base + grus.n
                        dve.wait_ge(gates_done, n)
                        dve.scalar_tensor_tensor(rz[:], RZ, 1.0 / WS, brz[:], ALU.mult, ALU.add).then_inc(rz_sum, 1)
                        dve.scalar_tensor_tensor(xn_[:], NB[:, 0:D], 1.0 / WS, bxn[:], ALU.mult, ALU.add)
                        dve.scalar_tensor_tensor(cand[:], NB[:, D:2 * D], 1.0 / WS, bhn[:], ALU.mult,
                                                 ALU.add).then_inc(gates_free, 1)
                        dve.wait_ge(rz_tanh, n)
                        dve.wait_ge(gates_free, n + ONE)
                        link(dve.tensor_scalar(rz[:], rz[:], 0.5, 0.5, ALU.mult, ALU.add))
                        link(dve.tensor_tensor(cand[:], cand[:], rz[:, 0:D], ALU.mult))
                        dve.tensor_tensor(cand[:], cand[:], xn_[:], ALU.add).then_inc(n_sum, 1)
                        dve.wait_ge(n_tanh, n)
                        link(dve.tensor_tensor(xn_[:], h32[:, X], cand[:], ALU.subtract))
                        link(dve.tensor_tensor(xn_[:], xn_[:], rz[:, D:2 * D], ALU.mult))
                        dve.tensor_tensor(h32[:, X], cand[:], xn_[:], ALU.add).then_inc(h_ready, 1)
                        if h >= HS - 2:
                            dve.wait_ge(h_ready, g * 8 + 2 + h + 1 + ONE)
                            link(dve.tensor_tensor(x_sb[:, bass.ds(2 * g + X, 1), :].rearrange("p a d -> p (a d)"),
                                                   x_sb[:, bass.ds(2 * g + X, 1), :].rearrange("p a d -> p (a d)"),
                                                   h32[:, X], ALU.add))

                    def att(h, prev):
                        if prev is not None:
                            take_update(prev)
                        shift(h, 0)
                        if prev is not None:
                            take_update_T()
                        shift(h, 1)
                        norm(h, 0)
                        norm(h, 1)
                        if prev is not None:
                            gate(prev)

                    def gru(h):
                        take_update(h)
                        take_update_T()
                        gate(h)

                    def fin(f):
                        X = f % 2
                        n = fins.next()
                        if f < 2:
                            dve.tensor_copy(h32[:, X], s0[:, bass.ds(2 * g + X, 1), :].rearrange("p a d -> p (a d)")
                                            ).then_inc(h_ready, 1)
                        dve.wait_ge(h_ready, g * 8 + f + 1 + ONE)
                        dve.wait_ge(r1_ready, n)
                        dve.tensor_scalar(sn32[:], h32[:, X], r1[:, X:X + 1], float(D) ** 0.5, ALU.mult, ALU.mult).then_inc(sn_ready, 1)
                        dve.wait_ge(hhi_done, n)
                        dve.tensor_tensor(hs16[:, 0, 1], h32[:, X], hs16[:, 0, 0], ALU.subtract)
                        dve.wait_ge(snhi_done, n)
                        dve.wait_ge(sn_ready, n)
                        dve.tensor_tensor(hs16[:, 1, 1], sn32[:], hs16[:, 1, 0], ALU.subtract).then_inc(hslo_done, 1)
                        dve.wait_ge(t_full, uses.next())
                        dve.tensor_copy(hT16[:, X].rearrange("p a n -> p (a n)"), T16).then_inc(t_free, 1)
                        dve.wait_ge(qhi_done, n)
                        dve.scalar_tensor_tensor(qT16[:, X, 1].rearrange("p c n -> p (c n)"), TQ[:, 0:D], 1.0 / WS,
                                                 qT16[:, X, 0].rearrange("p c n -> p (c n)"),
                                                 ALU.mult, ALU.subtract).then_inc(q_ready, 1)
                        dve.wait_ge(q_ready, n)

                    order(prep, fin, gru, att)
                    for c in (step, prepped, slots, uses, fins, grus, exps):
                        c.done()

        phase1.close()
        HW = H * N
        W65 = H * V1
        KC = H * DH // P
        BITS = [64, 32, 16, 8, 4, 2, 1]

        with ExitStack() as p2:
            wq32 = sb("wq32", [P, C, H * DH], F32, p2)
            wkv32 = sb("wkv32", [P, C, 2 * H * DH], F32, p2)
            wo32 = sb("wo32", [P, KC, D], F32, p2)
            pos32 = sb("pos32", [P, DH], F32, p2)
            wq16 = sb("wq16", [P, 2, C, H * DH], F16, p2)
            wkv16 = sb("wkv16", [P, 2, C, 2 * H * DH], F16, p2)
            wo16 = sb("wo16", [P, 2, KC, D], F16, p2)
            pos16 = sb("pos16", [P, 2, DH], F16, p2)
            bo = sb("bo", [P, D], F32, p2)
            reset = sb("reset", [P, H, V1], F32, p2)
            ones = sb("ones", [P, H, V1], F32, p2)
            vpos = sb("vpos", [P, H, V1], F32, p2)
            a_stats = sb("a_stats", [P, PAIRS, 6], F32, p2)
            a_mv = sb("a_mv", [P, PAIRS, 2], F32, p2)
            a_r = sb("a_r", [P, PAIRS], F32, p2)
            a_x = sb("a_x", [P, D], F32, p2)
            a_x16 = sb("a_x16", [P, 2, D], F16, p2)
            xT16 = sb("xT16", [P, 2, 2, C, P], F16, p2)
            q16 = sb("q16", [P, 2, 2, KC, P], F16, p2)
            k16 = sb("k16", [P, 2, 2, KC, P], F16, p2)
            v16 = sb("v16", [P, 2, 2, H * DH], F16, p2)
            gs = sb("gs", [P, H, V1], F32, p2)
            fl = sb("fl", [P, H, V1], F32, p2)
            ar = sb("ar", [P, H, V1], F32, p2)
            s32 = sb("s32", [P, H, V1], I32, p2)
            mask = sb("mask", [P, 2, H, V1], I32, p2)
            tab = sb("tab", [P, 2, 2, H, V1], F32, p2)
            lg = sb("lg", [P, H, N], F32, p2)
            hs_ = sb("hs_", [P, 2, H], F32, p2)
            p16 = sb("p16", [P, 2, 2, H, 2, N], F16, p2)
            pT16 = sb("pT16", [P, 2, H, P], F16, p2)
            o16 = sb("o16", [P, 2, KC, P], F16, p2)
            tmp = sb("tmp", [P, D], F32, p2)

            a_load = sem("a_load")
            a_const = sem("a_const")
            a_zero = sem("a_zero")
            a_whi = sem("a_whi")
            a_wlo = sem("a_wlo")
            ln_st = sem("ln_st")
            ln_mv = sem("ln_mv")
            ln_r = sem("ln_r")
            ln_pool = sem("ln_pool")
            ln_x = sem("ln_x")
            ln_hi = sem("ln_hi")
            ln_lo = sem("ln_lo")
            xT_full = sem("xT_full")
            xT_done = sem("xT_done")
            proj_full = sem("proj_full")
            proj_hi = sem("proj_hi")
            proj_lo = sem("proj_lo")
            sim_full = sem("sim_full")
            gate_tanh = sem("gate_tanh")
            tab_copied = sem("tab_copied")
            logit_done = sem("logit_done")
            a_exp = sem("a_exp")
            p32_done = sem("p32_done")
            phi_done = sem("phi_done")
            plo_done = sem("plo_done")
            pT_full = sem("pT_full")
            pT_done = sem("pT_done")
            o_full = sem("o_full")
            o_hi = sem("o_hi")
            o_lo = sem("o_lo")
            y_full = sem("y_full")
            y_done = sem("y_done")
            a_step = sem("a_step")
            block = p2.enter_context(nc.Block())

            def banks(X, b0, n):
                return bank[:, 4 * X + b0:4 * X + b0 + n, :].rearrange("p b n -> p (b n)")

            def banks16(X, b0, n):
                return bank16[:, 4 * X + b0:4 * X + b0 + n, :].rearrange("p b n -> p (b n)")

            def order2(proj, cope, av):
                proj(0)
                cope(0)
                proj(1)
                cope(1)
                av(0)
                av(1)

            @block.sync
            def _(sp):
                sp.dma_start(wq32[:], aWq.rearrange("(c p) n -> p c n", p=P)).then_inc(a_load, 16)
                sp.dma_start(wkv32[:], aWkv.rearrange("(c p) n -> p c n", p=P)).then_inc(a_load, 16)
                sp.dma_start(pos32[0:DH, :], pos_emb).then_inc(a_load, 16)
                sp.dma_start(pos32[DH:P, :], pos_emb).then_inc(a_load, 16)
                sp.dma_start(wo32[:], aWout.rearrange("(c p) n -> p c n", p=P)).then_inc(a_load, 16)
                sp.dma_start(bo[:], ab_out.rearrange("(a n) -> a n", a=1).broadcast_to([P, D])).then_inc(a_load, 16)

            @block.gpsimd
            def _(pool):
                pool.wait_ge(ln_mv, PAIRS)
                pool.tensor_scalar(a_r[:], a_mv[:, :, 1], 1.0, 1e-5, ALU.mult, ALU.add).then_inc(ln_pool, 1)
                pool.wait_ge(ln_pool, 1)
                pool.tensor_tensor(a_r[:], a_r[:], half[:, 0:PAIRS], ALU.pow).then_inc(ln_r, 1)
                pool.iota(s32[:], pattern=[[0, H], [1, V1]], base=0, channel_multiplier=0).then_inc(a_const, 1)
                pool.memset(reset[:], 1.0).then_inc(a_const, 1)
                pool.memset(ones[:], 1.0).then_inc(a_const, 1)
                pool.wait_ge(a_const, 3)
                pool.memset(reset[:, :, 0:1], 0.0).then_inc(a_const, 1)
                pool.tensor_scalar(vpos[:], s32[:], 1.0, MAGIC, ALU.mult, ALU.add).then_inc(a_const, 1)
                pool.memset(gs[:, :, 0:1], 0.0).then_inc(a_const, 1)
                for X in range(2):
                    pool.memset(p16[:, X].rearrange("p a h b n -> p (a h b n)"), 0.0).then_inc(a_zero, 1)
                pool.wait_ge(a_zero, 2)
                credit(pool, plo_done)
                with pool.Fori(0, GROUPS) as g:
                    def cope(X):
                        n = g * 2 + X + 1
                        pool.wait_ge(phi_done, n)
                        for b in range(2):
                            r = slice(b * N, (b + 1) * N)
                            pool.tensor_tensor(p16[r, X, 1, :, b, :], lg[r], p16[r, X, 0, :, b, :],
                                               ALU.subtract).then_inc(plo_done, 1)
                            pool.wait_ge(plo_done, (n - 1) * 2 + b + 1 + ONE)

                    order2(lambda X: None, cope, lambda X: None)

            @block.scalar
            def _(act):
                act.wait_ge(a_zero, 2)
                act.wait_ge(a_load, 96)
                for w16, w32 in ((wq16, wq32), (wkv16, wkv32), (wo16, wo32), (pos16, pos32)):
                    act.activation(w16[:, 0], w32[:], ACT.Copy, scale=WS).then_inc(a_whi, 1)
                with act.Fori(0, GROUPS) as g:
                    def proj(X):
                        n = g * 2 + X + 1
                        act.wait_ge(ln_x, n)
                        act.activation(a_x16[:, 0], a_x[:], ACT.Copy).then_inc(ln_hi, 1)
                        for i, (dst, b0) in enumerate(((q16, 2), (k16, 0))):
                            act.wait_ge(proj_full, (n - 1) * 3 + i + 1)
                            act.activation(dst[:, X, 0].rearrange("p c n -> p (c n)"), banks(X, b0, 2),
                                           ACT.Copy, scale=1.0 / WS).then_inc(proj_hi, 1)
                        act.wait_ge(proj_full, (n - 1) * 3 + 3)
                        act.activation(v16[:, X, 0], banks(X, 2, 2), ACT.Copy, scale=1.0 / WS).then_inc(proj_hi, 1)

                    def cope(X):
                        n = g * 2 + X + 1
                        act.wait_ge(sim_full, n)
                        act.wait_ge(logit_done, n - 1 + ONE)
                        act.activation(gs[:, :, 1:V1], banks(X, 0, 2).rearrange("p (h n) -> p h n", n=N),
                                       ACT.Tanh, scale=0.5 * DH ** -0.5).then_inc(gate_tanh, 1)
                        e = banks(X, 2, 2).rearrange("p (h n) -> p h n", n=N)
                        act.activation(tab[:, 0, 0, :, 0:N], e, ACT.Copy, scale=1.0 / WS)
                        act.activation(tab[:, 0, 1, :, 0:N - 1], e[:, :, 1:N], ACT.Copy, scale=1.0 / WS)
                        act.activation(tab[:, 0, 0, :, N:V1], e[:, :, N - 1:N], ACT.Copy, scale=1.0 / WS)
                        act.activation(tab[:, 0, 1, :, N - 1:V1], e[:, :, N - 1:N].broadcast_to([P, H, 2]),
                                       ACT.Copy, scale=1.0 / WS).then_inc(tab_copied, 1)
                        act.wait_ge(logit_done, n + ONE)
                        act.activation(lg[:], lg[:], ACT.Exp).then_inc(a_exp, 1)
                        act.wait_ge(p32_done, n)
                        for b in range(2):
                            r = slice(b * N, (b + 1) * N)
                            ins = act.activation(p16[r, X, 0, :, b, :], lg[r], ACT.Copy)
                        ins.then_inc(phi_done, 1)

                    def av(X):
                        n = g * 2 + X + 1
                        act.wait_ge(o_full, n)
                        act.activation(o16[:, 0].rearrange("p c n -> p (c n)"), banks(X, 0, 2), ACT.Copy,
                                       scale=1.0 / AS).then_inc(o_hi, 1)

                    order2(proj, cope, av)

            @block.tensor
            def _(pe):
                def split(out_, stat, mov, cs):
                    todo = [(c, a, b) for c in cs for a, b in PASSES]
                    for i, (c, a, b) in enumerate(todo):
                        ins = pe.matmul(out_, stat(a, c), mov(b, c), start=(i == 0), stop=(i == len(todo) - 1))
                    return ins

                pe.wait_ge(a_wlo, 4)
                with pe.Fori(0, GROUPS) as g:
                    def proj(X):
                        n = g * 2 + X + 1
                        pe.wait_ge(ln_lo, n)
                        pe.wait_ge(y_done, 2 * g + ONE)
                        for i, perm in enumerate((ident16, flip16)):
                            for part in range(2):
                                for c in range(C):
                                    o = (part * C + c) * P
                                    last = pe.matmul(banks(X, i, 1)[:, o:o + P], a_x16[:, part, c * P:(c + 1) * P],
                                                     perm[:], start=True, stop=True)
                            last.then_inc(xT_full, 1)
                        pe.wait_ge(xT_done, n)
                        for i, (b0, rev, col) in enumerate(((2, 0, None), (0, 1, 0))):
                            w16 = wq16 if i == 0 else wkv16
                            for t in range(KC):
                                last = split(banks(X, b0, 2)[:, t * P:(t + 1) * P],
                                             lambda a, c: w16[:, a, c, t * P:(t + 1) * P],
                                             lambda b, c: xT16[:, rev, b, c, :], range(C))
                            last.then_inc(proj_full, 1)
                        pe.wait_ge(proj_lo, (n - 1) * 3 + 1)
                        for t in range(2):
                            last = split(banks(X, 2 + t, 1), lambda a, c: xT16[:, 1, a, c, :],
                                         lambda b, c: wkv16[:, b, c, H * DH + t * 512:H * DH + (t + 1) * 512], range(C))
                        last.then_inc(proj_full, 1)

                    def cope(X):
                        n = g * 2 + X + 1
                        pe.wait_ge(proj_lo, (n - 1) * 3 + 3)
                        for t in range(KC):
                            for r in range(2):
                                rows = slice(r * DH, (r + 1) * DH)
                                split(banks(X, 2 + r, 1)[:, t * N:(t + 1) * N], lambda a, c: q16[rows, X, a, t, :],
                                      lambda a, c: pos16[rows, a, :], range(1))
                        for t in range(KC):
                            for r in range(2):
                                rows = slice(r * DH, (r + 1) * DH)
                                for b in range(2):
                                    cols = slice(b * N, (b + 1) * N)
                                    last = split(banks(X, r, 1)[cols, t * N:(t + 1) * N],
                                                 lambda a, c: q16[rows, X, a, t, cols],
                                                 lambda a, c: k16[rows, X, a, t, cols], range(1))
                        last.then_inc(sim_full, 1)

                    def av(X):
                        n = g * 2 + X + 1
                        pe.wait_ge(phi_done, n)
                        pe.wait_ge(plo_done, n * 2 + ONE)
                        pe.wait_ge(pT_done, n - 1 + ONE)
                        for part in range(2):
                            for h in range(H):
                                last = pe.transpose(banks16(X, 0, 4)[:, (part * H + h) * P:(part * H + h + 1) * P],
                                                    p16[:, X, part, h].rearrange("p b n -> p (b n)"), ident16[:])
                        last.then_inc(pT_full, 1)
                        pe.wait_ge(pT_done, n + ONE)
                        for h in range(H):
                            r, t = h // KC, h % KC
                            head = 2 * t + r
                            last = split(banks(X, 0, 2)[r * DH:(r + 1) * DH, t * P:(t + 1) * P],
                                         lambda a, c: v16[:, X, a, head * DH:(head + 1) * DH],
                                         lambda b, c: pT16[:, b, h, :], range(1))
                        last.then_inc(o_full, 1)
                        pe.wait_ge(o_lo, n)
                        last = split(banks(X, 2, 1)[:, 0:D], lambda a, c: o16[:, a, c, :],
                                     lambda b, c: wo16[:, b, c, :], range(KC))
                        last.then_inc(y_full, 1)

                    order2(proj, cope, av)

            @block.vector
            def _(dve):
                credit(dve, y_done, logit_done, pT_done)
                for q in range(PAIRS):
                    dve.bn_stats(a_stats[:, q], x_sb[:, q]).then_inc(ln_st, 1)
                dve.wait_ge(ln_st, PAIRS)
                for q in range(PAIRS):
                    dve.bn_aggr(a_mv[:, q], a_stats[:, q]).then_inc(ln_mv, 1)
                dve.wait_ge(ln_mv, PAIRS)
                dve.wait_ge(ln_r, 1)
                dve.wait_ge(a_const, 6)
                for i, (w16, w32) in enumerate(((wq16, wq32), (wkv16, wkv32), (wo16, wo32), (pos16, pos32))):
                    pat = "p c n -> p (c n)"
                    hi, lo, w = w16[:, 0], w16[:, 1], w32[:]
                    if i < 3:
                        hi, lo, w = hi.rearrange(pat), lo.rearrange(pat), w.rearrange(pat)
                    dve.wait_ge(a_whi, i + 1)
                    dve.scalar_tensor_tensor(lo, w, WS, hi, ALU.mult, ALU.subtract).then_inc(a_wlo, 1)
                STEPS2 = 2 * (14 + 2 * len(BITS))
                with dve.Fori(0, GROUPS) as g:
                    step = Count(g, STEPS2)

                    def link(ins):
                        ins.then_inc(a_step, 1)
                        dve.wait_ge(a_step, step.next())

                    def proj(X):
                        n = g * 2 + X + 1
                        row = x_sb[:, bass.ds(2 * g + X, 1), :].rearrange("p a d -> p (a d)")
                        q = bass.ds(2 * g + X, 1)
                        dve.tensor_scalar(a_x[:], row, a_mv[:, q, 0:1].rearrange("p a b -> p (a b)"), a_r[:, q],
                                          ALU.subtract, ALU.mult).then_inc(ln_x, 1)
                        dve.wait_ge(ln_x, n)
                        dve.wait_ge(ln_hi, n)
                        dve.tensor_tensor(a_x16[:, 1], a_x[:], a_x16[:, 0], ALU.subtract).then_inc(ln_lo, 1)
                        for i in range(2):
                            dve.wait_ge(xT_full, (n - 1) * 2 + i + 1)
                            ins = dve.tensor_copy(xT16[:, i].rearrange("p a c n -> p (a c n)"), banks(X, i, 1))
                        ins.then_inc(xT_done, 1)
                        for i, (dst, b0) in enumerate(((q16, 2), (k16, 0), (v16, 2))):
                            dve.wait_ge(proj_hi, (n - 1) * 3 + i + 1)
                            hi, lo = dst[:, X, 0], dst[:, X, 1]
                            if i < 2:
                                hi, lo = hi.rearrange("p c n -> p (c n)"), lo.rearrange("p c n -> p (c n)")
                            dve.scalar_tensor_tensor(lo, banks(X, b0, 2), 1.0 / WS, hi, ALU.mult,
                                                     ALU.subtract).then_inc(proj_lo, 1)

                    def flat(t):
                        return t[:].rearrange("p h v -> p (h v)")

                    def cope(X):
                        n = g * 2 + X + 1
                        sim = banks(X, 0, 2).rearrange("p (h n) -> p h n", n=N)
                        dve.wait_ge(gate_tanh, n)
                        link(dve.tensor_scalar(gs[:, :, 1:V1], gs[:, :, 1:V1], 0.5, 0.5, ALU.mult, ALU.add))
                        link(dve.tensor_tensor_scan(flat(ar), flat(reset), flat(gs), 0.0, ALU.mult, ALU.add))
                        link(dve.tensor_scalar(ar[:], ar[:], float(N - 1), -0.5, ALU.min, ALU.add))
                        link(dve.tensor_scalar(fl[:], ar[:], MAGIC, None, ALU.add))
                        link(dve.tensor_tensor_scan(flat(fl), flat(ones), flat(fl), MAGIC, ALU.add, ALU.min))
                        dve.scalar_tensor_tensor(flat(s32), flat(fl), -1.0, flat(vpos), ALU.mult, ALU.add)
                        link(dve.scalar_tensor_tensor(flat(ar), flat(fl), -MAGIC, flat(ar), ALU.add, ALU.subtract))
                        dve.wait_ge(tab_copied, n)
                        cur = 0
                        dve.tensor_scalar(mask[:, 0], s32[:], BITS[0], None, ALU.bitwise_and)
                        for i, bit in enumerate(BITS):
                            new = 1 - cur
                            link(dve.tensor_copy(tab[:, new], tab[:, cur]))
                            if i + 1 < len(BITS):
                                dve.tensor_scalar(mask[:, (i + 1) % 2], s32[:], BITS[i + 1], None, ALU.bitwise_and)
                            else:
                                dve.tensor_scalar(ar[:], ar[:], -0.5, None, ALU.add)
                            m = mask[:, i % 2, :, bit:V1].unsqueeze(1).broadcast_to([P, 2, H, V1 - bit])
                            link(dve.copy_predicated(tab[:, new, :, :, bit:V1], m, tab[:, cur, :, :, 0:V1 - bit]))
                            cur = new
                        value, nxt = tab[:, cur, 0, :, 1:V1], tab[:, cur, 1, :, 1:V1]
                        link(dve.tensor_tensor(nxt, nxt, value, ALU.subtract))
                        link(dve.tensor_tensor(nxt, ar[:, :, 1:V1], nxt, ALU.mult))
                        link(dve.tensor_tensor(value, value, nxt, ALU.subtract))
                        dve.wait_ge(plo_done, (n - 1) * 2 + ONE)
                        link(dve.scalar_tensor_tensor(lg[:], sim, DH ** -0.5, value, ALU.mult, ALU.add))
                        link(dve.reduce_max(hs_[:, 0], lg[:], AX_X))
                        dve.tensor_tensor(lg[:], lg[:], hs_[:, 0].unsqueeze(2).broadcast_to([P, H, N]),
                                          ALU.subtract).then_inc(logit_done, 1)
                        dve.wait_ge(a_exp, n)
                        link(dve.reduce_sum(hs_[:, 1], lg[:], AX_X))
                        link(dve.reciprocal(hs_[:, 1], hs_[:, 1]))
                        dve.scalar_tensor_tensor(lg[:], lg[:], AS, hs_[:, 1].unsqueeze(2).broadcast_to([P, H, N]),
                                                 ALU.mult, ALU.mult).then_inc(p32_done, 1)

                    def av(X):
                        n = g * 2 + X + 1
                        row = x_sb[:, bass.ds(2 * g + X, 1), :].rearrange("p a d -> p (a d)")
                        dve.wait_ge(pT_full, n)
                        dve.tensor_copy(pT16[:].rearrange("p a h n -> p (a h n)"), banks16(X, 0, 4)).then_inc(pT_done, 1)
                        dve.wait_ge(o_hi, n)
                        dve.scalar_tensor_tensor(o16[:, 1].rearrange("p c n -> p (c n)"), banks(X, 0, 2), 1.0 / AS,
                                                 o16[:, 0].rearrange("p c n -> p (c n)"),
                                                 ALU.mult, ALU.subtract).then_inc(o_lo, 1)
                        dve.wait_ge(y_full, n)
                        link(dve.scalar_tensor_tensor(tmp[:], banks(X, 2, 1)[:, 0:D], 1.0 / WS, bo[:],
                                                      ALU.mult, ALU.add))
                        dve.tensor_tensor(row, row, tmp[:], ALU.add).then_inc(y_done, 1)
                        dve.wait_ge(y_done, n + ONE)

                    order2(proj, cope, av)
                    step.done()

        HSC = 16.0
        with ExitStack() as p3:
            f_stats = sb("f_stats", [P, PAIRS, 6], F32, p3)
            f_mv = sb("f_mv", [P, PAIRS, 2], F32, p3)
            f_r = sb("f_r", [P, PAIRS], F32, p3)
            f_x = sb("f_x", [P, PAIRS, D], F32, p3)
            f_x16 = sb("f_x16", [P, 2, PAIRS, D], F16, p3)
            f_xT = sb("f_xT", [P, 2, C, TOK], F16, p3)
            gw32 = sb("gw32", [P, C, E], F32, p3)
            gw16 = sb("gw16", [P, 2, C, E], F16, p3)
            lg8 = sb("lg8", [P, PAIRS, E], F32, p3)
            rank_i = sb("rank_i", [P, PAIRS, E], I32, p3)
            rank = sb("rank", [P, PAIRS, E], F32, p3)
            pick = sb("pick", [P, 2, PAIRS, E], F32, p3)
            eq = sb("eq", [P, PAIRS, E], F32, p3)
            top = sb("top", [P, 4, PAIRS], F32, p3)
            share = sb("share", [P, PAIRS, E], F32, p3)
            gu32 = sb("gu32", [P, 2, C, 2 * F], F32, p3)
            dn32 = sb("dn32", [P, 2, FC, D], F32, p3)
            gu16 = sb("gu16", [P, 2, 2, C, 2 * F], F16, p3)
            dn16 = sb("dn16", [P, 2, 2, FC, D], F16, p3)
            th = sb("th", [P, 2, TOK], F32, p3)
            hid = sb("hid", [P, 2, TOK], F32, p3)
            hid16 = sb("hid16", [P, 2, 2, TOK], F16, p3)

            f_load = sem("f_load")
            f_const = sem("f_const")
            f_mvd = sem("f_mvd")
            f_pool = sem("f_pool")
            f_rr = sem("f_rr")
            f_xr = sem("f_xr")
            f_hi = sem("f_hi")
            f_lo = sem("f_lo")
            f_T = sem("f_T")
            f_Td = sem("f_Td")
            gw_hi = sem("gw_hi")
            gw_lo = sem("gw_lo")
            lg_full = sem("lg_full")
            e2_in = sem("e2_in")
            e2_out = sem("e2_out")
            w_loaded = [sem(f"w_loaded{i}") for i in range(2)]
            w_hi = sem("w_hi")
            w_lo = sem("w_lo")
            gu_full = sem("gu_full")
            th_done = sem("th_done")
            sg_done = sem("sg_done")
            hid_done = sem("hid_done")
            hid_hi = sem("hid_hi")
            hid_lo = sem("hid_lo")
            ffn_done = sem("ffn_done")
            y3_done = sem("y3_done")
            f_step = sem("f_step")
            gu_dram = gate_up_w.rearrange("e (c p) n -> e p c n", p=P)
            dn_dram = down_w.rearrange("e (c p) n -> e p c n", p=P)
            block = p3.enter_context(nc.Block())

            @block.sync
            def _(sp):
                sp.dma_start(gw32[:], gate_w.rearrange("(c p) n -> p c n", p=P)).then_inc(f_load, 16)
                with sp.Fori(0, E // 2) as i:
                    for s in range(2):
                        sp.wait_ge(w_lo, 4 * i + ONE)
                        sp.dma_start(gu32[:, s], gu_dram[i * 2 + s]).then_inc(w_loaded[s], 16)
                        sp.dma_start(dn32[:, s], dn_dram[i * 2 + s]).then_inc(w_loaded[s], 16)

            @block.gpsimd
            def _(pool):
                pool.iota(rank_i[:], pattern=[[0, PAIRS], [-1, E]], base=E, channel_multiplier=0).then_inc(f_const, 1)
                pool.wait_ge(f_const, 1)
                pool.tensor_copy(rank[:], rank_i[:]).then_inc(f_const, 1)
                pool.wait_ge(f_mvd, PAIRS)
                pool.tensor_scalar(f_r[:], f_mv[:, :, 1], 1.0, 1e-5, ALU.mult, ALU.add).then_inc(f_pool, 1)
                pool.wait_ge(f_pool, 1)
                pool.tensor_tensor(f_r[:], f_r[:], half[:, 0:PAIRS], ALU.pow).then_inc(f_rr, 1)

            @block.scalar
            def _(act):
                act.wait_ge(f_load, 16)
                act.activation(gw16[:, 0], gw32[:], ACT.Copy, scale=WS).then_inc(gw_hi, 1)
                act.wait_ge(f_xr, PAIRS)
                act.activation(f_x16[:, 0], f_x[:], ACT.Copy).then_inc(f_hi, 1)
                act.wait_ge(e2_in, 1)
                act.activation(top[:, 3], top[:, 2], ACT.Exp).then_inc(e2_out, 1)

                def split_weights(n, s, staged):
                    act.wait_ge(w_loaded[s], staged)
                    act.wait_ge(ffn_done, n)
                    for w32, w16 in ((gu32, gu16), (dn32, dn16)):
                        act.activation(w16[:, s, 0], w32[:, s], ACT.Copy, scale=WS).then_inc(w_hi, 1)

                def two_experts(i, more):
                    for k in range(2 * FC):
                        m = i * 2 * FC + k + 1
                        act.wait_ge(gu_full, m)
                        act.activation(th[:, k % 2], bank[:, 2 * (k % 2), :], ACT.Tanh,
                                       scale=0.5 / WS).then_inc(th_done, 1)
                        act.wait_ge(hid_done, m + 2)
                        act.activation(hid16[:, k % 2, 0], hid[:, k % 2], ACT.Copy).then_inc(hid_hi, 1)
                        if k == 1:
                            split_weights(i * 2 + 2, 1, i * 32 + 32)
                        if k == FC + 1 and more:
                            split_weights(i * 2 + 3, 0, i * 32 + 64)

                split_weights(1, 0, 32)
                with act.Fori(0, E // 2 - 1) as i:
                    two_experts(i, True)
                two_experts(E // 2 - 1, False)

            @block.tensor
            def _(pe):
                def split(out_, stat, mov, cs, first=True, last_=True):
                    todo = [(c, a, b) for c in cs for a, b in PASSES]
                    for i, (c, a, b) in enumerate(todo):
                        ins = pe.matmul(out_, stat(a, c), mov(b, c), start=(first and i == 0),
                                        stop=(last_ and i == len(todo) - 1))
                    return ins

                pe.wait_ge(f_lo, 1)
                for q in range(PAIRS):
                    for part in range(2):
                        for c in range(C):
                            o = (part * C + c) * P
                            last = pe.transpose(bank16[:, q, o:o + P], f_x16[:, part, q, c * P:(c + 1) * P],
                                                ident16[:])
                    last.then_inc(f_T, 1)
                pe.wait_ge(f_Td, PAIRS)
                pe.wait_ge(gw_lo, 1)
                for q in range(PAIRS):
                    last = split(bank[:, 4, q * E:(q + 1) * E], lambda a, c: f_xT[:, a, c, q * P:(q + 1) * P],
                                 lambda b, c: gw16[:, b, c, :], range(C))
                last.then_inc(lg_full, 1)
                pe.matmul(bank[:, 5, 0:E], f_xT[:, 0, 0, 0:P], gw16[:, 0, 0, :], start=True,
                          stop=True).then_inc(ffn_done, 2)
                with pe.Fori(0, E // 2) as i:
                    def up(k):
                        s, j = k // FC, k % FC
                        if j == 0:
                            pe.wait_ge(w_lo, 4 * i + 2 * s + 2 + ONE)
                        pe.wait_ge(hid_done, i * 2 * FC + k + 1)
                        for u in range(2):
                            last = split(bank[:, 2 * (k % 2) + u, :],
                                         lambda a, c: gu16[:, s, a, c, u * F + j * P:u * F + (j + 1) * P],
                                         lambda b, c: f_xT[:, b, c, :], range(C))
                        last.then_inc(gu_full, 1)

                    def down(k):
                        s, j = k // FC, k % FC
                        if j == 0:
                            pe.wait_ge(y3_done, i * 2 + s + ONE)
                        pe.wait_ge(hid_lo, i * 2 * FC + k + 1)
                        for t in range(PAIRS):
                            last = split(bank[:, 4 + t, 0:D], lambda a, c: hid16[:, k % 2, a, t * P:(t + 1) * P],
                                         lambda b, c: dn16[:, s, b, j, :], range(1), j == 0, j == FC - 1)
                        if j == FC - 1:
                            last.then_inc(ffn_done, 1)

                    for k in range(2 * FC):
                        up(k)
                        if k:
                            down(k - 1)
                    down(2 * FC - 1)

            @block.vector
            def _(dve):
                credit(dve, w_lo, y3_done)
                steps = [0]

                def link(ins):
                    steps[0] += 1
                    ins.then_inc(f_step, 1)
                    dve.wait_ge(f_step, steps[0])

                for q in range(PAIRS):
                    last = dve.bn_stats(f_stats[:, q], x_sb[:, q])
                link(last)
                for q in range(PAIRS):
                    dve.bn_aggr(f_mv[:, q], f_stats[:, q]).then_inc(f_mvd, 1)
                dve.wait_ge(f_mvd, PAIRS)
                dve.wait_ge(f_rr, 1)
                for q in range(PAIRS):
                    dve.tensor_scalar(f_x[:, q], x_sb[:, q], f_mv[:, q, 0:1], f_r[:, q:q + 1],
                                      ALU.subtract, ALU.mult).then_inc(f_xr, 1)
                dve.wait_ge(f_xr, PAIRS)
                dve.wait_ge(f_hi, 1)
                dve.tensor_tensor(f_x16[:, 1], f_x[:], f_x16[:, 0], ALU.subtract).then_inc(f_lo, 1)
                dve.wait_ge(gw_hi, 1)
                dve.scalar_tensor_tensor(gw16[:, 1], gw32[:], WS, gw16[:, 0], ALU.mult, ALU.subtract).then_inc(gw_lo, 1)
                for q in range(PAIRS):
                    dve.wait_ge(f_T, q + 1)
                    dve.tensor_copy(f_xT[:, :, :, q * P:(q + 1) * P],
                                    bank16[:, q, 0:4 * P].rearrange("p (a c n) -> p a c n", a=2, c=C)).then_inc(f_Td, 1)
                dve.wait_ge(lg_full, 1)
                dve.wait_ge(f_const, 2)
                link(dve.tensor_scalar(lg8[:].rearrange("p q e -> p (q e)"), bank[:, 4, 0:PAIRS * E], 1.0 / WS,
                                       None, ALU.mult))
                bc = lambda t: t.unsqueeze(2).broadcast_to([P, PAIRS, E])
                for r in range(2):
                    link(dve.reduce_max(top[:, r], lg8[:], AX_X))
                    link(dve.tensor_tensor(eq[:], lg8[:], bc(top[:, r]), ALU.is_equal))
                    link(dve.tensor_tensor(eq[:], eq[:], rank[:], ALU.mult))
                    link(dve.reduce_max(top[:, 2], eq[:], AX_X))
                    link(dve.tensor_tensor(pick[:, r], rank[:], bc(top[:, 2]), ALU.is_equal))
                    link(dve.scalar_tensor_tensor(lg8[:], pick[:, r], -3e38, lg8[:], ALU.mult, ALU.add))
                dve.tensor_tensor(top[:, 2], top[:, 1], top[:, 0], ALU.subtract).then_inc(e2_in, 1)
                dve.wait_ge(e2_out, 1)
                link(dve.tensor_scalar(top[:, 2], top[:, 3], 1.0, None, ALU.add))
                link(dve.reciprocal(top[:, 2], top[:, 2]))
                link(dve.tensor_tensor(share[:], pick[:, 1], bc(top[:, 3]), ALU.mult))
                link(dve.tensor_tensor(share[:], share[:], pick[:, 0], ALU.add))
                link(dve.scalar_tensor_tensor(share[:], share[:], 1.0 / (WS * HSC), bc(top[:, 2]),
                                              ALU.mult, ALU.mult))
                dve.memset(eq[:], 0.0).then_inc(hid_done, 2)

                def split_weights(n, s):
                    pat = "p c n -> p (c n)"
                    for k, (w32, w16) in enumerate(((gu32, gu16), (dn32, dn16))):
                        dve.wait_ge(w_hi, 2 * (n - 1) + k + 1)
                        dve.scalar_tensor_tensor(w16[:, s, 1].rearrange(pat), w32[:, s].rearrange(pat), WS,
                                                 w16[:, s, 0].rearrange(pat), ALU.mult, ALU.subtract).then_inc(w_lo, 1)

                def two_experts(i, more):
                    for k in range(2 * FC):
                        m = i * 2 * FC + k + 1
                        s, j = k // FC, k % FC
                        dve.wait_ge(th_done, m)
                        dve.scalar_tensor_tensor(hid[:, k % 2], th[:, k % 2], 1.0, bank[:, 2 * (k % 2), :],
                                                 ALU.add, ALU.mult).then_inc(sg_done, 1)
                        dve.wait_ge(sg_done, m)
                        dve.scalar_tensor_tensor(hid[:, k % 2], hid[:, k % 2], HSC / (2 * WS * WS),
                                                 bank[:, 2 * (k % 2) + 1, :], ALU.mult, ALU.mult).then_inc(hid_done, 1)
                        dve.wait_ge(hid_done, m + 2)
                        dve.wait_ge(hid_hi, m)
                        dve.tensor_tensor(hid16[:, k % 2, 1], hid[:, k % 2], hid16[:, k % 2, 0],
                                          ALU.subtract).then_inc(hid_lo, 1)
                        if k == 1:
                            split_weights(i * 2 + 2, 1)
                        if k == FC + 1 and more:
                            split_weights(i * 2 + 3, 0)
                        if j == FC - 1:
                            n = i * 2 + s + 1
                            dve.wait_ge(ffn_done, n + 2)
                            dve.wait_ge(y3_done, n - 1 + ONE)
                            for t in range(PAIRS):
                                last = dve.scalar_tensor_tensor(x_sb[:, t], bank[:, 4 + t, 0:D],
                                                                share[:, t, bass.ds(i * 2 + s, 1)], x_sb[:, t],
                                                                ALU.mult, ALU.add)
                            last.then_inc(y3_done, 1)

                split_weights(1, 0)
                with dve.Fori(0, E // 2 - 1) as i:
                    two_experts(i, True)
                two_experts(E // 2 - 1, False)

        stored = sem("stored")
        with ExitStack() as p4:
            block = p4.enter_context(nc.Block())

            @block.sync
            def _(sp):
                sp.dma_start(out.rearrange("b k d -> (b k) d").rearrange("(q p) d -> p q d", p=P),
                             x_sb[:]).then_inc(stored, 16)
                sp.wait_ge(stored, 16)


_INS = ['x', 'ctx_1024', 'L0_xattn_Wq', 'L0_xattn_Wk', 'L0_xattn_Wv', 'L0_xattn_gru_wih',
        'L0_xattn_gru_whh', 'L0_xattn_gru_bih', 'L0_xattn_gru_bhh', 'L0_xattn_slot_norm_w',
        'L0_xattn_input_norm_w', 'L0_attn_Wq', 'L0_attn_Wkv', 'L0_attn_Wout', 'L0_attn_b_out',
        'L0_attn_pos_emb', 'L0_ffn_gate_w', 'L0_ffn_gate_up_w', 'L0_ffn_down_w']


def kernel(**inputs):
    import numpy as _np
    import concourse.bacc as _bacc
    from concourse.bass_utils import run_bass_kernel_spmd as _run

    nc = _bacc.Bacc("TRN2", target_bir_lowering=False, num_devices=1)
    arrays, args = {}, []
    for name in _INS:
        a = _np.ascontiguousarray(inputs[name])
        arrays[f"in_{name}_dram"] = a
        args.append(nc.dram_tensor(f"in_{name}_dram", a.shape, mybir.dt.from_np(a.dtype), kind="ExternalInput").ap())
    shape = tuple(inputs['x'].shape)
    args.append(nc.dram_tensor("out_dram", shape, F32, kind="ExternalOutput").ap())
    perceiver_kernel(nc, *args)
    r = _run(nc, [arrays], core_ids=[0])
    return r.results[0]["out_dram"]
```

```python
from contextlib import ExitStack

import concourse.bass as bass
from concourse import mybir

ALU = mybir.AluOpType
ACT = mybir.ActivationFunctionType
AX_X = mybir.AxisListType.X
F32 = mybir.dt.float32
F16 = mybir.dt.float16
I32 = mybir.dt.int32
I16 = mybir.dt.int16

P = 128
WS = 64.0
AS = 1024.0
MAGIC = 12582912.0
PASSES = ((0, 0), (1, 0), (0, 1))


ONE = 1


def credit(eng, *sems):
    for s in sems:
        eng.sem_inc(s, ONE)


class Count:

    def __init__(self):
        self.n = 0

    def next(self, by=1):
        self.n += by
        return self.n


def perceiver_kernel(nc, x, ctx_1024, xWq, xWk, xWv, wih, whh, bih, bhh, slot_w, input_w,
                     aWq, aWkv, aWout, ab_out, pos_emb, gate_w, gate_up_w, down_w, out):
    B, N, D = x.shape
    M = ctx_1024.shape[1]
    C = D // P
    PAIRS = B * N // P
    MR = M // P
    MT = MR + 1
    TAIL = M - MR * P
    G = 3 * D
    XW = D + 2
    H = aWq.shape[1] // N
    DH = pos_emb.shape[0]
    HP = H // 2
    V1 = N + 1
    E = gate_up_w.shape[0]
    F = down_w.shape[1]
    FC = F // P
    TOK = B * N

    with ExitStack() as ctx:
        def sb(name, shape, dt, on=ctx):
            return on.enter_context(nc.sbuf_tensor(name, shape, dt))

        def sem(name):
            return ctx.enter_context(nc.semaphore(name))

        bank = ctx.enter_context(nc.psum_tensor("bank", [P, 8, 512], F32))
        bank16 = bank[:].bitcast(F16)
        x_sb = sb("x_sb", [P, PAIRS, D], F32)
        ident = sb("ident", [P, P], F32)
        ident16 = sb("ident16", [P, P], F16)
        flip16 = sb("flip16", [P, P], F16)
        stats = sb("stats", [P, PAIRS, 6], F32)
        mv = sb("mv", [P, PAIRS, 2], F32)
        half = sb("half", [P, 16], F32)
        lnr = sb("lnr", [P, PAIRS], F32)
        eps_rms = sb("eps_rms", [P, 16], F32)

        phase1 = ctx.enter_context(ExitStack())
        s0 = sb("s0", [P, PAIRS, D], F32, phase1)
        A16 = sb("A16", [P, 2, C, D], F16, phase1)
        wihT16 = sb("wihT16", [P, 2, C, G], F16, phase1)
        whhT16 = sb("whhT16", [P, 2, C, G], F16, phase1)
        ones16 = sb("ones16", [P, P], F16, phase1)
        LO = 32
        bias16 = sb("bias16", [P, 4 * D], F16, phase1)
        X32 = sb("X32", [P, 2, MT, D], F32, phase1)
        junk = sb("junk", [P, MT, D], F16, phase1)
        ssq = sb("ssq", [P, 2, MT], F32, phase1)

        loaded = [sem(f"loaded{i}") for i in range(2)]
        tail_clear = sem("tail_clear")
        sq_done = sem("sq_done")
        eps_added = sem("eps_added")
        ctx_main = ctx_1024[:, 0:MR * P, :].rearrange("b (p t) d -> b p t d", t=MR)
        ctx_tail = ctx_1024[:, MR * P:M, :]

        def load_rows(sp, b):
            sp.dma_start(X32[:, b % 2, 0:MR, :], ctx_main[b]).then_inc(loaded[b % 2], 16)
            sp.dma_start(X32[0:TAIL, b % 2, MR, :], ctx_tail[b]).then_inc(loaded[b % 2], 16)

        PIECES = ((0, MT // 2 + 1), (MT // 2 + 1, MT))

        def square_rows(act, b, piece):
            n = 2 * b + piece
            act.wait_ge(loaded[b % 2], 32 * (b // 2 + 1))
            act.wait_ge(tail_clear, 2)
            if n > 1:
                act.wait_ge(sq_done, n - 1)
            if b > 1:
                act.wait_ge(eps_added, b - 1)
            for t in range(*PIECES[piece]):
                ins = act.activation(junk[:, t, :], X32[:, b % 2, t, :], ACT.Square, scale=float(D) ** -0.5,
                                     accum_out=ssq[:, b % 2, t:t + 1])
            ins.then_inc(sq_done, 1)

        in_x, in_g, in_w, in_b, in_n = (sem(n) for n in ("in_x", "in_g", "in_w", "in_b", "in_n"))
        made = sem("made")
        folded = sem("folded")
        bias_sum = sem("bias_sum")
        bias_hi = sem("bias_hi")
        lv = sem("lv")
        la = sem("la")
        lp = sem("lp")
        lr = sem("lr")
        iw_done = sem("iw_done")
        A_full = sem("A_full")
        A_sw = sem("A_sw")
        A_done = sem("A_done")
        A_hi = sem("A_hi")
        gT_full = sem("gT_full")
        gT_done = sem("gT_done")
        hh_hi = sem("hh_hi")
        hh_lo = sem("hh_lo")
        ih_full = sem("ih_full")
        ih_hi = sem("ih_hi")
        with ExitStack() as p0:
            w3 = sb("w3", [P, 3, C, D], F32, p0)
            wg = sb("wg", [P, 2, G // P, D], F32, p0)
            wgT = sb("wgT", [P, C, G], F32, p0)
            A32 = sb("A32", [P, C, D], F32, p0)
            swc = sb("swc", [P, C], F32, p0)
            iwc = sb("iwc", [P, C], F32, p0)
            iwcs = sb("iwcs", [P, C], F32, p0)
            iwb = sb("iwb", [P, D], F32, p0)
            bb = sb("bb", [P, 2, G], F32, p0)
            b32 = sb("b32", [P, 4 * D], F32, p0)
            bhi = sb("bhi", [P, 4 * D], F16, p0)
            block = p0.enter_context(nc.Block())
            HALVES = ((0, 3 * P), (3 * P, G))

            @block.sync
            def _(sp):
                sp.dma_start(wg[:, 0], wih.rearrange("(c p) n -> p c n", p=P)).then_inc(in_g, 16)
                sp.dma_start(w3[:, 2], xWv.rearrange("(c p) n -> p c n", p=P)).then_inc(in_g, 16)
                sp.dma_start(wg[:, 1], whh.rearrange("(c p) n -> p c n", p=P)).then_inc(in_g, 16)
                for i, w in enumerate((xWq, xWk)):
                    sp.dma_start(w3[:, i], w.rearrange("(c p) n -> p c n", p=P)).then_inc(in_w, 16)
                for b in range(2):
                    sp.wait_ge(tail_clear, 2)
                    load_rows(sp, b)

            @block.gpsimd
            def _(pool):
                for q in range(2):
                    pool.memset(X32[:, q, MR, :], 0.0).then_inc(tail_clear, 1)
                pool.memset(eps_rms[:], 1e-6)
                pool.memset(half[:], -0.5).then_inc(made, 1)
                pool.memset(ident[:], 0.0).then_inc(made, 1)
                pool.memset(flip16[:], 0.0).then_inc(made, 1)
                pool.memset(ones16[:], 1.0)
                pool.memset(bias16[:], 0.0).then_inc(made, 1)
                pool.wait_ge(made, 4)
                pool.affine_select(out=ident[:], in_=ident[:], compare_op=ALU.not_equal, fill=1.0,
                                   base=0, pattern=[[-1, P]], channel_multiplier=1).then_inc(made, 1)
                for b in range(2):
                    part = flip16[:, b * N:(b + 1) * N]
                    pool.affine_select(out=part, in_=part, compare_op=ALU.not_equal, fill=1.0,
                                       base=-(N - 1) - b * N, pattern=[[1, N]],
                                       channel_multiplier=1).then_inc(made, 1)
                pool.wait_ge(made, 5)
                pool.tensor_copy(ident16[:], ident[:]).then_inc(made, 1)
                pool.wait_ge(la, PAIRS)
                pool.tensor_scalar(lnr[:], mv[:, :, 1], 1.0, 1e-5, ALU.mult, ALU.add).then_inc(lp, 1)
                pool.wait_ge(lp, 1)
                pool.tensor_tensor(lnr[:], lnr[:], half[:, 0:PAIRS], ALU.pow).then_inc(lr, 1)
                pool.wait_ge(bias_sum, 1)

            @block.tensor
            def _(pe):
                pe.wait_ge(made, 5)
                pe.wait_ge(in_g, 48)
                for i in range(2):
                    for c in range(C):
                        for k, (g0, g1) in enumerate(HALVES):
                            for g in range(g0, g1, P):
                                last = pe.transpose(bank[:, i * 4 + c * 2 + k, g - g0:g - g0 + P],
                                                    wg[:, i, g // P, c * P:(c + 1) * P], ident[:])
                            last.then_inc(gT_full, 1)
                pe.wait_ge(in_w, 32)
                pe.wait_ge(gT_done, 4)
                for d in range(C):
                    for o in range(C):
                        last = pe.matmul(bank[:, d, 0:D], w3[:, 0, o, d * P:(d + 1) * P], w3[:, 1, o, :],
                                         start=(o == 0), stop=(o == C - 1))
                last.then_inc(A_full, 1)
                pe.wait_ge(hh_lo, 4)
                for e in range(C):
                    for k, (g0, g1) in enumerate(HALVES):
                        for o in range(C):
                            last = pe.matmul(bank[:, 4 + 2 * e + k, 0:g1 - g0], w3[:, 2, o, e * P:(e + 1) * P],
                                             wgT[:, o, g0:g1], start=(o == 0), stop=(o == C - 1))
                        last.then_inc(ih_full, 1)

            @block.scalar
            def _(act):
                act.dma_start(x_sb[:], x.rearrange("b k d -> (b k) d").rearrange("(q p) d -> p q d", p=P)
                              ).then_inc(in_x, 16)
                for i, b in enumerate((bih, bhh)):
                    act.dma_start(bb[:, i], b.rearrange("(a n) -> a n", a=1).broadcast_to([P, G])).then_inc(in_b, 16)
                act.dma_start(iwb[:], input_w.rearrange("(a n) -> a n", a=1).broadcast_to([P, D])).then_inc(in_n, 16)
                act.dma_start(swc[:], slot_w.rearrange("(c p) -> p c", p=P),
                              allow_slow_non_contiguous=True).then_inc(in_n, 16)
                act.dma_start(iwc[:], input_w.rearrange("(c p) -> p c", p=P),
                              allow_slow_non_contiguous=True).then_inc(in_n, 16)
                act.wait_ge(bias_sum, 1)
                act.activation(bhi[:], b32[:], ACT.Copy, scale=WS).then_inc(bias_hi, 1)
                for c in range(C):
                    for k, (g0, g1) in enumerate(HALVES):
                        act.wait_ge(gT_full, 4 + c * 2 + k + 1)
                        act.activation(whhT16[:, 0, c, g0:g1], bank[:, 4 + c * 2 + k, 0:g1 - g0], ACT.Copy,
                                       scale=WS).then_inc(hh_hi, 1)
                act.wait_ge(A_done, 1)
                act.activation(A16[:, 0], A32[:], ACT.Copy).then_inc(A_hi, 1)
                for piece in range(2):
                    square_rows(act, 0, piece)
                act.wait_ge(iw_done, 1)
                for e in range(C):
                    for k, (g0, g1) in enumerate(HALVES):
                        act.wait_ge(ih_full, e * 2 + k + 1)
                        act.activation(wihT16[:, 0, e, g0:g1], bank[:, 4 + 2 * e + k, 0:g1 - g0], ACT.Copy,
                                       scale=iwcs[:, e:e + 1]).then_inc(ih_hi, 1)
                for piece in range(2):
                    square_rows(act, 1, piece)

            @block.vector
            def _(dve):
                dve.wait_ge(in_x, 16)
                for q in range(PAIRS):
                    dve.bn_stats(stats[:, q, :], x_sb[:, q, :]).then_inc(lv, 1)
                for q in range(PAIRS):
                    dve.wait_ge(lv, q + 1)
                    dve.bn_aggr(mv[:, q, :], stats[:, q, :]).then_inc(la, 1)
                dve.wait_ge(in_b, 32)
                dve.tensor_tensor(b32[:, 0:2 * D], bb[:, 0, 0:2 * D], bb[:, 1, 0:2 * D], ALU.add)
                dve.tensor_copy(b32[:, 2 * D:3 * D], bb[:, 0, 2 * D:G])
                dve.tensor_copy(b32[:, 3 * D:4 * D], bb[:, 1, 2 * D:G]).then_inc(bias_sum, 1)
                dve.wait_ge(bias_hi, 1)
                dve.wait_ge(bias_sum, 1)
                dve.wait_ge(made, 4)
                dve.tensor_copy(bias16[0:1, :], bhi[0:1, :])
                dve.scalar_tensor_tensor(bias16[LO:LO + 1, :], b32[LO:LO + 1, :], WS, bhi[LO:LO + 1, :],
                                         ALU.mult, ALU.subtract).then_inc(folded, 1)
                dve.wait_ge(in_n, 48)
                dve.tensor_scalar(iwcs[:], iwc[:], WS, None, ALU.mult).then_inc(iw_done, 1)
                dve.wait_ge(la, PAIRS)
                dve.wait_ge(lr, 1)
                for q in range(PAIRS):
                    dve.tensor_scalar(s0[:, q], x_sb[:, q], mv[:, q, 0:1], lnr[:, q:q + 1],
                                      ALU.subtract, ALU.mult).then_inc(folded, 1)
                for c in range(C):
                    for k, (g0, g1) in enumerate(HALVES):
                        dve.wait_ge(gT_full, c * 2 + k + 1)
                        dve.tensor_copy(wgT[:, c, g0:g1], bank[:, c * 2 + k, 0:g1 - g0]).then_inc(gT_done, 1)
                for c in range(C):
                    for k, (g0, g1) in enumerate(HALVES):
                        dve.wait_ge(hh_hi, c * 2 + k + 1)
                        dve.scalar_tensor_tensor(whhT16[:, 1, c, g0:g1], bank[:, 4 + c * 2 + k, 0:g1 - g0], WS,
                                                 whhT16[:, 0, c, g0:g1], ALU.mult, ALU.subtract).then_inc(hh_lo, 1)
                dve.wait_ge(A_full, 1)
                for d in range(C):
                    ins = dve.scalar_tensor_tensor(A32[:, d], bank[:, d, 0:D], swc[:, d:d + 1], iwb[:],
                                                   ALU.mult, ALU.mult)
                ins.then_inc(A_sw, 1)
                dve.wait_ge(A_sw, 1)
                dve.tensor_scalar(A32[:], A32[:], WS, None, ALU.mult).then_inc(A_done, 1)
                dve.wait_ge(A_done, 1)
                dve.wait_ge(A_hi, 1)
                dve.tensor_tensor(A16[:, 1], A32[:], A16[:, 0], ALU.subtract).then_inc(folded, 1)
                dve.wait_ge(iw_done, 1)
                for e in range(C):
                    for k, (g0, g1) in enumerate(HALVES):
                        dve.wait_ge(ih_hi, e * 2 + k + 1)
                        dve.scalar_tensor_tensor(wihT16[:, 1, e, g0:g1], bank[:, 4 + 2 * e + k, 0:g1 - g0],
                                                 iwcs[:, e:e + 1], wihT16[:, 0, e, g0:g1], ALU.mult,
                                                 ALU.subtract).then_inc(folded, 1)

        GROUP = 6
        STEPS = GROUP * PAIRS // 2
        XN = sb("XN", [P, 2, 2, MT, 2, XW], F16, phase1)
        XT = sb("XT", [P, 2, 2, MT, 4, P], F16, phase1)
        rinv = sb("rinv", [P, 2, MT], F32, phase1)
        LOW_DVE = 9
        rest32 = sb("rest32", [P, MT - LOW_DVE, D], F32, phase1)
        mx = sb("mx", [P, 2, MT], F32, phase1)
        sm = sb("sm", [P, 2, MT], F32, phase1)
        e32 = sb("e32", [P, 2, MT, N], F32, phase1)
        at16 = sb("at16", [P, 2, 2, MT, N], F16, phase1)
        h32 = sb("h32", [P, 2, D], F32, phase1)
        snT16 = sb("snT16", [P, 4, P], F16, phase1)
        gT16 = sb("gT16", [P, 2, 4, P], F16, phase1)
        hs16 = sb("hs16", [P, 2, 2, D], F16, phase1)
        sn32 = sb("sn32", [P, D], F32, phase1)
        qT16 = sb("qT16", [P, 2, 2, C, P], F16, phase1)
        ssq1 = sb("ssq1", [P, 2], F32, phase1)
        r1 = sb("r1", [P, 2], F32, phase1)
        urs = sb("urs", [P, 1], F32, phase1)
        upd = sb("upd", [P, D], F32, phase1)
        upd16 = sb("upd16", [P, 2, D], F16, phase1)
        rz = sb("rz", [P, 2 * D], F32, phase1)
        cand = sb("cand", [P, D], F32, phase1)
        gtmp = sb("gtmp", [P, D], F32, phase1)

        SC = [bank[:, 2 * k:2 * k + 2, :].rearrange("p b n -> p (b n)") for k in range(2)]
        SC16 = [bank16[:, 2 * k:2 * k + 2, :].rearrange("p b n -> p (b n)") for k in range(2)]
        U = bank[:, 4, :]
        T16, TQ = bank16[:, 5, :], bank[:, 5, :]
        RZ, NB = bank[:, 6, :], bank[:, 7, :]

        split_done = sem("split_done")
        split_rest = sem("split_rest")
        rest_scaled = sem("rest_scaled")
        ones_set = sem("ones_set")
        rinv_ready = sem("rinv_ready")
        xhi_done = sem("xhi_done")
        slot_full = sem("slot_full")
        slot_free = sem("slot_free")
        exp_done = sem("exp_done")
        at32_done = sem("at32_done")
        athi_done = sem("athi_done")
        atlo0_done = sem("atlo0_done")
        atlo1_done = sem("atlo1_done")
        u_done = sem("u_done")
        u_free = sem("u_free")
        uhi_done = sem("uhi_done")
        ulo_done = sem("ulo_done")
        rz_full = sem("rz_full")
        new_full = sem("new_full")
        rz_tanh = sem("rz_tanh")
        n_sum = sem("n_sum")
        n_tanh = sem("n_tanh")
        state_set = sem("state_set")
        state_done = sem("state_done")
        x_added = sem("x_added")
        ssq1_done = sem("ssq1_done")
        r1_eps = sem("r1_eps")
        r1_ready = sem("r1_ready")
        sn_ready = sem("sn_ready")
        snhi_done = sem("snhi_done")
        snlo_done = sem("snlo_done")
        hhi_done = sem("hhi_done")
        hlo_done = sem("hlo_done")
        t_full = sem("t_full")
        snT_ready = sem("snT_ready")
        turned_gates = sem("turned_gates")
        gT_ready = sem("gT_ready")
        q_full = sem("q_full")
        qhi_done = sem("qhi_done")
        q_ready = sem("q_ready")
        dve_step = sem("dve_step")

        def pair_of(s):
            return 2 * (s // GROUP) + s % 2

        def first_step(s):
            return s % GROUP < 2

        def last_step(s):
            return s % GROUP >= GROUP - 2

        def batches_before(s):
            return (2 * pair_of(s), 2 * pair_of(s) + 1) if s < STEPS and first_step(s) else ()

        def wait_state(eng, s):
            if first_step(s):
                eng.wait_ge(state_set, pair_of(s) + 1)
            else:
                eng.wait_ge(state_done, s - 1)

        SQUARE = {-1: {"end": ((2, 0), (2, 1))}, 0: {"early": ((3, 0), (3, 1))}, 1: {"early": ((4, 0),)},
                  2: {"early": ((4, 1),)}, 3: {"early": ((5, 0),)}, 4: {"early": ((5, 1),)},
                  5: {"end": ((6, 0), (6, 1))}, 6: {"middle": ((7, 0),), "late": ((7, 1),)}}
        HIGH = {-1: {"late": ((0, 0), (0, 1), (1, 0), (1, 1))},
                0: {"early": ((2, 0),), "middle": ((2, 1),), "late": ((3, 0), (3, 1))},
                5: {"early": ((4, 0),), "middle": ((4, 1),), "late": ((5, 0), (5, 1))},
                6: {"early": ((6, 0),), "middle": ((6, 1),), "late": ((7, 0), (7, 1))}}
        SCALE = {-1: ((0, 1), (2,)), 0: ((3,), ()), 3: ((4,), ()), 5: ((5,), (6,)), 6: ((), (7,))}
        TH = 7

        with ExitStack() as p1:
            block = p1.enter_context(nc.Block())

            @block.sync
            def _(sp):
                for b in range(2, B):
                    sp.wait_ge(split_done, b - 1)
                    sp.wait_ge(split_rest, b - 1)
                    load_rows(sp, b)

            @block.gpsimd
            def _(pool):
                def rinv_of(b):
                    pool.wait_ge(sq_done, 2 * b + 2)
                    if b > 1:
                        pool.wait_ge(split_done, b - 1)
                        pool.wait_ge(split_rest, b - 1)
                    pool.tensor_tensor(rinv[:, b % 2], ssq[:, b % 2], eps_rms[:, 0:MT],
                                       ALU.add).then_inc(eps_added, 1)
                    pool.wait_ge(eps_added, b + 1)
                    pool.tensor_tensor(rinv[:, b % 2], rinv[:, b % 2], half[:, 0:MT],
                                       ALU.pow).then_inc(rinv_ready, 1)

                def low_attention(s):
                    if s:
                        pool.wait_ge(u_done, 2 * s - 1)
                    for i, t in enumerate((slice(0, TH), slice(TH, MT))):
                        pool.wait_ge(at32_done, 2 * s + 1)
                        pool.wait_ge(athi_done, 3 * s + i + 1)
                        pool.tensor_tensor(at16[:, 0, 1, t], e32[:, 0, t], at16[:, 0, 0, t],
                                           ALU.subtract).then_inc(atlo0_done, 1)

                def low_rows(b):
                    rows = slice(LOW_DVE, MT)
                    pool.wait_ge(rinv_ready, b + 1)
                    if b:
                        pool.wait_ge(split_rest, b)
                    pool.tensor_tensor(rest32[:], X32[:, b % 2, rows, :],
                                       rinv[:, b % 2, rows].unsqueeze(2).broadcast_to([P, MT - LOW_DVE, D]),
                                       ALU.mult).then_inc(rest_scaled, 1)
                    pool.wait_ge(rest_scaled, b + 1)
                    pool.wait_ge(xhi_done, 2 * b + 2)
                    pool.tensor_tensor(XN[:, (b // 2) % 2, b % 2, rows, 1, 0:D], rest32[:],
                                       XN[:, (b // 2) % 2, b % 2, rows, 0, 0:D],
                                       ALU.subtract).then_inc(split_rest, 1)

                def state_scale(s):
                    X = s % 2
                    pool.wait_ge(ssq1_done, s + 1)
                    if s > 1:
                        pool.wait_ge(sn_ready, s - 1)
                    pool.tensor_tensor(r1[:, X:X + 1], ssq1[:, X:X + 1], eps_rms[:, 0:1],
                                       ALU.add).then_inc(r1_eps, 1)
                    pool.wait_ge(r1_eps, s + 1)
                    pool.tensor_tensor(r1[:, X:X + 1], r1[:, X:X + 1], half[:, 0:1], ALU.pow).then_inc(r1_ready, 1)
                    pool.wait_ge(hhi_done, s + 1)
                    if s:
                        pool.wait_ge(turned_gates, s)
                    wait_state(pool, s)
                    pool.tensor_tensor(hs16[:, 1, 1], h32[:, X], hs16[:, 1, 0], ALU.subtract).then_inc(hlo_done, 1)

                def add_state(s):
                    pool.wait_ge(state_done, s + 1)
                    pool.tensor_tensor(x_sb[:, pair_of(s)], x_sb[:, pair_of(s)], h32[:, s % 2],
                                       ALU.add).then_inc(x_added, 1)

                for s in range(-1, STEPS + 1):
                    if s - 1 >= 0 and s == STEPS:
                        add_state(s - 1)
                        continue
                    early, late = SCALE.get(s, ((), ()))
                    for b in early:
                        rinv_of(b)
                    if s >= 0:
                        low_attention(s)
                    if s >= 1 and last_step(s - 1):
                        add_state(s - 1)
                    if s + 1 < STEPS:
                        state_scale(s + 1)
                    ahead = batches_before(s + 1)
                    for b in ahead:
                        for r in late:
                            if r == b:
                                rinv_of(b)
                        low_rows(b)
                    for b in late:
                        if b not in ahead:
                            rinv_of(b)

            @block.scalar
            def _(act):
                slots = Count()

                def high_rows(b, piece):
                    act.wait_ge(rinv_ready, b + 1)
                    X = (b // 2) % 2
                    if b > 3:
                        act.wait_ge(u_done, 2 * (GROUP * (b // 4) + X - 2) + 2)
                    for t in range(*PIECES[piece]):
                        ins = act.activation(XN[:, X, b % 2, t, 0, 0:D], X32[:, b % 2, t, :], ACT.Copy,
                                             scale=rinv[:, b % 2, t:t + 1])
                    ins.then_inc(xhi_done, 1)

                def high_update(s):
                    act.wait_ge(u_free, s + 1)
                    if s:
                        act.wait_ge(turned_gates, s + 1)
                    act.activation(upd16[:, 0], upd[:], ACT.Copy).then_inc(uhi_done, 1)

                def take_turned(s):
                    a, b = (0 if s < STEPS else 1), (2 if s else 1)
                    act.wait_ge(turned_gates, s + 1)
                    act.activation(gT16[:, a:b].rearrange("p g a n -> p (g a n)"),
                                   T16[:, a * 4 * P:b * 4 * P], ACT.Copy).then_inc(gT_ready, 1)

                def exponentials(s, j):
                    act.wait_ge(slot_free, slots.next())
                    act.activation(e32[:, j], e32[:, j], ACT.Exp, scale=float(D) ** -0.5).then_inc(exp_done, 1)

                def high_attention(s, j):
                    act.wait_ge(at32_done, 2 * s + j + 1)
                    if s:
                        act.wait_ge(u_done, 2 * s + j - 1)
                    for t in (slice(0, TH), slice(TH, MT)) if j == 0 else (slice(0, MT),):
                        act.activation(at16[:, j, 0, t], e32[:, j, t], ACT.Copy).then_inc(athi_done, 1)

                def gates(s):
                    act.wait_ge(rz_full, s + 1)
                    if s:
                        act.wait_ge(state_done, s)
                    for half_ in range(2):
                        cols = slice(half_ * D, (half_ + 1) * D)
                        act.activation(rz[:, cols], RZ[:, cols], ACT.Tanh, scale=0.5 / WS).then_inc(rz_tanh, 1)

                def candidate(s):
                    act.wait_ge(n_sum, s + 1)
                    act.activation(cand[:], cand[:], ACT.Tanh, scale=1.0 / WS).then_inc(n_tanh, 1)

                def high_state(s):
                    X = s % 2
                    wait_state(act, s)
                    if s:
                        act.wait_ge(turned_gates, s)
                    if s > 1:
                        act.wait_ge(r1_ready, s - 1)
                    act.activation(hs16[:, 0, 0], h32[:, X], ACT.Square, scale=float(D) ** -0.5,
                                   accum_out=ssq1[:, X:X + 1]).then_inc(ssq1_done, 1)
                    act.activation(hs16[:, 1, 0], h32[:, X], ACT.Copy).then_inc(hhi_done, 1)

                def high_normalised(s):
                    act.wait_ge(sn_ready, s + 1)
                    act.activation(hs16[:, 0, 0], sn32[:], ACT.Copy).then_inc(snhi_done, 1)

                def high_query(s):
                    act.wait_ge(q_full, s + 1)
                    act.activation(qT16[:, s % 2, 0].rearrange("p c n -> p (c n)"), TQ[:, 0:D],
                                   ACT.Copy, scale=1.0 / WS).then_inc(qhi_done, 1)

                for s in range(-1, STEPS + 1):
                    def squares(when):
                        for b, piece in SQUARE.get(s, {}).get(when, ()):
                            square_rows(act, b, piece)

                    def highs(when, which=range(B)):
                        for b, piece in HIGH.get(s, {}).get(when, ()):
                            if b in which:
                                high_rows(b, piece)

                    ahead = batches_before(s + 1)
                    if s >= 1:
                        high_update(s - 1)
                    squares("early")
                    highs("early")
                    if s >= 0:
                        take_turned(s)
                    if 0 <= s < STEPS:
                        exponentials(s, 0)
                    if s >= 1:
                        gates(s - 1)
                    if 0 <= s < STEPS:
                        exponentials(s, 1)
                    highs("middle")
                    squares("middle")
                    if 0 <= s < STEPS:
                        high_attention(s, 0)
                    if s >= 1:
                        candidate(s - 1)
                    if 0 <= s < STEPS:
                        high_attention(s, 1)
                    squares("late")
                    if s + 1 < STEPS:
                        high_state(s + 1)
                        highs("late", ahead[:1])
                        high_normalised(s + 1)
                        highs("late", ahead[1:])
                        high_query(s + 1)
                    slots.next(4 * len(ahead))
                    squares("end")

            @block.tensor
            def _(pe):
                slots = Count()

                def slot():
                    k = slots.n % 2
                    if slots.next() > 2:
                        pe.wait_ge(slot_free, slots.n - 2)
                    return k

                def split_matmul(out_, stat, mov, cs, first=True, last_=True):
                    todo = [(c, a, b) for c in cs for a, b in PASSES]
                    for i, (c, a, b) in enumerate(todo):
                        ins = pe.matmul(out_, stat(a, c), mov(b, c), start=(first and i == 0),
                                        stop=(last_ and i == len(todo) - 1))
                    return ins

                def turn_rows(b):
                    pe.wait_ge(split_done, b + 1)
                    for t0 in range(0, MT, 4):
                        if t0 + 4 > LOW_DVE:
                            pe.wait_ge(split_rest, b + 1)
                        k = slot()
                        for t in range(t0, min(t0 + 4, MT)):
                            for part in range(2):
                                for c in range(C):
                                    o = ((t - t0) * 4 + part * C + c) * P
                                    last = pe.transpose(SC16[k][:, o:o + P],
                                                        XN[:, (b // 2) % 2, b % 2, t, part, c * P:(c + 1) * P],
                                                        ident16[:])
                        last.then_inc(slot_full, 1)

                def bias(out_, cols, **kw):
                    pe.matmul(out_, ones16[0:LO + 1, :], bias16[0:LO + 1, cols], start=True, **kw)

                def gates_of_state(s):
                    pe.wait_ge(gT_ready, s + 1)
                    if s:
                        pe.wait_ge(rz_tanh, 2 * s)
                    hp = lambda a, c: gT16[:, 0, a * C + c, :]
                    bias(RZ, slice(0, 2 * D), stop=False)
                    split_matmul(RZ, hp, lambda b, c: whhT16[:, b, c, 0:2 * D], range(C), False, False)
                    if s:
                        pe.wait_ge(n_sum, s)
                    bias(NB[:, D:2 * D], slice(3 * D, 4 * D), stop=False)
                    split_matmul(NB[:, D:2 * D], hp, lambda b, c: whhT16[:, b, c, 2 * D:G], range(C), False)

                def gates_of_update(s):
                    pe.wait_ge(gT_ready, s + 2)
                    up = lambda a, c: gT16[:, 1, a * C + c, :]
                    split_matmul(RZ, up, lambda b, c: wihT16[:, b, c, 0:2 * D], range(C), False).then_inc(rz_full, 1)
                    bias(NB[:, 0:D], slice(2 * D, 3 * D), stop=False)
                    split_matmul(NB[:, 0:D], up, lambda b, c: wihT16[:, b, c, 2 * D:G], range(C),
                                 False).then_inc(new_full, 1)

                def scores(s):
                    X = s % 2
                    pe.wait_ge(q_ready, s + 1)
                    if first_step(s):
                        pe.wait_ge(slot_free, slots.n)
                    for j in range(2):
                        k = slot()
                        for t in range(MT):
                            last = split_matmul(SC[k][:, t * N:(t + 1) * N],
                                                lambda a, c: XT[:, X, j, t, a * C + c, :],
                                                lambda b, c: qT16[:, X, b, c, j * N:(j + 1) * N], range(C))
                        last.then_inc(slot_full, 1)
                        if j == 0:
                            turn_gates(s)

                def update(s, j, t0, t1):
                    for t in range(t0, t1):
                        for i, (a, b) in enumerate(PASSES):
                            w = D + 1 if b == 0 else D
                            ins = pe.matmul(U[j * N:(j + 1) * N, 0:w], at16[:, j, a, t, :],
                                            XN[:, s % 2, j, t, b, 0:w], start=(t == 0 and i == 0),
                                            stop=(t == MT - 1 and i == 2))
                    return ins

                def update_first(s):
                    if s:
                        pe.wait_ge(u_free, s)
                    for i, (t0, t1) in enumerate(((0, TH), (TH, MT))):
                        pe.wait_ge(athi_done, 3 * s + i + 1)
                        pe.wait_ge(atlo0_done, 2 * s + i + 1)
                        last = update(s, 0, t0, t1)
                    last.then_inc(u_done, 1)

                def turn(o, tile):
                    for part in range(2):
                        for c in range(C):
                            last = pe.transpose(T16[:, o:o + P], tile[:, part, c * P:(c + 1) * P], ident16[:])
                            o += P
                    return last

                def turn_state(s):
                    if s:
                        pe.wait_ge(gT_ready, s)
                    pe.wait_ge(snlo_done, s + 1)
                    turn(0, hs16[:, 0]).then_inc(t_full, 1)

                def turn_gates(s):
                    if s < STEPS:
                        pe.wait_ge(q_ready, s + 1)
                        pe.wait_ge(hlo_done, s + 1)
                        last = turn(0, hs16[:, 1])
                    if s:
                        pe.wait_ge(ulo_done, s)
                        last = turn(4 * P, upd16)
                    last.then_inc(turned_gates, 1)

                def query(s):
                    pe.wait_ge(snT_ready, s + 1)
                    for e in range(C):
                        last = split_matmul(TQ[:, e * P:(e + 1) * P],
                                            lambda a, c: A16[:, a, c, e * P:(e + 1) * P],
                                            lambda b, c: snT16[:, b * C + c, :], range(C))
                    last.then_inc(q_full, 1)

                for s in range(-1, STEPS + 1):
                    live = 0 <= s < STEPS
                    if live:
                        scores(s)
                    elif s == STEPS:
                        turn_gates(s)
                    if s >= 1:
                        gates_of_update(s - 1)
                    if live:
                        gates_of_state(s)
                        update_first(s)
                        pe.wait_ge(athi_done, 3 * s + 3)
                        pe.wait_ge(atlo1_done, s + 1)
                        update(s, 1, 0, MT // 3)
                    if s + 1 < STEPS:
                        ahead = batches_before(s + 1)
                        if not ahead:
                            turn_state(s + 1)
                        if live:
                            update(s, 1, MT // 3, 2 * MT // 3)
                        if not ahead:
                            query(s + 1)
                        if live:
                            update(s, 1, 2 * MT // 3, MT).then_inc(u_done, 1)
                        if ahead:
                            turn_state(s + 1)
                            turn_rows(ahead[0])
                            query(s + 1)
                            turn_rows(ahead[1])
                    elif live:
                        update(s, 1, MT // 3, MT).then_inc(u_done, 1)

            @block.vector
            def _(dve):
                slots = Count()
                steps = Count()
                for q in range(4):
                    col = XN[:, q // 2, q % 2]
                    dve.memset(col[:, 0:MR, 0, D:XW], 1.0)
                    dve.memset(col[:, :, 1, D:XW], 0.0)
                    dve.memset(col[:, MR, 0, D:XW], 0.0).then_inc(ones_set, 1)
                dve.wait_ge(ones_set, 4)
                for q in range(4):
                    dve.memset(XN[0:TAIL, q // 2, q % 2, MR, 0, D:XW], 1.0).then_inc(ones_set, 1)

                def link(ins):
                    ins.then_inc(dve_step, 1)
                    dve.wait_ge(dve_step, steps.next())

                def low_rows(b):
                    X = (b // 2) % 2
                    dve.wait_ge(xhi_done, 2 * b + 1)
                    for t in range(LOW_DVE):
                        if t == PIECES[1][0]:
                            dve.wait_ge(xhi_done, 2 * b + 2)
                        ins = dve.scalar_tensor_tensor(XN[:, X, b % 2, t, 1, 0:D], X32[:, b % 2, t, :],
                                                       rinv[:, b % 2, t:t + 1], XN[:, X, b % 2, t, 0, 0:D],
                                                       ALU.mult, ALU.subtract)
                    ins.then_inc(split_done, 1)

                def take_rows(b):
                    for t0 in range(0, MT, 4):
                        k = slots.n % 2
                        w = min(4, MT - t0)
                        dve.wait_ge(slot_full, slots.next())
                        dve.tensor_copy(XT[:, (b // 2) % 2, b % 2, t0:t0 + w].rearrange("p t a n -> p (t a n)"),
                                        SC16[k][:, 0:w * 4 * P]).then_inc(slot_free, 1)

                def shift(s, j):
                    k = slots.n % 2
                    dve.wait_ge(slot_full, slots.next())
                    sc = SC[k][:, 0:MT * N].rearrange("p (t n) -> p t n", n=N)
                    link(dve.reduce_max(mx[:, j], sc, AX_X))
                    if s and j == 0:
                        dve.wait_ge(atlo0_done, 2 * s)
                    elif s:
                        dve.wait_ge(atlo1_done, s)
                    dve.tensor_tensor(e32[:, j], sc, mx[:, j].unsqueeze(2).broadcast_to([P, MT, N]),
                                      ALU.subtract).then_inc(slot_free, 1)

                def norm(s, j):
                    dve.wait_ge(exp_done, 2 * s + j + 1)
                    link(dve.reduce_sum(sm[:, j], e32[:, j], AX_X))
                    link(dve.reciprocal(sm[:, j], sm[:, j]))
                    dve.scalar_tensor_tensor(e32[:, j], e32[:, j], AS,
                                             sm[:, j].unsqueeze(2).broadcast_to([P, MT, N]),
                                             ALU.mult, ALU.mult).then_inc(at32_done, 1)

                def low_attention(s):
                    dve.wait_ge(at32_done, 2 * s + 2)
                    dve.wait_ge(athi_done, 3 * s + 3)
                    if s:
                        dve.wait_ge(u_done, 2 * s)
                    dve.tensor_tensor(at16[:, 1, 1], e32[:, 1], at16[:, 1, 0], ALU.subtract).then_inc(atlo1_done, 1)

                def take_update(s):
                    dve.wait_ge(u_done, 2 * s + 2)
                    if s:
                        dve.wait_ge(ulo_done, s)
                    link(dve.tensor_scalar(urs[:], U[:, D:D + 1], AS * 1e-6, None, ALU.add))
                    link(dve.reciprocal(urs[:], urs[:]))
                    dve.tensor_scalar(upd[:], U[:, 0:D], urs[:], None, ALU.mult).then_inc(u_free, 1)
                    dve.wait_ge(u_free, s + 1)
                    dve.wait_ge(uhi_done, s + 1)
                    dve.tensor_tensor(upd16[:, 1], upd[:], upd16[:, 0], ALU.subtract).then_inc(ulo_done, 1)

                def candidate(s):
                    dve.wait_ge(rz_tanh, 2 * s + 1)
                    dve.wait_ge(new_full, s + 1)
                    if s:
                        dve.wait_ge(state_done, s)
                    link(dve.scalar_tensor_tensor(gtmp[:], rz[:, 0:D], 1.0, NB[:, D:2 * D], ALU.add, ALU.mult))
                    dve.scalar_tensor_tensor(cand[:], gtmp[:], 0.5, NB[:, 0:D], ALU.mult, ALU.add).then_inc(n_sum, 1)

                def new_state(s):
                    X = s % 2
                    dve.wait_ge(n_tanh, s + 1)
                    dve.wait_ge(rz_tanh, 2 * s + 2)
                    link(dve.tensor_tensor(gtmp[:], h32[:, X], cand[:], ALU.subtract))
                    link(dve.scalar_tensor_tensor(gtmp[:], rz[:, D:2 * D], 1.0, gtmp[:], ALU.add, ALU.mult))
                    dve.scalar_tensor_tensor(h32[:, X], gtmp[:], 0.5, cand[:], ALU.mult,
                                             ALU.add).then_inc(state_done, 1)

                def first_state(s):
                    if s > 1:
                        dve.wait_ge(x_added, pair_of(s) - 1)
                    dve.tensor_copy(h32[:, s % 2], s0[:, pair_of(s)]).then_inc(state_set, 1)

                def normalise_state(s):
                    X = s % 2
                    wait_state(dve, s)
                    dve.wait_ge(r1_ready, s + 1)
                    dve.tensor_scalar(sn32[:], h32[:, X], r1[:, X:X + 1], None, ALU.mult).then_inc(sn_ready, 1)

                def low_normalised(s):
                    dve.wait_ge(snhi_done, s + 1)
                    dve.wait_ge(sn_ready, s + 1)
                    dve.tensor_tensor(hs16[:, 0, 1], sn32[:], hs16[:, 0, 0], ALU.subtract).then_inc(snlo_done, 1)

                def query(s):
                    X = s % 2
                    dve.wait_ge(t_full, s + 1)
                    dve.tensor_copy(snT16[:].rearrange("p a n -> p (a n)"), T16[:, 0:4 * P]).then_inc(snT_ready, 1)
                    dve.wait_ge(qhi_done, s + 1)
                    dve.scalar_tensor_tensor(qT16[:, X, 1].rearrange("p c n -> p (c n)"), TQ[:, 0:D], 1.0 / WS,
                                             qT16[:, X, 0].rearrange("p c n -> p (c n)"),
                                             ALU.mult, ALU.subtract).then_inc(q_ready, 1)

                for s in range(-1, STEPS + 1):
                    live = 0 <= s < STEPS
                    ahead = batches_before(s + 1)
                    if s >= 1:
                        take_update(s - 1)
                    if live:
                        shift(s, 0)
                        shift(s, 1)
                        norm(s, 0)
                    if s >= 1:
                        candidate(s - 1)
                    if live:
                        norm(s, 1)
                    if s >= 1:
                        new_state(s - 1)
                    if live:
                        low_attention(s)
                    if s + 1 < STEPS:
                        if ahead:
                            first_state(s + 1)
                        normalise_state(s + 1)
                        for b in ahead[:1]:
                            low_rows(b)
                        low_normalised(s + 1)
                        for b in ahead[:1]:
                            take_rows(b)
                        for b in ahead[1:]:
                            low_rows(b)
                        query(s + 1)
                        for b in ahead[1:]:
                            take_rows(b)

        phase1.close()
        HW = H * N
        W65 = H * V1
        KC = H * DH // P
        BITS = [64, 32, 16, 8, 4, 2, 1]

        with ExitStack() as p2:
            wq32 = sb("wq32", [P, C, H * DH], F32, p2)
            wkv32 = sb("wkv32", [P, C, 2 * H * DH], F32, p2)
            wo32 = sb("wo32", [P, KC, D], F32, p2)
            pos32 = sb("pos32", [P, DH], F32, p2)
            wq16 = sb("wq16", [P, 2, C, H * DH], F16, p2)
            wkv16 = sb("wkv16", [P, 2, C, 2 * H * DH], F16, p2)
            wo16 = sb("wo16", [P, 2, KC, D], F16, p2)
            pos16 = sb("pos16", [P, 2, DH], F16, p2)
            bo = sb("bo", [P, D], F32, p2)
            reset = sb("reset", [P, H, V1], F32, p2)
            ones = sb("ones", [P, H, V1], F32, p2)
            vpos = sb("vpos", [P, H, V1], F32, p2)
            a_stats = sb("a_stats", [P, PAIRS, 6], F32, p2)
            a_mv = sb("a_mv", [P, PAIRS, 2], F32, p2)
            a_r = sb("a_r", [P, PAIRS], F32, p2)
            a_x = sb("a_x", [P, D], F32, p2)
            a_x16 = sb("a_x16", [P, 2, D], F16, p2)
            xT16 = sb("xT16", [P, 2, 2, C, P], F16, p2)
            q16 = sb("q16", [P, 2, 2, KC, P], F16, p2)
            k16 = sb("k16", [P, 2, 2, KC, P], F16, p2)
            v16 = sb("v16", [P, 2, 2, H * DH], F16, p2)
            gs = sb("gs", [P, H, V1], F32, p2)
            fl = sb("fl", [P, H, V1], F32, p2)
            ar = sb("ar", [P, H, V1], F32, p2)
            viota = sb("viota", [P, H, V1], I32, p2)
            s16 = sb("s16", [P, H, V1], I16, p2)
            mask = sb("mask", [P, len(BITS), H, V1], I16, p2)
            tab = sb("tab", [P, 2, 2, H, V1], F32, p2)
            lg = sb("lg", [P, 2, H, N], F32, p2)
            hs_ = sb("hs_", [P, 2, H], F32, p2)
            p16 = sb("p16", [P, 2, 2, H, 2, N], F16, p2)
            pT16 = sb("pT16", [P, 2, H, P], F16, p2)
            o16 = sb("o16", [P, 2, KC, P], F16, p2)
            tmp = sb("tmp", [P, D], F32, p2)

            w_in = [sem(f"w_in{i}") for i in range(4)]
            a_const = sem("a_const")
            a_zero = sem("a_zero")
            a_whi = sem("a_whi")
            a_wlo = sem("a_wlo")
            ln_st = sem("ln_st")
            ln_mv = sem("ln_mv")
            ln_pool = sem("ln_pool")
            ln_r = sem("ln_r")
            ln_x = sem("ln_x")
            ln_hi = sem("ln_hi")
            ln_lo = sem("ln_lo")
            xT_full = sem("xT_full")
            xT_done = sem("xT_done")
            proj_full = sem("proj_full")
            proj_hi = sem("proj_hi")
            proj_lo = sem("proj_lo")
            sim_full = sem("sim_full")
            gate_tanh = sem("gate_tanh")
            tab_made = sem("tab_made")
            tab_moved = sem("tab_moved")
            tab_picked = sem("tab_picked")
            logit_done = sem("logit_done")
            a_exp = sem("a_exp")
            p32_done = sem("p32_done")
            phi_done = sem("phi_done")
            plo_done = sem("plo_done")
            pT_full = sem("pT_full")
            pT_done = sem("pT_done")
            o_full = sem("o_full")
            o_hi = sem("o_hi")
            o_lo = sem("o_lo")
            y_full = sem("y_full")
            y_done = sem("y_done")
            blocks_picked = sem("blocks_picked")
            a_step = sem("a_step")
            block = p2.enter_context(nc.Block())
            BLOCKED = [b for b in BITS if b >= 16]
            COPIED = [b for b in BITS if b < 16]

            def banks(X, b0, n):
                return bank[:, 4 * X + b0:4 * X + b0 + n, :].rearrange("p b n -> p (b n)")

            def banks16(X, b0, n):
                return bank16[:, 4 * X + b0:4 * X + b0 + n, :].rearrange("p b n -> p (b n)")

            flat3 = lambda t: t.rearrange("p h v -> p (h v)")
            flat_c = lambda t: t.rearrange("p c n -> p (c n)")

            @block.sync
            def _(sp):
                sp.dma_start(wq32[:], aWq.rearrange("(c p) n -> p c n", p=P)).then_inc(w_in[0], 16)
                sp.dma_start(wkv32[:], aWkv.rearrange("(c p) n -> p c n", p=P)).then_inc(w_in[1], 16)
                sp.dma_start(pos32[0:DH, :], pos_emb).then_inc(w_in[2], 16)
                sp.dma_start(pos32[DH:P, :], pos_emb).then_inc(w_in[2], 16)
                sp.dma_start(wo32[:], aWout.rearrange("(c p) n -> p c n", p=P)).then_inc(w_in[3], 16)
                sp.dma_start(bo[:], ab_out.rearrange("(a n) -> a n", a=1).broadcast_to([P, D])).then_inc(w_in[3], 16)

            WEIGHTS = ((wq16, wq32, w_in[0], 16), (wkv16, wkv32, w_in[1], 16),
                       (pos16, pos32, w_in[2], 32), (wo16, wo32, w_in[3], 32))

            @block.gpsimd
            def _(pool):
                pool.iota(viota[:], pattern=[[0, H], [1, V1]], base=0, channel_multiplier=0).then_inc(a_const, 1)
                pool.memset(reset[:], 1.0).then_inc(a_const, 1)
                pool.memset(ones[:], 1.0).then_inc(a_const, 1)
                pool.wait_ge(ln_mv, PAIRS)
                pool.tensor_scalar(a_r[:], a_mv[:, :, 1], 1.0, 1e-5, ALU.mult, ALU.add).then_inc(ln_pool, 1)
                pool.wait_ge(ln_pool, 1)
                pool.tensor_tensor(a_r[:], a_r[:], half[:, 0:PAIRS], ALU.pow).then_inc(ln_r, 1)
                pool.wait_ge(a_const, 3)
                pool.memset(reset[:, :, 0:1], 0.0).then_inc(a_const, 1)
                pool.tensor_scalar(vpos[:], viota[:], 1.0, MAGIC, ALU.mult, ALU.add).then_inc(a_const, 1)
                pool.memset(gs[:, :, 0:1], 0.0).then_inc(a_const, 1)
                for X in range(2):
                    pool.memset(p16[:, X].rearrange("p a h b n -> p (a h b n)"), 0.0).then_inc(a_zero, 1)
                pool.wait_ge(a_zero, 2)
                for q in range(PAIRS):
                    X = q % 2
                    pool.wait_ge(phi_done, q + 1)
                    for b in range(2):
                        r = slice(b * N, (b + 1) * N)
                        pool.tensor_tensor(p16[r, X, 1, :, b, :], lg[r, X], p16[r, X, 0, :, b, :],
                                           ALU.subtract).then_inc(plo_done, 1)
                        pool.wait_ge(plo_done, q * 2 + b + 1)

            @block.scalar
            def _(act):
                def weights(i):
                    w16, w32, s, n = WEIGHTS[i]
                    act.wait_ge(s, n)
                    act.activation(w16[:, 0], w32[:], ACT.Copy, scale=WS).then_inc(a_whi, 1)

                def high_x(q):
                    act.wait_ge(ln_x, q + 1)
                    act.activation(a_x16[:, 0], a_x[:], ACT.Copy).then_inc(ln_hi, 1)

                def high_proj(q, i):
                    X = q % 2
                    dst, b0 = ((q16, 2), (k16, 0), (v16, 2))[i]
                    act.wait_ge(proj_full, q * 3 + i + 1)
                    hi = flat_c(dst[:, X, 0]) if i < 2 else dst[:, X, 0]
                    act.activation(hi, banks(X, b0, 2), ACT.Copy, scale=1.0 / WS).then_inc(proj_hi, 1)

                def tables(q):
                    X = q % 2
                    act.wait_ge(sim_full, q + 1)
                    if q:
                        act.wait_ge(tab_picked, 2 * (q * len(COPIED) - 1))
                    act.activation(gs[:, :, 1:V1], banks(X, 0, 2).rearrange("p (h n) -> p h n", n=N),
                                   ACT.Tanh, scale=0.5 * DH ** -0.5).then_inc(gate_tanh, 1)
                    e = banks(X, 2, 2).rearrange("p (h n) -> p h n", n=N)
                    act.activation(tab[:, X, 0, :, 0:N], e, ACT.Copy, scale=1.0 / WS)
                    act.activation(tab[:, X, 1, :, 0:N - 1], e[:, :, 1:N], ACT.Copy, scale=1.0 / WS)
                    act.activation(tab[:, X, 0, :, N:V1], e[:, :, N - 1:N], ACT.Copy, scale=1.0 / WS)
                    act.activation(tab[:, X, 1, :, N - 1:V1], e[:, :, N - 1:N].broadcast_to([P, H, 2]),
                                   ACT.Copy, scale=1.0 / WS).then_inc(tab_made, 1)

                def move(q, i):
                    cur = (q + i) % 2
                    for t in range(2):
                        if i == 0:
                            act.wait_ge(blocks_picked, 2 * q + t + 1)
                        else:
                            act.wait_ge(tab_picked, 2 * (q * len(COPIED) + i - 1) + t + 1)
                        act.activation(tab[:, 1 - cur, t], tab[:, cur, t], ACT.Copy).then_inc(tab_moved, 1)

                def transposed(q):
                    act.wait_ge(pT_full, q + 1)
                    act.activation(pT16[:].rearrange("p a h n -> p (a h n)"), banks16(q % 2, 0, 4),
                                   ACT.Copy).then_inc(pT_done, 1)

                def high_o(q):
                    act.wait_ge(o_full, q + 1)
                    act.activation(flat_c(o16[:, 0]), banks(q % 2, 0, 2), ACT.Copy, scale=1.0 / AS).then_inc(o_hi, 1)

                def soft(q):
                    X = q % 2
                    act.wait_ge(logit_done, q + 1)
                    act.activation(lg[:, X], lg[:, X], ACT.Exp).then_inc(a_exp, 1)

                def high_p(q):
                    X = q % 2
                    act.wait_ge(p32_done, q + 1)
                    for b in range(2):
                        r = slice(b * N, (b + 1) * N)
                        ins = act.activation(p16[r, X, 0, :, b, :], lg[r, X], ACT.Copy)
                    ins.then_inc(phi_done, 1)

                act.wait_ge(a_zero, 2)
                weights(0)
                high_x(0)
                weights(1)
                high_proj(0, 0)
                high_proj(0, 1)
                high_proj(0, 2)
                weights(2)
                high_x(1)
                tables(0)
                weights(3)
                for i in range(3):
                    high_proj(1, i)
                for q in range(PAIRS):
                    if q:
                        transposed(q - 1)
                        high_o(q - 1)
                    move(q, 0)
                    move(q, 1)
                    nxt = q + 1 if 0 < q < PAIRS - 1 else None
                    if nxt:
                        high_x(nxt)
                    move(q, 2)
                    if nxt:
                        high_proj(nxt, 0)
                    move(q, 3)
                    if nxt:
                        high_proj(nxt, 1)
                    soft(q)
                    if nxt:
                        high_proj(nxt, 2)
                    high_p(q)
                    if q + 1 < PAIRS:
                        tables(q + 1)
                transposed(PAIRS - 1)
                high_o(PAIRS - 1)

            @block.tensor
            def _(pe):
                def split(out_, stat, mov, cs):
                    todo = [(c, a, b) for c in cs for a, b in PASSES]
                    for i, (c, a, b) in enumerate(todo):
                        ins = pe.matmul(out_, stat(a, c), mov(b, c), start=(i == 0), stop=(i == len(todo) - 1))
                    return ins

                def proj(q):
                    X = q % 2
                    pe.wait_ge(ln_lo, q + 1)
                    if q > 1:
                        pe.wait_ge(y_done, q - 1)
                    for i, perm in enumerate((ident16, flip16)):
                        for part in range(2):
                            for c in range(C):
                                o = (part * C + c) * P
                                last = pe.matmul(banks(X, i, 1)[:, o:o + P], a_x16[:, part, c * P:(c + 1) * P],
                                                 perm[:], start=True, stop=True)
                        last.then_inc(xT_full, 1)
                    pe.wait_ge(xT_done, q + 1)
                    for i, (b0, w16) in enumerate(((2, wq16), (0, wkv16))):
                        pe.wait_ge(a_wlo, i + 1)
                        for t in range(KC):
                            last = split(banks(X, b0, 2)[:, t * P:(t + 1) * P],
                                         lambda a, c: w16[:, a, c, t * P:(t + 1) * P],
                                         lambda b, c: xT16[:, i, b, c, :], range(C))
                        last.then_inc(proj_full, 1)
                    pe.wait_ge(proj_lo, q * 3 + 1)
                    for t in range(2):
                        last = split(banks(X, 2 + t, 1), lambda a, c: xT16[:, 1, a, c, :],
                                     lambda b, c: wkv16[:, b, c, H * DH + t * 512:H * DH + (t + 1) * 512], range(C))
                    last.then_inc(proj_full, 1)

                def scores(q):
                    X = q % 2
                    pe.wait_ge(proj_lo, q * 3 + 3)
                    pe.wait_ge(a_wlo, 3)
                    for t in range(KC):
                        for r in range(2):
                            rows = slice(r * DH, (r + 1) * DH)
                            split(banks(X, 2 + r, 1)[:, t * N:(t + 1) * N], lambda a, c: q16[rows, X, a, t, :],
                                  lambda a, c: pos16[rows, a, :], range(1))
                    for t in range(KC):
                        for r in range(2):
                            rows = slice(r * DH, (r + 1) * DH)
                            for b in range(2):
                                cols = slice(b * N, (b + 1) * N)
                                last = split(banks(X, r, 1)[cols, t * N:(t + 1) * N],
                                             lambda a, c: q16[rows, X, a, t, cols],
                                             lambda a, c: k16[rows, X, a, t, cols], range(1))
                    last.then_inc(sim_full, 1)

                def av(q):
                    X = q % 2
                    pe.wait_ge(phi_done, q + 1)
                    pe.wait_ge(plo_done, 2 * q + 2)
                    for part in range(2):
                        for h in range(H):
                            last = pe.transpose(banks16(X, 0, 4)[:, (part * H + h) * P:(part * H + h + 1) * P],
                                                p16[:, X, part, h].rearrange("p b n -> p (b n)"), ident16[:])
                    last.then_inc(pT_full, 1)
                    pe.wait_ge(pT_done, q + 1)
                    for h in range(H):
                        r, t = h // KC, h % KC
                        head = 2 * t + r
                        last = split(banks(X, 0, 2)[r * DH:(r + 1) * DH, t * P:(t + 1) * P],
                                     lambda a, c: v16[:, X, a, head * DH:(head + 1) * DH],
                                     lambda b, c: pT16[:, b, h, :], range(1))
                    last.then_inc(o_full, 1)
                    pe.wait_ge(a_wlo, 4)
                    pe.wait_ge(o_lo, q + 1)
                    last = split(banks(X, 2, 1)[:, 0:D], lambda a, c: o16[:, a, c, :],
                                 lambda b, c: wo16[:, b, c, :], range(KC))
                    last.then_inc(y_full, 1)

                proj(0)
                scores(0)
                proj(1)
                scores(1)
                for q in range(PAIRS):
                    av(q)
                    if q + 2 < PAIRS:
                        proj(q + 2)
                        scores(q + 2)

            @block.vector
            def _(dve):
                steps = [0]

                def link(ins):
                    ins.then_inc(a_step, 1)
                    steps[0] += 1
                    dve.wait_ge(a_step, steps[0])

                def weights(i):
                    w16, w32, _, _ = WEIGHTS[i]
                    hi, lo, w = w16[:, 0], w16[:, 1], w32[:]
                    if i != 2:
                        hi, lo, w = flat_c(hi), flat_c(lo), flat_c(w)
                    dve.wait_ge(a_whi, i + 1)
                    dve.scalar_tensor_tensor(lo, w, WS, hi, ALU.mult, ALU.subtract).then_inc(a_wlo, 1)

                def norm_x(q):
                    dve.tensor_scalar(a_x[:], x_sb[:, q], a_mv[:, q, 0:1], a_r[:, q:q + 1],
                                      ALU.subtract, ALU.mult).then_inc(ln_x, 1)
                    dve.wait_ge(ln_x, q + 1)
                    dve.wait_ge(ln_hi, q + 1)
                    dve.tensor_tensor(a_x16[:, 1], a_x[:], a_x16[:, 0], ALU.subtract).then_inc(ln_lo, 1)

                def take_xT(q):
                    for i in range(2):
                        dve.wait_ge(xT_full, q * 2 + i + 1)
                        ins = dve.tensor_copy(xT16[:, i].rearrange("p a c n -> p (a c n)"), banks(q % 2, i, 1))
                    ins.then_inc(xT_done, 1)

                def low_proj(q, i):
                    X = q % 2
                    dst, b0 = ((q16, 2), (k16, 0), (v16, 2))[i]
                    dve.wait_ge(proj_hi, q * 3 + i + 1)
                    hi, lo = dst[:, X, 0], dst[:, X, 1]
                    if i < 2:
                        hi, lo = flat_c(hi), flat_c(lo)
                    dve.scalar_tensor_tensor(lo, banks(X, b0, 2), 1.0 / WS, hi, ALU.mult,
                                             ALU.subtract).then_inc(proj_lo, 1)

                def look_back(q):
                    dve.wait_ge(gate_tanh, q + 1)
                    link(dve.tensor_scalar(gs[:, :, 1:V1], gs[:, :, 1:V1], 0.5, 0.5, ALU.mult, ALU.add))
                    link(dve.tensor_tensor_scan(flat3(ar[:]), flat3(reset[:]), flat3(gs[:]), 0.0, ALU.mult, ALU.add))
                    link(dve.tensor_scalar(ar[:], ar[:], float(N - 1), -0.5, ALU.min, ALU.add))
                    link(dve.tensor_scalar(fl[:], ar[:], MAGIC, None, ALU.add))
                    link(dve.tensor_tensor_scan(flat3(fl[:]), flat3(ones[:]), flat3(fl[:]), MAGIC, ALU.add, ALU.min))
                    link(dve.scalar_tensor_tensor(flat3(s16[:]), flat3(fl[:]), -1.0, flat3(vpos[:]), ALU.mult, ALU.add))
                    for i, bit in enumerate(BITS):
                        dve.tensor_scalar(mask[:, i], s16[:], bit, None, ALU.bitwise_and)
                    link(dve.scalar_tensor_tensor(flat3(ar[:]), flat3(fl[:]), -MAGIC, flat3(ar[:]), ALU.add,
                                                  ALU.subtract))
                    link(dve.tensor_scalar(ar[:], ar[:], -0.5, None, ALU.add))


                def pick_blocks(q):
                    X = q % 2
                    dve.wait_ge(tab_made, q + 1)
                    for i, bit in enumerate(BLOCKED):
                        for v in list(range(V1 - bit, bit, -bit)) + [bit]:
                            w = bit if v > bit else 1
                            for t in range(2):
                                ins = dve.copy_predicated(tab[:, X, t, :, v:v + w], mask[:, i, :, v:v + w],
                                                          tab[:, X, t, :, v - bit:v - bit + w])
                                if (bit, v) == (BLOCKED[-1], bit):
                                    ins.then_inc(blocks_picked, 1)
                                elif t == 1:
                                    link(ins)

                def pick_copy(q, i):
                    cur, bit = (q + i) % 2, COPIED[i]
                    for t in range(2):
                        n = 2 * (q * len(COPIED) + i) + t + 1
                        dve.wait_ge(tab_moved, n)
                        dve.copy_predicated(tab[:, 1 - cur, t, :, bit:V1], mask[:, len(BLOCKED) + i, :, bit:V1],
                                            tab[:, cur, t, :, 0:V1 - bit]).then_inc(tab_picked, 1)

                def logits(q):
                    X = q % 2
                    value, nxt = tab[:, X, 0, :, 1:V1], tab[:, X, 1, :, 1:V1]
                    L = lg[:, X]
                    sim = banks(X, 0, 2).rearrange("p (h n) -> p h n", n=N)
                    dve.wait_ge(tab_picked, 2 * (q + 1) * len(COPIED))
                    link(dve.tensor_tensor(nxt, nxt, value, ALU.subtract))
                    link(dve.tensor_tensor(nxt, ar[:, :, 1:V1], nxt, ALU.mult))
                    link(dve.tensor_tensor(value, value, nxt, ALU.subtract))
                    if q > 1:
                        dve.wait_ge(plo_done, 2 * (q - 1))
                    link(dve.scalar_tensor_tensor(L, sim, DH ** -0.5, value, ALU.mult, ALU.add))
                    link(dve.reduce_max(hs_[:, 0], L, AX_X))
                    dve.tensor_tensor(L, L, hs_[:, 0].unsqueeze(2).broadcast_to([P, H, N]),
                                      ALU.subtract).then_inc(logit_done, 1)

                def weigh(q):
                    X = q % 2
                    L = lg[:, X]
                    dve.wait_ge(a_exp, q + 1)
                    link(dve.reduce_sum(hs_[:, 1], L, AX_X))
                    link(dve.reciprocal(hs_[:, 1], hs_[:, 1]))
                    dve.scalar_tensor_tensor(L, L, AS, hs_[:, 1].unsqueeze(2).broadcast_to([P, H, N]),
                                             ALU.mult, ALU.mult).then_inc(p32_done, 1)

                def low_o(q):
                    dve.wait_ge(o_hi, q + 1)
                    dve.scalar_tensor_tensor(flat_c(o16[:, 1]), banks(q % 2, 0, 2), 1.0 / AS, flat_c(o16[:, 0]),
                                             ALU.mult, ALU.subtract).then_inc(o_lo, 1)

                def residual(q):
                    dve.wait_ge(y_full, q + 1)
                    link(dve.scalar_tensor_tensor(tmp[:], banks(q % 2, 2, 1)[:, 0:D], 1.0 / WS, bo[:],
                                                  ALU.mult, ALU.add))
                    dve.tensor_tensor(x_sb[:, q], x_sb[:, q], tmp[:], ALU.add).then_inc(y_done, 1)

                for q in range(PAIRS):
                    dve.bn_stats(a_stats[:, q], x_sb[:, q]).then_inc(ln_st, 1)
                dve.wait_ge(ln_st, PAIRS)
                for q in range(PAIRS):
                    dve.bn_aggr(a_mv[:, q], a_stats[:, q]).then_inc(ln_mv, 1)
                dve.wait_ge(ln_mv, PAIRS)
                dve.wait_ge(ln_r, 1)
                weights(0)
                norm_x(0)
                take_xT(0)
                weights(1)
                for i in range(3):
                    low_proj(0, i)
                weights(2)
                norm_x(1)
                take_xT(1)
                dve.wait_ge(a_const, 6)
                for q in range(PAIRS):
                    nxt = q + 1 if 0 < q < PAIRS - 1 else None
                    if q == 0:
                        weights(3)
                        for i in range(3):
                            low_proj(1, i)
                    look_back(q)
                    pick_blocks(q)
                    if q:
                        low_o(q - 1)
                    pick_copy(q, 0)
                    if q:
                        residual(q - 1)
                    pick_copy(q, 1)
                    if nxt:
                        norm_x(nxt)
                    pick_copy(q, 2)
                    if nxt:
                        take_xT(nxt)
                        low_proj(nxt, 0)
                    pick_copy(q, 3)
                    if nxt:
                        low_proj(nxt, 1)
                    logits(q)
                    if nxt:
                        low_proj(nxt, 2)
                    weigh(q)
                low_o(PAIRS - 1)
                residual(PAIRS - 1)

        HSC = 16.0
        with ExitStack() as p3:
            f_stats = sb("f_stats", [P, PAIRS, 6], F32, p3)
            f_mv = sb("f_mv", [P, PAIRS, 2], F32, p3)
            f_r = sb("f_r", [P, PAIRS], F32, p3)
            f_x = sb("f_x", [P, PAIRS, D], F32, p3)
            f_x16 = sb("f_x16", [P, 2, PAIRS, D], F16, p3)
            f_xT = sb("f_xT", [P, 2, C, TOK], F16, p3)
            gw32 = sb("gw32", [P, C, E], F32, p3)
            gw16 = sb("gw16", [P, 2, C, E], F16, p3)
            lg8 = sb("lg8", [P, PAIRS, E], F32, p3)
            rank_i = sb("rank_i", [P, PAIRS, E], I32, p3)
            rank = sb("rank", [P, PAIRS, E], F32, p3)
            pick = sb("pick", [P, 2, PAIRS, E], F32, p3)
            eq = sb("eq", [P, PAIRS, E], F32, p3)
            top = sb("top", [P, 4, PAIRS], F32, p3)
            share = sb("share", [P, PAIRS, E], F32, p3)
            gu32 = sb("gu32", [P, 2, C, 2 * F], F32, p3)
            dn32 = sb("dn32", [P, 2, FC, D], F32, p3)
            gu16 = sb("gu16", [P, 2, 2, C, 2 * F], F16, p3)
            dn16 = sb("dn16", [P, 2, 2, FC, D], F16, p3)
            th = sb("th", [P, 2, TOK], F32, p3)
            hid = sb("hid", [P, 2, TOK], F32, p3)
            hid16 = sb("hid16", [P, 2, 2, TOK], F16, p3)

            f_load = sem("f_load")
            f_const = sem("f_const")
            f_mvd = sem("f_mvd")
            f_pool = sem("f_pool")
            f_rr = sem("f_rr")
            f_xr = sem("f_xr")
            f_hi = sem("f_hi")
            f_lo = sem("f_lo")
            f_T = sem("f_T")
            f_Td = sem("f_Td")
            gw_hi = sem("gw_hi")
            gw_lo = sem("gw_lo")
            lg_full = sem("lg_full")
            e2_in = sem("e2_in")
            e2_out = sem("e2_out")
            w_loaded = [sem(f"w_loaded{i}") for i in range(2)]
            w_hi = sem("w_hi")
            w_lo = sem("w_lo")
            gu_full = sem("gu_full")
            th_done = sem("th_done")
            sg_done = sem("sg_done")
            hid_done = sem("hid_done")
            hid_hi = sem("hid_hi")
            hid_lo = sem("hid_lo")
            ffn_done = sem("ffn_done")
            y3_done = sem("y3_done")
            f_step = sem("f_step")
            gu_dram = gate_up_w.rearrange("e (c p) n -> e p c n", p=P)
            dn_dram = down_w.rearrange("e (c p) n -> e p c n", p=P)
            block = p3.enter_context(nc.Block())

            @block.sync
            def _(sp):
                sp.dma_start(gw32[:], gate_w.rearrange("(c p) n -> p c n", p=P)).then_inc(f_load, 16)
                with sp.Fori(0, E // 2) as i:
                    for s in range(2):
                        sp.wait_ge(w_lo, 4 * i + ONE)
                        sp.dma_start(gu32[:, s], gu_dram[i * 2 + s]).then_inc(w_loaded[s], 16)
                        sp.dma_start(dn32[:, s], dn_dram[i * 2 + s]).then_inc(w_loaded[s], 16)

            @block.gpsimd
            def _(pool):
                pool.iota(rank_i[:], pattern=[[0, PAIRS], [-1, E]], base=E, channel_multiplier=0).then_inc(f_const, 1)
                pool.wait_ge(f_const, 1)
                pool.tensor_copy(rank[:], rank_i[:]).then_inc(f_const, 1)
                pool.wait_ge(f_mvd, PAIRS)
                pool.tensor_scalar(f_r[:], f_mv[:, :, 1], 1.0, 1e-5, ALU.mult, ALU.add).then_inc(f_pool, 1)
                pool.wait_ge(f_pool, 1)
                pool.tensor_tensor(f_r[:], f_r[:], half[:, 0:PAIRS], ALU.pow).then_inc(f_rr, 1)

            @block.scalar
            def _(act):
                act.wait_ge(f_load, 16)
                act.activation(gw16[:, 0], gw32[:], ACT.Copy, scale=WS).then_inc(gw_hi, 1)
                act.wait_ge(f_xr, PAIRS)
                act.activation(f_x16[:, 0], f_x[:], ACT.Copy).then_inc(f_hi, 1)
                act.wait_ge(e2_in, 1)
                act.activation(top[:, 3], top[:, 2], ACT.Exp).then_inc(e2_out, 1)

                def split_weights(n, s, staged):
                    act.wait_ge(w_loaded[s], staged)
                    act.wait_ge(ffn_done, n)
                    for w32, w16 in ((gu32, gu16), (dn32, dn16)):
                        act.activation(w16[:, s, 0], w32[:, s], ACT.Copy, scale=WS).then_inc(w_hi, 1)

                def two_experts(i, more):
                    for k in range(2 * FC):
                        m = i * 2 * FC + k + 1
                        act.wait_ge(gu_full, m)
                        act.activation(th[:, k % 2], bank[:, 2 * (k % 2), :], ACT.Tanh,
                                       scale=0.5 / WS).then_inc(th_done, 1)
                        act.wait_ge(hid_done, m + 2)
                        act.activation(hid16[:, k % 2, 0], hid[:, k % 2], ACT.Copy).then_inc(hid_hi, 1)
                        if k == 1:
                            split_weights(i * 2 + 2, 1, i * 32 + 32)
                        if k == FC + 1 and more:
                            split_weights(i * 2 + 3, 0, i * 32 + 64)

                split_weights(1, 0, 32)
                with act.Fori(0, E // 2 - 1) as i:
                    two_experts(i, True)
                two_experts(E // 2 - 1, False)

            @block.tensor
            def _(pe):
                def split(out_, stat, mov, cs, first=True, last_=True):
                    todo = [(c, a, b) for c in cs for a, b in PASSES]
                    for i, (c, a, b) in enumerate(todo):
                        ins = pe.matmul(out_, stat(a, c), mov(b, c), start=(first and i == 0),
                                        stop=(last_ and i == len(todo) - 1))
                    return ins

                pe.wait_ge(f_lo, 1)
                for q in range(PAIRS):
                    for part in range(2):
                        for c in range(C):
                            o = (part * C + c) * P
                            last = pe.transpose(bank16[:, q, o:o + P], f_x16[:, part, q, c * P:(c + 1) * P],
                                                ident16[:])
                    last.then_inc(f_T, 1)
                pe.wait_ge(f_Td, PAIRS)
                pe.wait_ge(gw_lo, 1)
                for q in range(PAIRS):
                    last = split(bank[:, 4, q * E:(q + 1) * E], lambda a, c: f_xT[:, a, c, q * P:(q + 1) * P],
                                 lambda b, c: gw16[:, b, c, :], range(C))
                last.then_inc(lg_full, 1)
                pe.matmul(bank[:, 5, 0:E], f_xT[:, 0, 0, 0:P], gw16[:, 0, 0, :], start=True,
                          stop=True).then_inc(ffn_done, 2)
                with pe.Fori(0, E // 2) as i:
                    def up(k):
                        s, j = k // FC, k % FC
                        if j == 0:
                            pe.wait_ge(w_lo, 4 * i + 2 * s + 2 + ONE)
                        pe.wait_ge(hid_done, i * 2 * FC + k + 1)
                        for u in range(2):
                            last = split(bank[:, 2 * (k % 2) + u, :],
                                         lambda a, c: gu16[:, s, a, c, u * F + j * P:u * F + (j + 1) * P],
                                         lambda b, c: f_xT[:, b, c, :], range(C))
                        last.then_inc(gu_full, 1)

                    def down(k):
                        s, j = k // FC, k % FC
                        if j == 0:
                            pe.wait_ge(y3_done, i * 2 + s + ONE)
                        pe.wait_ge(hid_lo, i * 2 * FC + k + 1)
                        for t in range(PAIRS):
                            last = split(bank[:, 4 + t, 0:D], lambda a, c: hid16[:, k % 2, a, t * P:(t + 1) * P],
                                         lambda b, c: dn16[:, s, b, j, :], range(1), j == 0, j == FC - 1)
                        if j == FC - 1:
                            last.then_inc(ffn_done, 1)

                    for k in range(2 * FC):
                        up(k)
                        if k:
                            down(k - 1)
                    down(2 * FC - 1)

            @block.vector
            def _(dve):
                credit(dve, w_lo, y3_done)
                steps = [0]

                def link(ins):
                    steps[0] += 1
                    ins.then_inc(f_step, 1)
                    dve.wait_ge(f_step, steps[0])

                for q in range(PAIRS):
                    last = dve.bn_stats(f_stats[:, q], x_sb[:, q])
                link(last)
                for q in range(PAIRS):
                    dve.bn_aggr(f_mv[:, q], f_stats[:, q]).then_inc(f_mvd, 1)
                dve.wait_ge(f_mvd, PAIRS)
                dve.wait_ge(f_rr, 1)
                for q in range(PAIRS):
                    dve.tensor_scalar(f_x[:, q], x_sb[:, q], f_mv[:, q, 0:1], f_r[:, q:q + 1],
                                      ALU.subtract, ALU.mult).then_inc(f_xr, 1)
                dve.wait_ge(f_xr, PAIRS)
                dve.wait_ge(f_hi, 1)
                dve.tensor_tensor(f_x16[:, 1], f_x[:], f_x16[:, 0], ALU.subtract).then_inc(f_lo, 1)
                dve.wait_ge(gw_hi, 1)
                dve.scalar_tensor_tensor(gw16[:, 1], gw32[:], WS, gw16[:, 0], ALU.mult, ALU.subtract).then_inc(gw_lo, 1)
                for q in range(PAIRS):
                    dve.wait_ge(f_T, q + 1)
                    dve.tensor_copy(f_xT[:, :, :, q * P:(q + 1) * P],
                                    bank16[:, q, 0:4 * P].rearrange("p (a c n) -> p a c n", a=2, c=C)).then_inc(f_Td, 1)
                dve.wait_ge(lg_full, 1)
                dve.wait_ge(f_const, 2)
                link(dve.tensor_scalar(lg8[:].rearrange("p q e -> p (q e)"), bank[:, 4, 0:PAIRS * E], 1.0 / WS,
                                       None, ALU.mult))
                bc = lambda t: t.unsqueeze(2).broadcast_to([P, PAIRS, E])
                for r in range(2):
                    link(dve.reduce_max(top[:, r], lg8[:], AX_X))
                    link(dve.tensor_tensor(eq[:], lg8[:], bc(top[:, r]), ALU.is_equal))
                    link(dve.tensor_tensor(eq[:], eq[:], rank[:], ALU.mult))
                    link(dve.reduce_max(top[:, 2], eq[:], AX_X))
                    link(dve.tensor_tensor(pick[:, r], rank[:], bc(top[:, 2]), ALU.is_equal))
                    link(dve.scalar_tensor_tensor(lg8[:], pick[:, r], -3e38, lg8[:], ALU.mult, ALU.add))
                dve.tensor_tensor(top[:, 2], top[:, 1], top[:, 0], ALU.subtract).then_inc(e2_in, 1)
                dve.wait_ge(e2_out, 1)
                link(dve.tensor_scalar(top[:, 2], top[:, 3], 1.0, None, ALU.add))
                link(dve.reciprocal(top[:, 2], top[:, 2]))
                link(dve.tensor_tensor(share[:], pick[:, 1], bc(top[:, 3]), ALU.mult))
                link(dve.tensor_tensor(share[:], share[:], pick[:, 0], ALU.add))
                link(dve.scalar_tensor_tensor(share[:], share[:], 1.0 / (WS * HSC), bc(top[:, 2]),
                                              ALU.mult, ALU.mult))
                dve.memset(eq[:], 0.0).then_inc(hid_done, 2)

                def split_weights(n, s):
                    pat = "p c n -> p (c n)"
                    for k, (w32, w16) in enumerate(((gu32, gu16), (dn32, dn16))):
                        dve.wait_ge(w_hi, 2 * (n - 1) + k + 1)
                        dve.scalar_tensor_tensor(w16[:, s, 1].rearrange(pat), w32[:, s].rearrange(pat), WS,
                                                 w16[:, s, 0].rearrange(pat), ALU.mult, ALU.subtract).then_inc(w_lo, 1)

                def two_experts(i, more):
                    for k in range(2 * FC):
                        m = i * 2 * FC + k + 1
                        s, j = k // FC, k % FC
                        dve.wait_ge(th_done, m)
                        dve.scalar_tensor_tensor(hid[:, k % 2], th[:, k % 2], 1.0, bank[:, 2 * (k % 2), :],
                                                 ALU.add, ALU.mult).then_inc(sg_done, 1)
                        dve.wait_ge(sg_done, m)
                        dve.scalar_tensor_tensor(hid[:, k % 2], hid[:, k % 2], HSC / (2 * WS * WS),
                                                 bank[:, 2 * (k % 2) + 1, :], ALU.mult, ALU.mult).then_inc(hid_done, 1)
                        dve.wait_ge(hid_done, m + 2)
                        dve.wait_ge(hid_hi, m)
                        dve.tensor_tensor(hid16[:, k % 2, 1], hid[:, k % 2], hid16[:, k % 2, 0],
                                          ALU.subtract).then_inc(hid_lo, 1)
                        if k == 1:
                            split_weights(i * 2 + 2, 1)
                        if k == FC + 1 and more:
                            split_weights(i * 2 + 3, 0)
                        if j == FC - 1:
                            n = i * 2 + s + 1
                            dve.wait_ge(ffn_done, n + 2)
                            dve.wait_ge(y3_done, n - 1 + ONE)
                            for t in range(PAIRS):
                                last = dve.scalar_tensor_tensor(x_sb[:, t], bank[:, 4 + t, 0:D],
                                                                share[:, t, bass.ds(i * 2 + s, 1)], x_sb[:, t],
                                                                ALU.mult, ALU.add)
                            last.then_inc(y3_done, 1)

                split_weights(1, 0)
                with dve.Fori(0, E // 2 - 1) as i:
                    two_experts(i, True)
                two_experts(E // 2 - 1, False)

        stored = sem("stored")
        with ExitStack() as p4:
            block = p4.enter_context(nc.Block())

            @block.sync
            def _(sp):
                sp.dma_start(out.rearrange("b k d -> (b k) d").rearrange("(q p) d -> p q d", p=P),
                             x_sb[:]).then_inc(stored, 16)
                sp.wait_ge(stored, 16)


_INS = ['x', 'ctx_1024', 'L0_xattn_Wq', 'L0_xattn_Wk', 'L0_xattn_Wv', 'L0_xattn_gru_wih',
        'L0_xattn_gru_whh', 'L0_xattn_gru_bih', 'L0_xattn_gru_bhh', 'L0_xattn_slot_norm_w',
        'L0_xattn_input_norm_w', 'L0_attn_Wq', 'L0_attn_Wkv', 'L0_attn_Wout', 'L0_attn_b_out',
        'L0_attn_pos_emb', 'L0_ffn_gate_w', 'L0_ffn_gate_up_w', 'L0_ffn_down_w']


def kernel(**inputs):
    import numpy as _np
    import concourse.bacc as _bacc
    from concourse.bass_utils import run_bass_kernel_spmd as _run

    nc = _bacc.Bacc("TRN2", target_bir_lowering=False, num_devices=1)
    arrays, args = {}, []
    for name in _INS:
        a = _np.ascontiguousarray(inputs[name])
        arrays[f"in_{name}_dram"] = a
        args.append(nc.dram_tensor(f"in_{name}_dram", a.shape, mybir.dt.from_np(a.dtype), kind="ExternalInput").ap())
    shape = tuple(inputs['x'].shape)
    args.append(nc.dram_tensor("out_dram", shape, F32, kind="ExternalOutput").ap())
    perceiver_kernel(nc, *args)
    r = _run(nc, [arrays], core_ids=[0])
    return r.results[0]["out_dram"]
```

```python
from contextlib import ExitStack

import concourse.bass as bass
from concourse import mybir

ALU = mybir.AluOpType
ACT = mybir.ActivationFunctionType
AX_X = mybir.AxisListType.X
F32 = mybir.dt.float32
F16 = mybir.dt.float16
I32 = mybir.dt.int32
I16 = mybir.dt.int16

P = 128
WS = 64.0
AS = 1024.0
MAGIC = 12582912.0
PASSES = ((0, 0), (1, 0), (0, 1))


ONE = 1


def credit(eng, *sems):
    for s in sems:
        eng.sem_inc(s, ONE)


class Count:

    def __init__(self):
        self.n = 0

    def next(self, by=1):
        self.n += by
        return self.n


def perceiver_kernel(nc, x, ctx_1024, xWq, xWk, xWv, wih, whh, bih, bhh, slot_w, input_w,
                     aWq, aWkv, aWout, ab_out, pos_emb, gate_w, gate_up_w, down_w, out):
    B, N, D = x.shape
    M = ctx_1024.shape[1]
    C = D // P
    PAIRS = B * N // P
    MR = M // P
    MT = MR + 1
    TAIL = M - MR * P
    G = 3 * D
    XW = D + 2
    H = aWq.shape[1] // N
    DH = pos_emb.shape[0]
    V1 = N + 1
    E = gate_up_w.shape[0]
    F = down_w.shape[1]
    FC = F // P
    TOK = B * N

    with ExitStack() as ctx:
        def sb(name, shape, dt, on=ctx):
            return on.enter_context(nc.sbuf_tensor(name, shape, dt))

        def sem(name):
            return ctx.enter_context(nc.semaphore(name))

        bank = ctx.enter_context(nc.psum_tensor("bank", [P, 8, 512], F32))
        bank16 = bank[:].bitcast(F16)
        x_sb = sb("x_sb", [P, PAIRS, D], F32)
        ident = sb("ident", [P, P], F32)
        ident16 = sb("ident16", [P, P], F16)
        flip16 = sb("flip16", [P, P], F16)
        stats = sb("stats", [P, PAIRS, 6], F32)
        mv = sb("mv", [P, PAIRS, 2], F32)
        half = sb("half", [P, 16], F32)
        lnr = sb("lnr", [P, PAIRS], F32)
        eps_rms = sb("eps_rms", [P, 16], F32)

        X32 = sb("X32", [P, 2, MT, D], F32)
        phase1 = ctx.enter_context(ExitStack())
        s0 = sb("s0", [P, PAIRS, D], F32, phase1)
        A16 = sb("A16", [P, 2, C, D], F16, phase1)
        wihT16 = sb("wihT16", [P, 2, C, G], F16, phase1)
        whhT16 = sb("whhT16", [P, 2, C, G], F16, phase1)
        ones16 = sb("ones16", [P, P], F16, phase1)
        LO = 32
        bias16 = sb("bias16", [P, 4 * D], F16, phase1)
        junk = sb("junk", [P, MT, D], F16, phase1)
        ssq = sb("ssq", [P, 2, MT], F32, phase1)

        loaded = [sem(f"loaded{i}") for i in range(2)]
        tail_clear = sem("tail_clear")
        sq_done = sem("sq_done")
        eps_added = sem("eps_added")
        rinv_ready = sem("rinv_ready")
        split_done = sem("split_done")
        split_rest = sem("split_rest")
        rinv = sb("rinv", [P, 2, MT], F32, phase1)
        ctx_main = ctx_1024[:, 0:MR * P, :].rearrange("b (p t) d -> b p t d", t=MR)
        ctx_tail = ctx_1024[:, MR * P:M, :]

        def load_rows(sp, b):
            sp.dma_start(X32[:, b % 2, 0:MR, :], ctx_main[b]).then_inc(loaded[b % 2], 16)
            sp.dma_start(X32[0:TAIL, b % 2, MR, :], ctx_tail[b]).then_inc(loaded[b % 2], 16)

        PIECES = ((0, MT // 2 + 1), (MT // 2 + 1, MT))

        def square_rows(act, b, piece):
            n = 2 * b + piece
            act.wait_ge(loaded[b % 2], 32 * (b // 2 + 1))
            act.wait_ge(tail_clear, 2)
            if n > 1:
                act.wait_ge(sq_done, n - 1)
            if b > 1:
                act.wait_ge(eps_added, b - 1)
            for t in range(*PIECES[piece]):
                ins = act.activation(junk[:, t, :], X32[:, b % 2, t, :], ACT.Square, scale=float(D) ** -0.5,
                                     accum_out=ssq[:, b % 2, t:t + 1])
            ins.then_inc(sq_done, 1)

        def rinv_of(pool, b):
            pool.wait_ge(sq_done, 2 * b + 2)
            if b > 1:
                pool.wait_ge(split_done, b - 1)
                pool.wait_ge(split_rest, b - 1)
            pool.tensor_tensor(rinv[:, b % 2], ssq[:, b % 2], eps_rms[:, 0:MT],
                               ALU.add).then_inc(eps_added, 1)
            pool.wait_ge(eps_added, b + 1)
            pool.tensor_tensor(rinv[:, b % 2], rinv[:, b % 2], half[:, 0:MT],
                               ALU.pow).then_inc(rinv_ready, 1)

        in_x, in_g, in_w, in_b, in_n = (sem(n) for n in ("in_x", "in_g", "in_w", "in_b", "in_n"))
        made = sem("made")
        folded = sem("folded")
        bias_sum = sem("bias_sum")
        bias_hi = sem("bias_hi")
        stats_done = sem("stats_done")
        moments_done = sem("moments_done")
        var_raised = sem("var_raised")
        lnr_ready = sem("lnr_ready")
        iw_done = sem("iw_done")
        A_full = sem("A_full")
        A_sw = sem("A_sw")
        A_done = sem("A_done")
        A_hi = sem("A_hi")
        gT_full = sem("gT_full")
        gT_done = sem("gT_done")
        hh_hi = sem("hh_hi")
        hh_lo = sem("hh_lo")
        ih_full = sem("ih_full")
        ih_hi = sem("ih_hi")
        with ExitStack() as p0:
            w3 = sb("w3", [P, 3, C, D], F32, p0)
            wg = sb("wg", [P, 2, G // P, D], F32, p0)
            wgT = sb("wgT", [P, C, G], F32, p0)
            A32 = sb("A32", [P, C, D], F32, p0)
            swc = sb("swc", [P, C], F32, p0)
            iwc = sb("iwc", [P, C], F32, p0)
            iwcs = sb("iwcs", [P, C], F32, p0)
            iwb = sb("iwb", [P, D], F32, p0)
            bb = sb("bb", [P, 2, G], F32, p0)
            b32 = sb("b32", [P, 4 * D], F32, p0)
            bhi = sb("bhi", [P, 4 * D], F16, p0)
            block = p0.enter_context(nc.Block())
            HALVES = ((0, 3 * P), (3 * P, G))

            @block.sync
            def _(sp):
                sp.dma_start(wg[:, 0], wih.rearrange("(c p) n -> p c n", p=P)).then_inc(in_g, 16)
                sp.dma_start(w3[:, 2], xWv.rearrange("(c p) n -> p c n", p=P)).then_inc(in_g, 16)
                sp.dma_start(wg[:, 1], whh.rearrange("(c p) n -> p c n", p=P)).then_inc(in_g, 16)
                for i, w in enumerate((xWq, xWk)):
                    sp.dma_start(w3[:, i], w.rearrange("(c p) n -> p c n", p=P)).then_inc(in_w, 16)
                for b in range(2):
                    sp.wait_ge(tail_clear, 2)
                    load_rows(sp, b)

            @block.gpsimd
            def _(pool):
                for q in range(2):
                    pool.memset(X32[:, q, MR, :], 0.0).then_inc(tail_clear, 1)
                pool.memset(eps_rms[:], 1e-6)
                pool.memset(half[:], -0.5).then_inc(made, 1)
                pool.memset(ident[:], 0.0).then_inc(made, 1)
                pool.memset(flip16[:], 0.0).then_inc(made, 1)
                pool.memset(ones16[:], 1.0)
                pool.memset(bias16[:], 0.0).then_inc(made, 1)
                pool.wait_ge(made, 4)
                pool.affine_select(out=ident[:], in_=ident[:], compare_op=ALU.not_equal, fill=1.0,
                                   base=0, pattern=[[-1, P]], channel_multiplier=1).then_inc(made, 1)
                for b in range(2):
                    part = flip16[:, b * N:(b + 1) * N]
                    pool.affine_select(out=part, in_=part, compare_op=ALU.not_equal, fill=1.0,
                                       base=-(N - 1) - b * N, pattern=[[1, N]],
                                       channel_multiplier=1).then_inc(made, 1)
                pool.wait_ge(made, 5)
                pool.tensor_copy(ident16[:], ident[:]).then_inc(made, 1)
                pool.wait_ge(moments_done, PAIRS)
                pool.tensor_scalar(lnr[:], mv[:, :, 1], 1.0, 1e-5, ALU.mult, ALU.add).then_inc(var_raised, 1)
                pool.wait_ge(var_raised, 1)
                pool.tensor_tensor(lnr[:], lnr[:], half[:, 0:PAIRS], ALU.pow).then_inc(lnr_ready, 1)
                rinv_of(pool, 0)

            @block.tensor
            def _(pe):
                pe.wait_ge(made, 5)
                pe.wait_ge(in_g, 48)
                for i in range(2):
                    for c in range(C):
                        for k, (g0, g1) in enumerate(HALVES):
                            for g in range(g0, g1, P):
                                last = pe.transpose(bank[:, i * 4 + c * 2 + k, g - g0:g - g0 + P],
                                                    wg[:, i, g // P, c * P:(c + 1) * P], ident[:])
                            last.then_inc(gT_full, 1)
                pe.wait_ge(in_w, 32)
                pe.wait_ge(gT_done, 4)
                for d in range(C):
                    for o in range(C):
                        last = pe.matmul(bank[:, d, 0:D], w3[:, 0, o, d * P:(d + 1) * P], w3[:, 1, o, :],
                                         start=(o == 0), stop=(o == C - 1))
                last.then_inc(A_full, 1)
                pe.wait_ge(hh_lo, 4)
                for e in range(C):
                    for k, (g0, g1) in enumerate(HALVES):
                        for o in range(C):
                            last = pe.matmul(bank[:, 4 + 2 * e + k, 0:g1 - g0], w3[:, 2, o, e * P:(e + 1) * P],
                                             wgT[:, o, g0:g1], start=(o == 0), stop=(o == C - 1))
                        last.then_inc(ih_full, 1)

            @block.scalar
            def _(act):
                act.dma_start(x_sb[:], x.rearrange("b k d -> (b k) d").rearrange("(q p) d -> p q d", p=P)
                              ).then_inc(in_x, 16)
                for i, b in enumerate((bih, bhh)):
                    act.dma_start(bb[:, i], b.rearrange("(a n) -> a n", a=1).broadcast_to([P, G])).then_inc(in_b, 16)
                act.dma_start(iwb[:], input_w.rearrange("(a n) -> a n", a=1).broadcast_to([P, D])).then_inc(in_n, 16)
                act.dma_start(swc[:], slot_w.rearrange("(c p) -> p c", p=P),
                              allow_slow_non_contiguous=True).then_inc(in_n, 16)
                act.dma_start(iwc[:], input_w.rearrange("(c p) -> p c", p=P),
                              allow_slow_non_contiguous=True).then_inc(in_n, 16)
                act.wait_ge(bias_sum, 1)
                act.activation(bhi[:], b32[:], ACT.Copy, scale=WS).then_inc(bias_hi, 1)
                for c in range(C):
                    for k, (g0, g1) in enumerate(HALVES):
                        act.wait_ge(gT_full, 4 + c * 2 + k + 1)
                        act.activation(whhT16[:, 0, c, g0:g1], bank[:, 4 + c * 2 + k, 0:g1 - g0], ACT.Copy,
                                       scale=WS).then_inc(hh_hi, 1)
                act.wait_ge(A_done, 1)
                act.activation(A16[:, 0], A32[:], ACT.Copy).then_inc(A_hi, 1)
                for piece in range(2):
                    square_rows(act, 0, piece)
                act.wait_ge(iw_done, 1)
                for e in range(C):
                    for k, (g0, g1) in enumerate(HALVES):
                        act.wait_ge(ih_full, e * 2 + k + 1)
                        act.activation(wihT16[:, 0, e, g0:g1], bank[:, 4 + 2 * e + k, 0:g1 - g0], ACT.Copy,
                                       scale=iwcs[:, e:e + 1]).then_inc(ih_hi, 1)

            @block.vector
            def _(dve):
                dve.wait_ge(in_x, 16)
                for q in range(PAIRS):
                    dve.bn_stats(stats[:, q, :], x_sb[:, q, :]).then_inc(stats_done, 1)
                for q in range(PAIRS):
                    dve.wait_ge(stats_done, q + 1)
                    dve.bn_aggr(mv[:, q, :], stats[:, q, :]).then_inc(moments_done, 1)
                dve.wait_ge(in_b, 32)
                dve.tensor_tensor(b32[:, 0:2 * D], bb[:, 0, 0:2 * D], bb[:, 1, 0:2 * D], ALU.add)
                dve.tensor_copy(b32[:, 2 * D:3 * D], bb[:, 0, 2 * D:G])
                dve.tensor_copy(b32[:, 3 * D:4 * D], bb[:, 1, 2 * D:G]).then_inc(bias_sum, 1)
                dve.wait_ge(bias_hi, 1)
                dve.wait_ge(bias_sum, 1)
                dve.wait_ge(made, 4)
                dve.tensor_copy(bias16[0:1, :], bhi[0:1, :])
                dve.scalar_tensor_tensor(bias16[LO:LO + 1, :], b32[LO:LO + 1, :], WS, bhi[LO:LO + 1, :],
                                         ALU.mult, ALU.subtract).then_inc(folded, 1)
                dve.wait_ge(in_n, 48)
                dve.tensor_scalar(iwcs[:], iwc[:], WS, None, ALU.mult).then_inc(iw_done, 1)
                dve.wait_ge(moments_done, PAIRS)
                dve.wait_ge(lnr_ready, 1)
                for q in range(PAIRS):
                    dve.tensor_scalar(s0[:, q], x_sb[:, q], mv[:, q, 0:1], lnr[:, q:q + 1],
                                      ALU.subtract, ALU.mult).then_inc(folded, 1)
                for c in range(C):
                    for k, (g0, g1) in enumerate(HALVES):
                        dve.wait_ge(gT_full, c * 2 + k + 1)
                        dve.tensor_copy(wgT[:, c, g0:g1], bank[:, c * 2 + k, 0:g1 - g0]).then_inc(gT_done, 1)
                for c in range(C):
                    for k, (g0, g1) in enumerate(HALVES):
                        dve.wait_ge(hh_hi, c * 2 + k + 1)
                        dve.scalar_tensor_tensor(whhT16[:, 1, c, g0:g1], bank[:, 4 + c * 2 + k, 0:g1 - g0], WS,
                                                 whhT16[:, 0, c, g0:g1], ALU.mult, ALU.subtract).then_inc(hh_lo, 1)
                dve.wait_ge(A_full, 1)
                for d in range(C):
                    ins = dve.scalar_tensor_tensor(A32[:, d], bank[:, d, 0:D], swc[:, d:d + 1], iwb[:],
                                                   ALU.mult, ALU.mult)
                ins.then_inc(A_sw, 1)
                dve.wait_ge(A_sw, 1)
                dve.tensor_scalar(A32[:], A32[:], WS, None, ALU.mult).then_inc(A_done, 1)
                dve.wait_ge(A_done, 1)
                dve.wait_ge(A_hi, 1)
                dve.tensor_tensor(A16[:, 1], A32[:], A16[:, 0], ALU.subtract).then_inc(folded, 1)
                dve.wait_ge(iw_done, 1)
                for e in range(C):
                    for k, (g0, g1) in enumerate(HALVES):
                        dve.wait_ge(ih_hi, e * 2 + k + 1)
                        dve.scalar_tensor_tensor(wihT16[:, 1, e, g0:g1], bank[:, 4 + 2 * e + k, 0:g1 - g0],
                                                 iwcs[:, e:e + 1], wihT16[:, 0, e, g0:g1], ALU.mult,
                                                 ALU.subtract).then_inc(folded, 1)

        GROUP = 6
        STEPS = GROUP * PAIRS // 2
        XN = sb("XN", [P, 2, 2, MT, 2, XW], F16, phase1)
        XT = sb("XT", [P, 2, 2, MT, 4, P], F16, phase1)
        LOW_DVE = 9
        rest32 = sb("rest32", [P, MT - LOW_DVE, D], F32, phase1)
        mx = sb("mx", [P, 2, MT], F32, phase1)
        sm = sb("sm", [P, 2, MT], F32, phase1)
        e32 = sb("e32", [P, 2, MT, N], F32, phase1)
        at16 = sb("at16", [P, 2, 2, MT, N], F16, phase1)
        h32 = sb("h32", [P, 2, D], F32, phase1)
        snT16 = sb("snT16", [P, 4, P], F16, phase1)
        gT16 = sb("gT16", [P, 2, 4, P], F16, phase1)
        hs16 = sb("hs16", [P, 2, 2, D], F16, phase1)
        sn32 = sb("sn32", [P, D], F32, phase1)
        qT16 = sb("qT16", [P, 2, 2, C, P], F16, phase1)
        ssq1 = sb("ssq1", [P, 2], F32, phase1)
        r1 = sb("r1", [P, 2], F32, phase1)
        urs = sb("urs", [P, 1], F32, phase1)
        upd = sb("upd", [P, D], F32, phase1)
        upd16 = sb("upd16", [P, 2, D], F16, phase1)
        rz = sb("rz", [P, 2 * D], F32, phase1)
        cand = sb("cand", [P, D], F32, phase1)
        gtmp = sb("gtmp", [P, D], F32, phase1)

        WP = 1024
        A_PIECES = [(0, c, 0) for c in range(C)] + [(1, c, n) for c in range(C) for n in range(0, 2 * H * DH, WP)]
        W_SPLIT = {8: (0,), 9: (1,), 10: (2,), 11: (3,), 12: (4, 5)}
        wst = sb("wst", [P, 2, WP], F32, phase1)
        split_room = X32[:].bitcast(F16).rearrange("p a t d -> p (a t d)")
        wq16 = split_room[:, 0:2 * C * H * DH].rearrange("p (a c n) -> p a c n", a=2, c=C)
        wkv16 = split_room[:, 2 * C * H * DH:6 * C * H * DH].rearrange("p (a c n) -> p a c n", a=2, c=C)

        def piece_of(k, part):
            kind, c, n = A_PIECES[k]
            return (wq16, wkv16)[kind][:, part, c, n:n + WP]

        SC = [bank[:, 2 * k:2 * k + 2, :].rearrange("p b n -> p (b n)") for k in range(2)]
        SC16 = [bank16[:, 2 * k:2 * k + 2, :].rearrange("p b n -> p (b n)") for k in range(2)]
        U = bank[:, 4, :]
        T16, TQ = bank16[:, 5, :], bank[:, 5, :]
        RZ, NB = bank[:, 6, :], bank[:, 7, :]

        rest_scaled = sem("rest_scaled")
        ones_set = sem("ones_set")
        xhi_done = sem("xhi_done")
        slot_full = sem("slot_full")
        slot_free = sem("slot_free")
        exp_done = sem("exp_done")
        at32_done = sem("at32_done")
        athi_done = sem("athi_done")
        atlo0_done = sem("atlo0_done")
        atlo1_done = sem("atlo1_done")
        u_done = sem("u_done")
        u_free = sem("u_free")
        uhi_done = sem("uhi_done")
        ulo_done = sem("ulo_done")
        rz_full = sem("rz_full")
        new_full = sem("new_full")
        rz_tanh = sem("rz_tanh")
        n_sum = sem("n_sum")
        n_tanh = sem("n_tanh")
        state_set = sem("state_set")
        state_done = sem("state_done")
        x_added = sem("x_added")
        ssq1_done = sem("ssq1_done")
        r1_eps = sem("r1_eps")
        r1_ready = sem("r1_ready")
        sn_ready = sem("sn_ready")
        snhi_done = sem("snhi_done")
        snlo_done = sem("snlo_done")
        hhi_done = sem("hhi_done")
        hlo_done = sem("hlo_done")
        t_full = sem("t_full")
        snT_ready = sem("snT_ready")
        turned_gates = sem("turned_gates")
        gT_ready = sem("gT_ready")
        q_full = sem("q_full")
        qhi_done = sem("qhi_done")
        q_ready = sem("q_ready")
        dve_step = sem("dve_step")
        wst_loaded = [sem(f"wst_loaded{i}") for i in range(2)]
        wst_hi = sem("wst_hi")
        wst_lo = sem("wst_lo")

        def pair_of(s):
            return 2 * (s // GROUP) + s % 2

        def first_step(s):
            return s % GROUP < 2

        def last_step(s):
            return s % GROUP >= GROUP - 2

        def batches_before(s):
            return (2 * pair_of(s), 2 * pair_of(s) + 1) if s < STEPS and first_step(s) else ()

        def wait_state(eng, s):
            if first_step(s):
                eng.wait_ge(state_set, pair_of(s) + 1)
            else:
                eng.wait_ge(state_done, s - 1)

        SQUARE = {-1: {"between": ((1, 0), (1, 1)), "end": ((2, 0), (2, 1))},
                  0: {"middle": ((3, 0),), "late": ((3, 1),)}, 1: {"early": ((4, 0),)}, 2: {"early": ((4, 1),)}, 3: {"early": ((5, 0),)}, 4: {"early": ((5, 1),)},
                  5: {"end": ((6, 0), (6, 1))}, 6: {"middle": ((7, 0),), "late": ((7, 1),)}}
        HIGH = {-1: {"late": ((0, 0), (0, 1), (1, 0), (1, 1))},
                0: {"early": ((2, 0),), "middle": ((2, 1),), "late": ((3, 0), (3, 1))},
                5: {"early": ((4, 0),), "middle": ((4, 1),), "late": ((5, 0), (5, 1))},
                6: {"early": ((6, 0),), "middle": ((6, 1),), "late": ((7, 0), (7, 1))}}
        SCALE = {-1: ((), (1, 2)), 0: ((), (3,)), 3: ((4,), ()), 5: ((5,), (6,)), 6: ((), (7,))}
        TH = 7

        with ExitStack() as p1:
            block = p1.enter_context(nc.Block())

            @block.sync
            def _(sp):
                for b in range(2, B):
                    sp.wait_ge(split_done, b - 1)
                    sp.wait_ge(split_rest, b - 1)
                    load_rows(sp, b)
                for k, (kind, c, n) in enumerate(A_PIECES):
                    if k > 1:
                        sp.wait_ge(wst_lo, k - 1)
                    w = (aWq, aWkv)[kind].rearrange("(c p) n -> p c n", p=P)
                    sp.dma_start(wst[:, k % 2], w[:, c, n:n + WP]).then_inc(wst_loaded[k % 2], 16)

            @block.gpsimd
            def _(pool):
                def low_attention(s):
                    if s:
                        pool.wait_ge(u_done, 2 * s - 1)
                    for i, t in enumerate((slice(0, TH), slice(TH, MT))):
                        pool.wait_ge(at32_done, 2 * s + 1)
                        pool.wait_ge(athi_done, 3 * s + i + 1)
                        pool.tensor_tensor(at16[:, 0, 1, t], e32[:, 0, t], at16[:, 0, 0, t],
                                           ALU.subtract).then_inc(atlo0_done, 1)

                def low_rows(b):
                    rows = slice(LOW_DVE, MT)
                    pool.wait_ge(rinv_ready, b + 1)
                    if b:
                        pool.wait_ge(split_rest, b)
                    pool.tensor_tensor(rest32[:], X32[:, b % 2, rows, :],
                                       rinv[:, b % 2, rows].unsqueeze(2).broadcast_to([P, MT - LOW_DVE, D]),
                                       ALU.mult).then_inc(rest_scaled, 1)
                    pool.wait_ge(rest_scaled, b + 1)
                    pool.wait_ge(xhi_done, 2 * b + 2)
                    pool.tensor_tensor(XN[:, (b // 2) % 2, b % 2, rows, 1, 0:D], rest32[:],
                                       XN[:, (b // 2) % 2, b % 2, rows, 0, 0:D],
                                       ALU.subtract).then_inc(split_rest, 1)

                def state_scale(s):
                    X = s % 2
                    pool.wait_ge(ssq1_done, s + 1)
                    if s > 1:
                        pool.wait_ge(sn_ready, s - 1)
                    pool.tensor_tensor(r1[:, X:X + 1], ssq1[:, X:X + 1], eps_rms[:, 0:1],
                                       ALU.add).then_inc(r1_eps, 1)
                    pool.wait_ge(r1_eps, s + 1)
                    pool.tensor_tensor(r1[:, X:X + 1], r1[:, X:X + 1], half[:, 0:1], ALU.pow).then_inc(r1_ready, 1)
                    pool.wait_ge(hhi_done, s + 1)
                    if s:
                        pool.wait_ge(turned_gates, s)
                    wait_state(pool, s)
                    pool.tensor_tensor(hs16[:, 1, 1], h32[:, X], hs16[:, 1, 0], ALU.subtract).then_inc(hlo_done, 1)

                def add_state(s):
                    pool.wait_ge(state_done, s + 1)
                    pool.tensor_tensor(x_sb[:, pair_of(s)], x_sb[:, pair_of(s)], h32[:, s % 2],
                                       ALU.add).then_inc(x_added, 1)

                for s in range(-1, STEPS + 1):
                    if s == STEPS:
                        add_state(s - 1)
                        continue
                    early, late = SCALE.get(s, ((), ()))
                    for b in early:
                        rinv_of(pool, b)
                    if s >= 0:
                        low_attention(s)
                    if s >= 1 and last_step(s - 1):
                        add_state(s - 1)
                    if s + 1 < STEPS:
                        state_scale(s + 1)
                    ahead = batches_before(s + 1)
                    for b in ahead:
                        for r in late:
                            if r == b:
                                rinv_of(pool, b)
                        low_rows(b)
                    for b in late:
                        if b not in ahead:
                            rinv_of(pool, b)

            @block.scalar
            def _(act):
                slots = Count()

                def high_rows(b, piece):
                    act.wait_ge(rinv_ready, b + 1)
                    X = (b // 2) % 2
                    if b > 3:
                        act.wait_ge(u_done, 2 * (GROUP * (b // 4) + X - 2) + 2)
                    for t in range(*PIECES[piece]):
                        ins = act.activation(XN[:, X, b % 2, t, 0, 0:D], X32[:, b % 2, t, :], ACT.Copy,
                                             scale=rinv[:, b % 2, t:t + 1])
                    ins.then_inc(xhi_done, 1)

                def high_update(s):
                    act.wait_ge(u_free, s + 1)
                    if s:
                        act.wait_ge(turned_gates, s + 1)
                    act.activation(upd16[:, 0], upd[:], ACT.Copy).then_inc(uhi_done, 1)

                def high_weights(k):
                    act.wait_ge(wst_loaded[k % 2], 16 * (k // 2 + 1))
                    act.wait_ge(split_done, B)
                    act.wait_ge(split_rest, B)
                    act.activation(piece_of(k, 0), wst[:, k % 2], ACT.Copy, scale=WS).then_inc(wst_hi, 1)

                def take_turned(s):
                    a, b = (0 if s < STEPS else 1), (2 if s else 1)
                    act.wait_ge(turned_gates, s + 1)
                    act.activation(gT16[:, a:b].rearrange("p g a n -> p (g a n)"),
                                   T16[:, a * 4 * P:b * 4 * P], ACT.Copy).then_inc(gT_ready, 1)

                def exponentials(s, j):
                    act.wait_ge(slot_free, slots.next())
                    act.activation(e32[:, j], e32[:, j], ACT.Exp, scale=float(D) ** -0.5).then_inc(exp_done, 1)

                def high_attention(s, j):
                    act.wait_ge(at32_done, 2 * s + j + 1)
                    if s:
                        act.wait_ge(u_done, 2 * s + j - 1)
                    for t in (slice(0, TH), slice(TH, MT)) if j == 0 else (slice(0, MT),):
                        act.activation(at16[:, j, 0, t], e32[:, j, t], ACT.Copy).then_inc(athi_done, 1)

                def gates(s):
                    act.wait_ge(rz_full, s + 1)
                    if s:
                        act.wait_ge(state_done, s)
                    for half_ in range(2):
                        cols = slice(half_ * D, (half_ + 1) * D)
                        act.activation(rz[:, cols], RZ[:, cols], ACT.Tanh, scale=0.5 / WS).then_inc(rz_tanh, 1)

                def candidate(s):
                    act.wait_ge(n_sum, s + 1)
                    act.activation(cand[:], cand[:], ACT.Tanh, scale=1.0 / WS).then_inc(n_tanh, 1)

                def high_state(s):
                    X = s % 2
                    wait_state(act, s)
                    if s:
                        act.wait_ge(turned_gates, s)
                    if s > 1:
                        act.wait_ge(r1_ready, s - 1)
                    act.activation(hs16[:, 0, 0], h32[:, X], ACT.Square, scale=float(D) ** -0.5,
                                   accum_out=ssq1[:, X:X + 1]).then_inc(ssq1_done, 1)
                    act.activation(hs16[:, 1, 0], h32[:, X], ACT.Copy).then_inc(hhi_done, 1)

                def high_normalised(s):
                    act.wait_ge(sn_ready, s + 1)
                    act.activation(hs16[:, 0, 0], sn32[:], ACT.Copy).then_inc(snhi_done, 1)

                def high_query(s):
                    act.wait_ge(q_full, s + 1)
                    act.activation(qT16[:, s % 2, 0].rearrange("p c n -> p (c n)"), TQ[:, 0:D],
                                   ACT.Copy, scale=1.0 / WS).then_inc(qhi_done, 1)

                for s in range(-1, STEPS + 1):
                    def squares(when):
                        for b, piece in SQUARE.get(s, {}).get(when, ()):
                            square_rows(act, b, piece)

                    def highs(when, which=range(B)):
                        for b, piece in HIGH.get(s, {}).get(when, ()):
                            if b in which:
                                high_rows(b, piece)

                    ahead = batches_before(s + 1)
                    if s >= 1:
                        high_update(s - 1)
                    squares("early")
                    highs("early")
                    if s >= 0:
                        take_turned(s)
                    for k in W_SPLIT.get(s, ()):
                        high_weights(k)
                    if 0 <= s < STEPS:
                        exponentials(s, 0)
                    if s >= 1:
                        gates(s - 1)
                    if 0 <= s < STEPS:
                        exponentials(s, 1)
                    highs("middle")
                    squares("middle")
                    if 0 <= s < STEPS:
                        high_attention(s, 0)
                    if s >= 1:
                        candidate(s - 1)
                    if 0 <= s < STEPS:
                        high_attention(s, 1)
                    squares("late")
                    if s + 1 < STEPS:
                        high_state(s + 1)
                        highs("late", ahead[:1])
                        high_normalised(s + 1)
                        squares("between")
                        highs("late", ahead[1:])
                        high_query(s + 1)
                    slots.next(4 * len(ahead))
                    squares("end")

            @block.tensor
            def _(pe):
                slots = Count()

                def slot():
                    k = slots.n % 2
                    if slots.next() > 2:
                        pe.wait_ge(slot_free, slots.n - 2)
                    return k

                def split_matmul(out_, stat, mov, cs, first=True, last_=True):
                    todo = [(c, a, b) for c in cs for a, b in PASSES]
                    for i, (c, a, b) in enumerate(todo):
                        ins = pe.matmul(out_, stat(a, c), mov(b, c), start=(first and i == 0),
                                        stop=(last_ and i == len(todo) - 1))
                    return ins

                def turn_rows(b):
                    pe.wait_ge(split_done, b + 1)
                    for t0 in range(0, MT, 4):
                        if t0 + 4 > LOW_DVE:
                            pe.wait_ge(split_rest, b + 1)
                        k = slot()
                        for t in range(t0, min(t0 + 4, MT)):
                            for part in range(2):
                                for c in range(C):
                                    o = ((t - t0) * 4 + part * C + c) * P
                                    last = pe.transpose(SC16[k][:, o:o + P],
                                                        XN[:, (b // 2) % 2, b % 2, t, part, c * P:(c + 1) * P],
                                                        ident16[:])
                        last.then_inc(slot_full, 1)

                def bias(out_, cols, **kw):
                    pe.matmul(out_, ones16[0:LO + 1, :], bias16[0:LO + 1, cols], start=True, **kw)

                def gates_of_state(s):
                    pe.wait_ge(gT_ready, s + 1)
                    if s:
                        pe.wait_ge(rz_tanh, 2 * s)
                    hp = lambda a, c: gT16[:, 0, a * C + c, :]
                    bias(RZ, slice(0, 2 * D), stop=False)
                    split_matmul(RZ, hp, lambda b, c: whhT16[:, b, c, 0:2 * D], range(C), False, False)
                    if s:
                        pe.wait_ge(n_sum, s)
                    bias(NB[:, D:2 * D], slice(3 * D, 4 * D), stop=False)
                    split_matmul(NB[:, D:2 * D], hp, lambda b, c: whhT16[:, b, c, 2 * D:G], range(C), False)

                def gates_of_update(s):
                    pe.wait_ge(gT_ready, s + 2)
                    up = lambda a, c: gT16[:, 1, a * C + c, :]
                    split_matmul(RZ, up, lambda b, c: wihT16[:, b, c, 0:2 * D], range(C), False).then_inc(rz_full, 1)
                    bias(NB[:, 0:D], slice(2 * D, 3 * D), stop=False)
                    split_matmul(NB[:, 0:D], up, lambda b, c: wihT16[:, b, c, 2 * D:G], range(C),
                                 False).then_inc(new_full, 1)

                def scores(s):
                    X = s % 2
                    pe.wait_ge(q_ready, s + 1)
                    if first_step(s):
                        pe.wait_ge(slot_free, slots.n)
                    for j in range(2):
                        k = slot()
                        for t in range(MT):
                            last = split_matmul(SC[k][:, t * N:(t + 1) * N],
                                                lambda a, c: XT[:, X, j, t, a * C + c, :],
                                                lambda b, c: qT16[:, X, b, c, j * N:(j + 1) * N], range(C))
                        last.then_inc(slot_full, 1)
                        if j == 0:
                            turn_gates(s)

                def update(s, j, t0, t1):
                    for t in range(t0, t1):
                        for i, (a, b) in enumerate(PASSES):
                            w = D + 1 if b == 0 else D
                            ins = pe.matmul(U[j * N:(j + 1) * N, 0:w], at16[:, j, a, t, :],
                                            XN[:, s % 2, j, t, b, 0:w], start=(t == 0 and i == 0),
                                            stop=(t == MT - 1 and i == 2))
                    return ins

                def update_first(s):
                    if s:
                        pe.wait_ge(u_free, s)
                    for i, (t0, t1) in enumerate(((0, TH), (TH, MT))):
                        pe.wait_ge(athi_done, 3 * s + i + 1)
                        pe.wait_ge(atlo0_done, 2 * s + i + 1)
                        last = update(s, 0, t0, t1)
                    last.then_inc(u_done, 1)

                def turn(o, tile):
                    for part in range(2):
                        for c in range(C):
                            last = pe.transpose(T16[:, o:o + P], tile[:, part, c * P:(c + 1) * P], ident16[:])
                            o += P
                    return last

                def turn_state(s):
                    if s:
                        pe.wait_ge(gT_ready, s)
                    pe.wait_ge(snlo_done, s + 1)
                    turn(0, hs16[:, 0]).then_inc(t_full, 1)

                def turn_gates(s):
                    if s < STEPS:
                        pe.wait_ge(q_ready, s + 1)
                        pe.wait_ge(hlo_done, s + 1)
                        last = turn(0, hs16[:, 1])
                    if s:
                        pe.wait_ge(ulo_done, s)
                        last = turn(4 * P, upd16)
                    last.then_inc(turned_gates, 1)

                def query(s):
                    pe.wait_ge(snT_ready, s + 1)
                    for e in range(C):
                        last = split_matmul(TQ[:, e * P:(e + 1) * P],
                                            lambda a, c: A16[:, a, c, e * P:(e + 1) * P],
                                            lambda b, c: snT16[:, b * C + c, :], range(C))
                    last.then_inc(q_full, 1)

                for s in range(-1, STEPS + 1):
                    live = 0 <= s < STEPS
                    if live:
                        scores(s)
                    elif s == STEPS:
                        turn_gates(s)
                    if s >= 1:
                        gates_of_update(s - 1)
                    if live:
                        gates_of_state(s)
                        update_first(s)
                        pe.wait_ge(athi_done, 3 * s + 3)
                        pe.wait_ge(atlo1_done, s + 1)
                        update(s, 1, 0, MT // 3)
                    if s + 1 < STEPS:
                        ahead = batches_before(s + 1)
                        if not ahead:
                            turn_state(s + 1)
                        if live:
                            update(s, 1, MT // 3, 2 * MT // 3)
                        if not ahead:
                            query(s + 1)
                        if live:
                            update(s, 1, 2 * MT // 3, MT).then_inc(u_done, 1)
                        if ahead:
                            turn_state(s + 1)
                            turn_rows(ahead[0])
                            query(s + 1)
                            turn_rows(ahead[1])
                    elif live:
                        update(s, 1, MT // 3, MT).then_inc(u_done, 1)

            @block.vector
            def _(dve):
                slots = Count()
                steps = Count()
                for q in range(4):
                    col = XN[:, q // 2, q % 2]
                    dve.memset(col[:, 0:MR, 0, D:XW], 1.0)
                    dve.memset(col[:, :, 1, D:XW], 0.0)
                    dve.memset(col[:, MR, 0, D:XW], 0.0).then_inc(ones_set, 1)
                dve.wait_ge(ones_set, 4)
                for q in range(4):
                    dve.memset(XN[0:TAIL, q // 2, q % 2, MR, 0, D:XW], 1.0).then_inc(ones_set, 1)

                def link(ins):
                    ins.then_inc(dve_step, 1)
                    dve.wait_ge(dve_step, steps.next())

                def low_rows(b):
                    X = (b // 2) % 2
                    dve.wait_ge(xhi_done, 2 * b + 1)
                    for t in range(LOW_DVE):
                        if t == PIECES[1][0]:
                            dve.wait_ge(xhi_done, 2 * b + 2)
                        ins = dve.scalar_tensor_tensor(XN[:, X, b % 2, t, 1, 0:D], X32[:, b % 2, t, :],
                                                       rinv[:, b % 2, t:t + 1], XN[:, X, b % 2, t, 0, 0:D],
                                                       ALU.mult, ALU.subtract)
                    ins.then_inc(split_done, 1)

                def take_rows(b):
                    for t0 in range(0, MT, 4):
                        k = slots.n % 2
                        w = min(4, MT - t0)
                        dve.wait_ge(slot_full, slots.next())
                        dve.tensor_copy(XT[:, (b // 2) % 2, b % 2, t0:t0 + w].rearrange("p t a n -> p (t a n)"),
                                        SC16[k][:, 0:w * 4 * P]).then_inc(slot_free, 1)

                def shift(s, j):
                    k = slots.n % 2
                    dve.wait_ge(slot_full, slots.next())
                    sc = SC[k][:, 0:MT * N].rearrange("p (t n) -> p t n", n=N)
                    link(dve.reduce_max(mx[:, j], sc, AX_X))
                    if s and j == 0:
                        dve.wait_ge(atlo0_done, 2 * s)
                    elif s:
                        dve.wait_ge(atlo1_done, s)
                    dve.tensor_tensor(e32[:, j], sc, mx[:, j].unsqueeze(2).broadcast_to([P, MT, N]),
                                      ALU.subtract).then_inc(slot_free, 1)

                def norm(s, j):
                    dve.wait_ge(exp_done, 2 * s + j + 1)
                    link(dve.reduce_sum(sm[:, j], e32[:, j], AX_X))
                    link(dve.reciprocal(sm[:, j], sm[:, j]))
                    dve.scalar_tensor_tensor(e32[:, j], e32[:, j], AS,
                                             sm[:, j].unsqueeze(2).broadcast_to([P, MT, N]),
                                             ALU.mult, ALU.mult).then_inc(at32_done, 1)

                def low_attention(s):
                    dve.wait_ge(at32_done, 2 * s + 2)
                    dve.wait_ge(athi_done, 3 * s + 3)
                    if s:
                        dve.wait_ge(u_done, 2 * s)
                    dve.tensor_tensor(at16[:, 1, 1], e32[:, 1], at16[:, 1, 0], ALU.subtract).then_inc(atlo1_done, 1)

                def low_weights(k):
                    dve.wait_ge(wst_hi, k + 1)
                    dve.scalar_tensor_tensor(piece_of(k, 1), wst[:, k % 2], WS, piece_of(k, 0), ALU.mult,
                                             ALU.subtract).then_inc(wst_lo, 1)

                def take_update(s):
                    dve.wait_ge(u_done, 2 * s + 2)
                    if s:
                        dve.wait_ge(ulo_done, s)
                    link(dve.tensor_scalar(urs[:], U[:, D:D + 1], AS * 1e-6, None, ALU.add))
                    link(dve.reciprocal(urs[:], urs[:]))
                    dve.tensor_scalar(upd[:], U[:, 0:D], urs[:], None, ALU.mult).then_inc(u_free, 1)
                    dve.wait_ge(u_free, s + 1)
                    dve.wait_ge(uhi_done, s + 1)
                    dve.tensor_tensor(upd16[:, 1], upd[:], upd16[:, 0], ALU.subtract).then_inc(ulo_done, 1)

                def candidate(s):
                    dve.wait_ge(rz_tanh, 2 * s + 1)
                    dve.wait_ge(new_full, s + 1)
                    if s:
                        dve.wait_ge(state_done, s)
                    link(dve.scalar_tensor_tensor(gtmp[:], rz[:, 0:D], 1.0, NB[:, D:2 * D], ALU.add, ALU.mult))
                    dve.scalar_tensor_tensor(cand[:], gtmp[:], 0.5, NB[:, 0:D], ALU.mult, ALU.add).then_inc(n_sum, 1)

                def new_state(s):
                    X = s % 2
                    dve.wait_ge(n_tanh, s + 1)
                    dve.wait_ge(rz_tanh, 2 * s + 2)
                    link(dve.tensor_tensor(gtmp[:], h32[:, X], cand[:], ALU.subtract))
                    link(dve.scalar_tensor_tensor(gtmp[:], rz[:, D:2 * D], 1.0, gtmp[:], ALU.add, ALU.mult))
                    dve.scalar_tensor_tensor(h32[:, X], gtmp[:], 0.5, cand[:], ALU.mult,
                                             ALU.add).then_inc(state_done, 1)

                def first_state(s):
                    if s > 1:
                        dve.wait_ge(x_added, pair_of(s) - 1)
                    dve.tensor_copy(h32[:, s % 2], s0[:, pair_of(s)]).then_inc(state_set, 1)

                def normalise_state(s):
                    X = s % 2
                    wait_state(dve, s)
                    dve.wait_ge(r1_ready, s + 1)
                    dve.tensor_scalar(sn32[:], h32[:, X], r1[:, X:X + 1], None, ALU.mult).then_inc(sn_ready, 1)

                def low_normalised(s):
                    dve.wait_ge(snhi_done, s + 1)
                    dve.wait_ge(sn_ready, s + 1)
                    dve.tensor_tensor(hs16[:, 0, 1], sn32[:], hs16[:, 0, 0], ALU.subtract).then_inc(snlo_done, 1)

                def query(s):
                    X = s % 2
                    dve.wait_ge(t_full, s + 1)
                    dve.tensor_copy(snT16[:].rearrange("p a n -> p (a n)"), T16[:, 0:4 * P]).then_inc(snT_ready, 1)
                    dve.wait_ge(qhi_done, s + 1)
                    dve.scalar_tensor_tensor(qT16[:, X, 1].rearrange("p c n -> p (c n)"), TQ[:, 0:D], 1.0 / WS,
                                             qT16[:, X, 0].rearrange("p c n -> p (c n)"),
                                             ALU.mult, ALU.subtract).then_inc(q_ready, 1)

                for s in range(-1, STEPS + 1):
                    live = 0 <= s < STEPS
                    ahead = batches_before(s + 1)
                    if s >= 1:
                        take_update(s - 1)
                    if live:
                        shift(s, 0)
                        shift(s, 1)
                        norm(s, 0)
                    if s >= 1:
                        candidate(s - 1)
                    if live:
                        norm(s, 1)
                    if s >= 1:
                        new_state(s - 1)
                    if live:
                        low_attention(s)
                    for k in W_SPLIT.get(s, ()):
                        low_weights(k)
                    if s + 1 < STEPS:
                        if ahead:
                            first_state(s + 1)
                        normalise_state(s + 1)
                        for b in ahead[:1]:
                            low_rows(b)
                        low_normalised(s + 1)
                        for b in ahead[:1]:
                            take_rows(b)
                        for b in ahead[1:]:
                            low_rows(b)
                        query(s + 1)
                        for b in ahead[1:]:
                            take_rows(b)

        phase1.close()
        KC = H * DH // P
        BITS = [64, 32, 16, 8, 4, 2, 1]

        gu32 = sb("gu32", [P, 2, C, 2 * F], F32)
        dn32 = sb("dn32", [P, 2, FC, D], F32)
        w_loaded = [sem(f"w_loaded{i}") for i in range(2)]
        gu_dram = gate_up_w.rearrange("e (c p) n -> e p c n", p=P)
        dn_dram = down_w.rearrange("e (c p) n -> e p c n", p=P)

        with ExitStack() as p2:
            wo32 = sb("wo32", [P, KC, D], F32, p2)
            pos32 = sb("pos32", [P, DH], F32, p2)
            wo16 = sb("wo16", [P, 2, KC, D], F16, p2)
            pos16 = sb("pos16", [P, 2, DH], F16, p2)
            bo = sb("bo", [P, D], F32, p2)
            reset = sb("reset", [P, H, V1], F32, p2)
            ones = sb("ones", [P, H, V1], F32, p2)
            vpos = sb("vpos", [P, H, V1], F32, p2)
            a_stats = sb("a_stats", [P, PAIRS, 6], F32, p2)
            a_mv = sb("a_mv", [P, PAIRS, 2], F32, p2)
            a_r = sb("a_r", [P, PAIRS], F32, p2)
            a_x = sb("a_x", [P, D], F32, p2)
            a_x16 = sb("a_x16", [P, 2, D], F16, p2)
            xT16 = sb("xT16", [P, 2, 2, C, P], F16, p2)
            q16 = sb("q16", [P, 2, 2, KC, P], F16, p2)
            k16 = sb("k16", [P, 2, 2, KC, P], F16, p2)
            v16 = sb("v16", [P, 3, 2, H * DH], F16, p2)
            gs = sb("gs", [P, H, V1], F32, p2)
            fl = sb("fl", [P, H, V1], F32, p2)
            ar = sb("ar", [P, H, V1], F32, p2)
            viota = sb("viota", [P, H, V1], I32, p2)
            s16 = sb("s16", [P, H, V1], I16, p2)
            mask = sb("mask", [P, len(BITS), H, V1], I16, p2)
            tab = sb("tab", [P, 2, 2, H, V1], F32, p2)
            lg = sb("lg", [P, 2, H, N], F32, p2)
            hs_ = sb("hs_", [P, 2, H], F32, p2)
            p16 = sb("p16", [P, 2, 2, H, 2, N], F16, p2)
            pT16 = sb("pT16", [P, 2, H, P], F16, p2)
            o16 = sb("o16", [P, 2, KC, P], F16, p2)
            tmp = sb("tmp", [P, D], F32, p2)

            w_in = [sem(f"w_in{i}") for i in range(2)]
            a_const = sem("a_const")
            a_zero = sem("a_zero")
            a_whi = sem("a_whi")
            a_wlo = sem("a_wlo")
            ln_st = sem("ln_st")
            ln_mv = sem("ln_mv")
            ln_pool = sem("ln_pool")
            ln_r = sem("ln_r")
            ln_x = sem("ln_x")
            ln_hi = sem("ln_hi")
            ln_lo = sem("ln_lo")
            xT_full = sem("xT_full")
            xT_done = sem("xT_done")
            proj_full = sem("proj_full")
            proj_hi = sem("proj_hi")
            proj_lo = sem("proj_lo")
            sim_full = sem("sim_full")
            sim_free = sem("sim_free")
            e_full = sem("e_full")
            gs_used = sem("gs_used")
            gs_ready = sem("gs_ready")
            tab_diff = sem("tab_diff")
            gate_tanh = sem("gate_tanh")
            tab_made = sem("tab_made")
            tab_moved = sem("tab_moved")
            tab_picked = sem("tab_picked")
            logit_done = sem("logit_done")
            a_exp = sem("a_exp")
            p32_done = sem("p32_done")
            phi_done = sem("phi_done")
            plo_done = sem("plo_done")
            pT_full = sem("pT_full")
            pT_done = sem("pT_done")
            o_full = sem("o_full")
            o_hi = sem("o_hi")
            o_lo = sem("o_lo")
            y_full = sem("y_full")
            y_done = sem("y_done")
            blocks_picked = sem("blocks_picked")
            a_step = sem("a_step")
            block = p2.enter_context(nc.Block())
            BLOCKED = [b for b in BITS if b >= 16]
            COPIED = [b for b in BITS if b < 16]

            def banks(X, b0, n):
                return bank[:, 4 * X + b0:4 * X + b0 + n, :].rearrange("p b n -> p (b n)")

            def banks16(X, b0, n):
                return bank16[:, 4 * X + b0:4 * X + b0 + n, :].rearrange("p b n -> p (b n)")

            flat3 = lambda t: t.rearrange("p h v -> p (h v)")
            flat_c = lambda t: t.rearrange("p c n -> p (c n)")

            @block.sync
            def _(sp):
                sp.dma_start(pos32[0:DH, :], pos_emb).then_inc(w_in[0], 16)
                sp.dma_start(pos32[DH:P, :], pos_emb).then_inc(w_in[0], 16)
                sp.dma_start(wo32[:], aWout.rearrange("(c p) n -> p c n", p=P)).then_inc(w_in[1], 16)
                sp.dma_start(bo[:], ab_out.rearrange("(a n) -> a n", a=1).broadcast_to([P, D])).then_inc(w_in[1], 16)
                for s in range(2):
                    sp.dma_start(gu32[:, s], gu_dram[s]).then_inc(w_loaded[s], 16)
                    sp.dma_start(dn32[:, s], dn_dram[s]).then_inc(w_loaded[s], 16)

            WEIGHTS = ((pos16, pos32, w_in[0], 32), (wo16, wo32, w_in[1], 32))

            @block.gpsimd
            def _(pool):
                pool.wait_ge(ln_mv, PAIRS)
                pool.tensor_scalar(a_r[:], a_mv[:, :, 1], 1.0, 1e-5, ALU.mult, ALU.add).then_inc(ln_pool, 1)
                pool.wait_ge(ln_pool, 1)
                pool.tensor_tensor(a_r[:], a_r[:], half[:, 0:PAIRS], ALU.pow).then_inc(ln_r, 1)
                pool.iota(viota[:], pattern=[[0, H], [1, V1]], base=0, channel_multiplier=0).then_inc(a_const, 1)
                pool.memset(reset[:], 1.0).then_inc(a_const, 1)
                pool.memset(ones[:], 1.0).then_inc(a_const, 1)
                pool.wait_ge(a_const, 3)
                pool.memset(reset[:, :, 0:1], 0.0).then_inc(a_const, 1)
                pool.tensor_scalar(vpos[:], viota[:], 1.0, MAGIC, ALU.mult, ALU.add).then_inc(a_const, 1)
                pool.memset(gs[:, :, 0:1], 0.0).then_inc(a_const, 1)
                for X in range(2):
                    pool.memset(p16[:, X].rearrange("p a h b n -> p (a h b n)"), 0.0).then_inc(a_zero, 1)
                pool.wait_ge(a_zero, 2)

                def sigmoid(q):
                    pool.wait_ge(gate_tanh, q + 1)
                    pool.tensor_scalar(gs[:, :, 1:V1], gs[:, :, 1:V1], 0.5, 0.5, ALU.mult, ALU.add).then_inc(gs_ready, 1)

                def differences(q):
                    X = q % 2
                    pool.wait_ge(tab_made, q + 1)
                    pool.tensor_tensor(tab[:, X, 1], tab[:, X, 1], tab[:, X, 0], ALU.subtract).then_inc(tab_diff, 1)

                def low_weights(q):
                    X = q % 2
                    pool.wait_ge(phi_done, q + 1)
                    for b in range(2):
                        r = slice(b * N, (b + 1) * N)
                        pool.tensor_tensor(p16[r, X, 1, :, b, :], lg[r, X], p16[r, X, 0, :, b, :],
                                           ALU.subtract).then_inc(plo_done, 1)
                        pool.wait_ge(plo_done, q * 2 + b + 1)

                for q in range(PAIRS):
                    if q == 0:
                        sigmoid(0)
                        differences(0)
                    if q + 1 < PAIRS:
                        sigmoid(q + 1)
                        differences(q + 1)
                    low_weights(q)

            @block.scalar
            def _(act):
                def weights(i):
                    w16, w32, s, n = WEIGHTS[i]
                    act.wait_ge(s, n)
                    act.activation(w16[:, 0], w32[:], ACT.Copy, scale=WS).then_inc(a_whi, 1)

                def high_x(q):
                    act.wait_ge(ln_x, q + 1)
                    act.activation(a_x16[:, 0], a_x[:], ACT.Copy).then_inc(ln_hi, 1)

                def high_proj(q, i):
                    X = q % 2
                    dst, b0 = ((q16, 2), (k16, 0), (v16, 2))[i]
                    act.wait_ge(proj_full, q * 3 + i + 1)
                    hi = flat_c(dst[:, X, 0]) if i < 2 else dst[:, q % 3, 0]
                    act.activation(hi, banks(X, b0, 2), ACT.Copy, scale=1.0 / WS).then_inc(proj_hi, 1)

                def gates(q):
                    X = q % 2
                    act.wait_ge(sim_full, q + 1)
                    if q:
                        act.wait_ge(gs_used, q)
                    act.activation(gs[:, :, 1:V1], banks(X, 0, 2).rearrange("p (h n) -> p h n", n=N),
                                   ACT.Tanh, scale=0.5 * DH ** -0.5).then_inc(gate_tanh, 1)

                def tables(q):
                    X = q % 2
                    if q:
                        act.wait_ge(tab_picked, 2 * q * len(COPIED))
                    act.wait_ge(e_full, q + 1)
                    e = banks(X, 2, 2).rearrange("p (h n) -> p h n", n=N)
                    act.activation(tab[:, X, 0, :, 0:N], e, ACT.Copy, scale=1.0 / WS)
                    act.activation(tab[:, X, 1, :, 0:N - 1], e[:, :, 1:N], ACT.Copy, scale=1.0 / WS)
                    act.activation(tab[:, X, 0, :, N:V1], e[:, :, N - 1:N], ACT.Copy, scale=1.0 / WS)
                    act.activation(tab[:, X, 1, :, N - 1:V1], e[:, :, N - 1:N].broadcast_to([P, H, 2]),
                                   ACT.Copy, scale=1.0 / WS).then_inc(tab_made, 1)

                def move(q, i):
                    cur = (q + i) % 2
                    for t in range(2):
                        if i == 0:
                            act.wait_ge(blocks_picked, 2 * q + t + 1)
                        else:
                            act.wait_ge(tab_picked, 2 * (q * len(COPIED) + i - 1) + t + 1)
                        act.activation(tab[:, 1 - cur, t], tab[:, cur, t], ACT.Copy).then_inc(tab_moved, 1)

                def transposed(q, part):
                    act.wait_ge(pT_full, 2 * q + part + 1)
                    act.activation(pT16[:, part].rearrange("p h n -> p (h n)"), banks16((q + 1) % 2, 2, 2),
                                   ACT.Copy).then_inc(pT_done, 1)

                def high_o(q):
                    act.wait_ge(o_full, q + 1)
                    act.activation(flat_c(o16[:, 0]), banks((q + 1) % 2, 2, 2), ACT.Copy, scale=1.0 / AS).then_inc(o_hi, 1)

                def soft(q):
                    X = q % 2
                    act.wait_ge(logit_done, q + 1)
                    if q:
                        act.wait_ge(p32_done, q)
                    for h in range(H):
                        ins = act.activation(lg[:, X, h], lg[:, X, h], ACT.Exp, bias=hs_[:, 0, h:h + 1],
                                             accum_out=hs_[:, 1, h:h + 1])
                    ins.then_inc(a_exp, 1)

                def high_p(q):
                    X = q % 2
                    if q < 2:
                        act.wait_ge(a_zero, q + 1)
                    act.wait_ge(p32_done, q + 1)
                    for b in range(2):
                        r = slice(b * N, (b + 1) * N)
                        ins = act.activation(p16[r, X, 0, :, b, :], lg[r, X], ACT.Copy)
                    ins.then_inc(phi_done, 1)

                weights(0)
                high_x(0)
                for i in range(3):
                    high_proj(0, i)
                high_x(1)
                weights(1)
                gates(0)
                tables(0)
                high_proj(1, 0)
                high_proj(1, 1)
                for q in range(PAIRS):
                    nxt = q + 1 < PAIRS
                    if q:
                        transposed(q - 1, 0)
                    move(q, 0)
                    if nxt:
                        high_proj(q + 1, 2)
                    if q:
                        transposed(q - 1, 1)
                    move(q, 1)
                    move(q, 2)
                    move(q, 3)
                    if q + 2 < PAIRS:
                        high_x(q + 2)
                    if nxt:
                        gates(q + 1)
                    if q:
                        high_o(q - 1)
                    if nxt:
                        tables(q + 1)
                    soft(q)
                    if q + 2 < PAIRS:
                        high_proj(q + 2, 0)
                        high_proj(q + 2, 1)
                    high_p(q)
                transposed(PAIRS - 1, 0)
                transposed(PAIRS - 1, 1)
                high_o(PAIRS - 1)

            @block.tensor
            def _(pe):
                def split(out_, stat, mov, cs):
                    todo = [(c, a, b) for c in cs for a, b in PASSES]
                    for i, (c, a, b) in enumerate(todo):
                        ins = pe.matmul(out_, stat(a, c), mov(b, c), start=(i == 0), stop=(i == len(todo) - 1))
                    return ins

                def turn_x(q):
                    X = q % 2
                    pe.wait_ge(ln_lo, q + 1)
                    if q > 1:
                        pe.wait_ge(sim_free, q - 1)
                    for i, perm in enumerate((ident16, flip16)):
                        for part in range(2):
                            for c in range(C):
                                o = (part * C + c) * P
                                last = pe.matmul(banks(X, i, 1)[:, o:o + P], a_x16[:, part, c * P:(c + 1) * P],
                                                 perm[:], start=True, stop=True)
                        last.then_inc(xT_full, 1)

                def queries_keys(q):
                    X = q % 2
                    if q > 2:
                        pe.wait_ge(y_done, q - 2)
                    pe.wait_ge(xT_done, q + 1)
                    for i, (b0, w16) in enumerate(((2, wq16), (0, wkv16))):
                        for t in range(KC):
                            last = split(banks(X, b0, 2)[:, t * P:(t + 1) * P],
                                         lambda a, c: w16[:, a, c, t * P:(t + 1) * P],
                                         lambda b, c: xT16[:, i, b, c, :], range(C))
                        last.then_inc(proj_full, 1)

                def values(q):
                    pe.wait_ge(proj_lo, q * 3 + 1)
                    for t in range(2):
                        last = split(banks(q % 2, 2 + t, 1), lambda a, c: xT16[:, 1, a, c, :],
                                     lambda b, c: wkv16[:, b, c, H * DH + t * 512:H * DH + (t + 1) * 512], range(C))
                    last.then_inc(proj_full, 1)

                def scores(q):
                    X = q % 2
                    pe.wait_ge(proj_lo, q * 3 + 2)
                    for t in range(KC):
                        for r in range(2):
                            rows = slice(r * DH, (r + 1) * DH)
                            for b in range(2):
                                cols = slice(b * N, (b + 1) * N)
                                last = split(banks(X, r, 1)[cols, t * N:(t + 1) * N],
                                             lambda a, c: q16[rows, X, a, t, cols],
                                             lambda a, c: k16[rows, X, a, t, cols], range(1))
                    last.then_inc(sim_full, 1)
                    pe.wait_ge(proj_lo, q * 3 + 3)
                    pe.wait_ge(a_wlo, 1)
                    for t in range(KC):
                        for r in range(2):
                            rows = slice(r * DH, (r + 1) * DH)
                            last = split(banks(X, 2 + r, 1)[:, t * N:(t + 1) * N], lambda a, c: q16[rows, X, a, t, :],
                                         lambda a, c: pos16[rows, a, :], range(1))
                    last.then_inc(e_full, 1)


                def turn_weights(q, part):
                    Y = (q + 1) % 2
                    if part:
                        pe.wait_ge(plo_done, 2 * q + 2)
                        pe.wait_ge(pT_done, 2 * q + 1)
                    else:
                        pe.wait_ge(phi_done, q + 1)
                        if q + 1 < PAIRS:
                            pe.wait_ge(tab_made, q + 2)
                        else:
                            pe.wait_ge(y_done, q - 1)
                    for h in range(H):
                        last = pe.transpose(banks16(Y, 2, 2)[:, h * P:(h + 1) * P],
                                            p16[:, q % 2, part, h].rearrange("p b n -> p (b n)"), ident16[:])
                    last.then_inc(pT_full, 1)

                def weigh_values(q):
                    Y = (q + 1) % 2
                    pe.wait_ge(pT_done, 2 * q + 2)
                    for h in range(H):
                        r, t = h // KC, h % KC
                        head = 2 * t + r
                        last = split(banks(Y, 2, 2)[r * DH:(r + 1) * DH, t * P:(t + 1) * P],
                                     lambda a, c: v16[:, q % 3, a, head * DH:(head + 1) * DH],
                                     lambda b, c: pT16[:, b, h, :], range(1))
                    last.then_inc(o_full, 1)

                def project_out(q):
                    Y = (q + 1) % 2
                    pe.wait_ge(a_wlo, 2)
                    pe.wait_ge(o_lo, q + 1)
                    last = split(banks(Y, 2, 1)[:, 0:D], lambda a, c: o16[:, a, c, :],
                                 lambda b, c: wo16[:, b, c, :], range(KC))
                    last.then_inc(y_full, 1)

                turn_x(0)
                queries_keys(0)
                values(0)
                scores(0)
                for q in range(PAIRS):
                    nxt = q + 1 < PAIRS
                    if nxt:
                        turn_x(q + 1)
                        queries_keys(q + 1)
                    if q:
                        turn_weights(q - 1, 0)
                    if nxt:
                        values(q + 1)
                    if q:
                        turn_weights(q - 1, 1)
                    if nxt:
                        scores(q + 1)
                    if q:
                        weigh_values(q - 1)
                        project_out(q - 1)
                turn_weights(PAIRS - 1, 0)
                turn_weights(PAIRS - 1, 1)
                weigh_values(PAIRS - 1)
                project_out(PAIRS - 1)

            @block.vector
            def _(dve):
                steps = [0]

                def link(ins):
                    ins.then_inc(a_step, 1)
                    steps[0] += 1
                    dve.wait_ge(a_step, steps[0])

                def weights(i):
                    w16, w32, _, _ = WEIGHTS[i]
                    hi, lo, w = w16[:, 0], w16[:, 1], w32[:]
                    if i:
                        hi, lo, w = flat_c(hi), flat_c(lo), flat_c(w)
                    dve.wait_ge(a_whi, i + 1)
                    dve.scalar_tensor_tensor(lo, w, WS, hi, ALU.mult, ALU.subtract).then_inc(a_wlo, 1)

                def norm_x(q):
                    dve.tensor_scalar(a_x[:], x_sb[:, q], a_mv[:, q, 0:1], a_r[:, q:q + 1],
                                      ALU.subtract, ALU.mult).then_inc(ln_x, 1)
                    dve.wait_ge(ln_x, q + 1)
                    dve.wait_ge(ln_hi, q + 1)
                    dve.tensor_tensor(a_x16[:, 1], a_x[:], a_x16[:, 0], ALU.subtract).then_inc(ln_lo, 1)

                def take_xT(q):
                    for i in range(2):
                        dve.wait_ge(xT_full, q * 2 + i + 1)
                        ins = dve.tensor_copy(xT16[:, i].rearrange("p a c n -> p (a c n)"), banks(q % 2, i, 1))
                    ins.then_inc(xT_done, 1)

                def low_proj(q, i):
                    X = q % 2
                    dst, b0 = ((q16, 2), (k16, 0), (v16, 2))[i]
                    dve.wait_ge(proj_hi, q * 3 + i + 1)
                    Z = X if i < 2 else q % 3
                    hi, lo = dst[:, Z, 0], dst[:, Z, 1]
                    if i < 2:
                        hi, lo = flat_c(hi), flat_c(lo)
                    dve.scalar_tensor_tensor(lo, banks(X, b0, 2), 1.0 / WS, hi, ALU.mult,
                                             ALU.subtract).then_inc(proj_lo, 1)

                def look_back(q):
                    dve.wait_ge(gs_ready, q + 1)
                    dve.tensor_tensor_scan(flat3(ar[:]), flat3(reset[:]), flat3(gs[:]), 0.0, ALU.mult,
                                           ALU.add).then_inc(gs_used, 1)
                    dve.wait_ge(gs_used, q + 1)
                    link(dve.tensor_scalar(ar[:], ar[:], float(N - 1), None, ALU.min))
                    link(dve.tensor_scalar(fl[:], ar[:], -0.5, MAGIC, ALU.add, ALU.add))
                    link(dve.tensor_tensor_scan(flat3(fl[:]), flat3(ones[:]), flat3(fl[:]), MAGIC, ALU.add, ALU.min))
                    link(dve.scalar_tensor_tensor(flat3(s16[:]), flat3(fl[:]), -1.0, flat3(vpos[:]), ALU.mult, ALU.add))
                    for i, bit in enumerate(BITS):
                        dve.tensor_scalar(mask[:, i], s16[:], bit, None, ALU.bitwise_and)
                    link(dve.scalar_tensor_tensor(flat3(ar[:]), flat3(fl[:]), -MAGIC, flat3(ar[:]), ALU.add,
                                                  ALU.subtract))


                def pick_blocks(q):
                    X = q % 2
                    dve.wait_ge(tab_diff, q + 1)
                    for i, bit in enumerate(BLOCKED):
                        for v in list(range(V1 - bit, bit, -bit)) + [bit]:
                            w = bit if v > bit else 1
                            for t in range(2):
                                ins = dve.copy_predicated(tab[:, X, t, :, v:v + w], mask[:, i, :, v:v + w],
                                                          tab[:, X, t, :, v - bit:v - bit + w])
                                if (bit, v) == (BLOCKED[-1], bit):
                                    ins.then_inc(blocks_picked, 1)
                                elif t == 1:
                                    link(ins)

                def pick_copy(q, i):
                    cur, bit = (q + i) % 2, COPIED[i]
                    for t in range(2):
                        n = 2 * (q * len(COPIED) + i) + t + 1
                        dve.wait_ge(tab_moved, n)
                        dve.copy_predicated(tab[:, 1 - cur, t, :, bit:V1], mask[:, len(BLOCKED) + i, :, bit:V1],
                                            tab[:, cur, t, :, 0:V1 - bit]).then_inc(tab_picked, 1)

                def logits(q):
                    X = q % 2
                    value, nxt = tab[:, X, 0, :, 1:V1], tab[:, X, 1, :, 1:V1]
                    L = lg[:, X]
                    sim = banks(X, 0, 2).rearrange("p (h n) -> p h n", n=N)
                    dve.wait_ge(tab_picked, 2 * (q + 1) * len(COPIED))
                    link(dve.tensor_tensor(nxt, ar[:, :, 1:V1], nxt, ALU.mult))
                    link(dve.tensor_tensor(value, value, nxt, ALU.subtract))
                    if q > 1:
                        dve.wait_ge(plo_done, 2 * (q - 1))
                    dve.scalar_tensor_tensor(L, sim, DH ** -0.5, value, ALU.mult, ALU.add).then_inc(sim_free, 1)
                    dve.wait_ge(sim_free, q + 1)
                    if q:
                        dve.wait_ge(a_exp, q)
                    link(dve.reduce_max(hs_[:, 0], L, AX_X))
                    dve.tensor_scalar(hs_[:, 0], hs_[:, 0], -1.0, None, ALU.mult).then_inc(logit_done, 1)

                def weigh(q):
                    X = q % 2
                    L = lg[:, X]
                    dve.wait_ge(a_exp, q + 1)
                    link(dve.reciprocal(hs_[:, 1], hs_[:, 1]))
                    dve.scalar_tensor_tensor(L, L, AS, hs_[:, 1].unsqueeze(2).broadcast_to([P, H, N]),
                                             ALU.mult, ALU.mult).then_inc(p32_done, 1)

                def low_o(q):
                    dve.wait_ge(o_hi, q + 1)
                    dve.scalar_tensor_tensor(flat_c(o16[:, 1]), banks((q + 1) % 2, 2, 2), 1.0 / AS, flat_c(o16[:, 0]),
                                             ALU.mult, ALU.subtract).then_inc(o_lo, 1)

                def residual(q):
                    dve.wait_ge(y_full, q + 1)
                    link(dve.scalar_tensor_tensor(tmp[:], banks((q + 1) % 2, 2, 1)[:, 0:D], 1.0 / WS, bo[:],
                                                  ALU.mult, ALU.add))
                    dve.tensor_tensor(x_sb[:, q], x_sb[:, q], tmp[:], ALU.add).then_inc(y_done, 1)

                for q in range(PAIRS):
                    dve.bn_stats(a_stats[:, q], x_sb[:, q]).then_inc(ln_st, 1)
                dve.wait_ge(ln_st, PAIRS)
                for q in range(PAIRS):
                    dve.bn_aggr(a_mv[:, q], a_stats[:, q]).then_inc(ln_mv, 1)
                dve.wait_ge(ln_mv, PAIRS)
                dve.wait_ge(ln_r, 1)
                norm_x(0)
                weights(0)
                take_xT(0)
                for i in range(3):
                    low_proj(0, i)
                norm_x(1)
                weights(1)
                dve.wait_ge(a_const, 6)
                take_xT(1)
                look_back(0)
                for q in range(PAIRS):
                    nxt = q + 1 < PAIRS
                    if nxt:
                        low_proj(q + 1, 0)
                        low_proj(q + 1, 1)
                    pick_blocks(q)
                    pick_copy(q, 0)
                    if nxt:
                        low_proj(q + 1, 2)
                    pick_copy(q, 1)
                    pick_copy(q, 2)
                    pick_copy(q, 3)
                    if q + 2 < PAIRS:
                        norm_x(q + 2)
                    if q:
                        low_o(q - 1)
                    logits(q)
                    if q:
                        residual(q - 1)
                    if q + 2 < PAIRS:
                        take_xT(q + 2)
                    if nxt:
                        look_back(q + 1)
                    weigh(q)
                low_o(PAIRS - 1)
                residual(PAIRS - 1)

        HSC = 16.0
        with ExitStack() as p3:
            f_stats = sb("f_stats", [P, PAIRS, 6], F32, p3)
            f_mv = sb("f_mv", [P, PAIRS, 2], F32, p3)
            f_r = sb("f_r", [P, PAIRS], F32, p3)
            f_x = sb("f_x", [P, PAIRS, D], F32, p3)
            f_x16 = sb("f_x16", [P, 2, PAIRS, D], F16, p3)
            f_xT = sb("f_xT", [P, 2, C, TOK], F16, p3)
            gw32 = sb("gw32", [P, C, E], F32, p3)
            gw16 = sb("gw16", [P, 2, C, E], F16, p3)
            lg8 = sb("lg8", [P, PAIRS, E], F32, p3)
            rank_i = sb("rank_i", [P, PAIRS, E], I32, p3)
            rank = sb("rank", [P, PAIRS, E], F32, p3)
            pick = sb("pick", [P, 2, PAIRS, E], F32, p3)
            eq = sb("eq", [P, PAIRS, E], F32, p3)
            top = sb("top", [P, 4, PAIRS], F32, p3)
            share = sb("share", [P, PAIRS, E], F32, p3)
            gu16 = sb("gu16", [P, 2, 2, C, 2 * F], F16, p3)
            dn16 = sb("dn16", [P, 2, 2, FC, D], F16, p3)
            th = sb("th", [P, 2, TOK], F32, p3)
            hid = sb("hid", [P, 2, TOK], F32, p3)
            hid16 = sb("hid16", [P, 4, 2, TOK], F16, p3)

            f_load = sem("f_load")
            f_const = sem("f_const")
            f_mvd = sem("f_mvd")
            f_pool = sem("f_pool")
            f_rr = sem("f_rr")
            f_xr = sem("f_xr")
            f_hi = sem("f_hi")
            f_lo = sem("f_lo")
            f_T = sem("f_T")
            f_Td = sem("f_Td")
            gw_hi = sem("gw_hi")
            gw_lo = sem("gw_lo")
            lg_full = sem("lg_full")
            e2_in = sem("e2_in")
            e2_out = sem("e2_out")
            w_hi = sem("w_hi")
            w_lo = sem("w_lo")
            gu_full = sem("gu_full")
            th_done = sem("th_done")
            sg_done = sem("sg_done")
            hid_done = sem("hid_done")
            hid_hi = sem("hid_hi")
            hid_lo = sem("hid_lo")
            ffn_done = sem("ffn_done")
            y3_done = sem("y3_done")
            f_step = sem("f_step")
            block = p3.enter_context(nc.Block())

            @block.sync
            def _(sp):
                sp.dma_start(gw32[:], gate_w.rearrange("(c p) n -> p c n", p=P)).then_inc(f_load, 16)
                with sp.Fori(0, E // 2 - 1) as i:
                    for s in range(2):
                        sp.wait_ge(w_lo, 4 * i + 2 * s + 2 + ONE)
                        sp.dma_start(gu32[:, s], gu_dram[i * 2 + 2 + s]).then_inc(w_loaded[s], 16)
                        sp.dma_start(dn32[:, s], dn_dram[i * 2 + 2 + s]).then_inc(w_loaded[s], 16)

            @block.gpsimd
            def _(pool):
                pool.iota(rank_i[:], pattern=[[0, PAIRS], [-1, E]], base=E, channel_multiplier=0).then_inc(f_const, 1)
                pool.wait_ge(f_const, 1)
                pool.tensor_copy(rank[:], rank_i[:]).then_inc(f_const, 1)
                pool.wait_ge(f_mvd, PAIRS)
                pool.tensor_scalar(f_r[:], f_mv[:, :, 1], 1.0, 1e-5, ALU.mult, ALU.add).then_inc(f_pool, 1)
                pool.wait_ge(f_pool, 1)
                pool.tensor_tensor(f_r[:], f_r[:], half[:, 0:PAIRS], ALU.pow).then_inc(f_rr, 1)

            @block.scalar
            def _(act):
                def split_first():
                    for w32, w16 in ((gu32, gu16), (dn32, dn16)):
                        act.activation(w16[:, 0, 0], w32[:, 0], ACT.Copy, scale=WS).then_inc(w_hi, 1)

                act.wait_ge(w_loaded[0], 32)
                split_first()
                act.wait_ge(f_load, 16)
                act.activation(gw16[:, 0], gw32[:], ACT.Copy, scale=WS).then_inc(gw_hi, 1)
                act.wait_ge(f_xr, PAIRS)
                act.activation(f_x16[:, 0], f_x[:], ACT.Copy).then_inc(f_hi, 1)
                act.wait_ge(e2_in, 1)
                act.activation(top[:, 3], top[:, 2], ACT.Exp).then_inc(e2_out, 1)

                def split_weights(n, s, staged, kind):
                    act.wait_ge(w_loaded[s], staged)
                    act.wait_ge(ffn_done, n)
                    w32, w16 = ((gu32, gu16), (dn32, dn16))[kind]
                    act.activation(w16[:, s, 0], w32[:, s], ACT.Copy, scale=WS).then_inc(w_hi, 1)

                def two_experts(i, more):
                    for k in range(2 * FC):
                        m = i * 2 * FC + k + 1
                        act.wait_ge(gu_full, m)
                        act.activation(th[:, k % 2], bank[:, 2 * (k % 2), :], ACT.Tanh,
                                       scale=0.5 / WS).then_inc(th_done, 1)
                        act.wait_ge(hid_done, m + 2)
                        act.activation(hid16[:, k % 4, 0], hid[:, k % 2], ACT.Copy).then_inc(hid_hi, 1)
                        if k in (1, 2):
                            split_weights(i * 2 + 2, 1, i * 32 + 32, k - 1)
                        if k in (FC + 1, FC + 2) and more:
                            split_weights(i * 2 + 3, 0, i * 32 + 64, k - FC - 1)

                with act.Fori(0, E // 2 - 1) as i:
                    two_experts(i, True)
                two_experts(E // 2 - 1, False)

            @block.tensor
            def _(pe):
                def split(out_, stat, mov, cs, first=True, last_=True):
                    todo = [(c, a, b) for c in cs for a, b in PASSES]
                    for i, (c, a, b) in enumerate(todo):
                        ins = pe.matmul(out_, stat(a, c), mov(b, c), start=(first and i == 0),
                                        stop=(last_ and i == len(todo) - 1))
                    return ins

                pe.wait_ge(f_lo, 1)
                for q in range(PAIRS):
                    for part in range(2):
                        for c in range(C):
                            o = (part * C + c) * P
                            last = pe.transpose(bank16[:, q, o:o + P], f_x16[:, part, q, c * P:(c + 1) * P],
                                                ident16[:])
                    last.then_inc(f_T, 1)
                pe.wait_ge(f_Td, PAIRS)
                pe.wait_ge(gw_lo, 1)
                for q in range(PAIRS):
                    last = split(bank[:, 4, q * E:(q + 1) * E], lambda a, c: f_xT[:, a, c, q * P:(q + 1) * P],
                                 lambda b, c: gw16[:, b, c, :], range(C))
                last.then_inc(lg_full, 1)
                pe.matmul(bank[:, 5, 0:E], f_xT[:, 0, 0, 0:P], gw16[:, 0, 0, :], start=True,
                          stop=True).then_inc(ffn_done, 2)

                def up(i, k):
                    s, j = k // FC, k % FC
                    if j == 0:
                        pe.wait_ge(w_lo, 4 * i + 2 * s + 1 + ONE)
                    pe.wait_ge(hid_done, i * 2 * FC + k + 1)
                    for u in range(2):
                        last = split(bank[:, 2 * (k % 2) + u, :],
                                     lambda a, c: gu16[:, s % 2, a, c, u * F + j * P:u * F + (j + 1) * P],
                                     lambda b, c: f_xT[:, b, c, :], range(C))
                    last.then_inc(gu_full, 1)

                def down(i, k):
                    s, j = k // FC, k % FC
                    if j == 0:
                        pe.wait_ge(w_lo, 4 * i + 2 * s + 2 + ONE)
                        pe.wait_ge(y3_done, i * 2 + s + ONE)
                    pe.wait_ge(hid_lo, i * 2 * FC + k + 1)
                    for t in range(PAIRS):
                        last = split(bank[:, 4 + t, 0:D], lambda a, c: hid16[:, k % 4, a, t * P:(t + 1) * P],
                                     lambda b, c: dn16[:, s, b, j, :], range(1), j == 0, j == FC - 1)
                    if j == FC - 1:
                        last.then_inc(ffn_done, 1)

                up(0, 0)
                up(0, 1)
                with pe.Fori(0, E // 2 - 1) as i:
                    for k in range(2 * FC):
                        up(i, k + 2)
                        down(i, k)
                for k in range(2 * FC):
                    if k + 2 < 2 * FC:
                        up(E // 2 - 1, k + 2)
                    down(E // 2 - 1, k)

            @block.vector
            def _(dve):
                credit(dve, w_lo, y3_done)
                steps = [0]

                def link(ins):
                    steps[0] += 1
                    ins.then_inc(f_step, 1)
                    dve.wait_ge(f_step, steps[0])

                for q in range(PAIRS):
                    last = dve.bn_stats(f_stats[:, q], x_sb[:, q])
                link(last)
                for q in range(PAIRS):
                    dve.bn_aggr(f_mv[:, q], f_stats[:, q]).then_inc(f_mvd, 1)
                dve.wait_ge(f_mvd, PAIRS)
                dve.wait_ge(f_rr, 1)
                for q in range(PAIRS):
                    dve.tensor_scalar(f_x[:, q], x_sb[:, q], f_mv[:, q, 0:1], f_r[:, q:q + 1],
                                      ALU.subtract, ALU.mult).then_inc(f_xr, 1)
                dve.wait_ge(f_xr, PAIRS)
                dve.wait_ge(f_hi, 1)
                dve.tensor_tensor(f_x16[:, 1], f_x[:], f_x16[:, 0], ALU.subtract).then_inc(f_lo, 1)
                dve.wait_ge(gw_hi, 1)
                dve.scalar_tensor_tensor(gw16[:, 1], gw32[:], WS, gw16[:, 0], ALU.mult, ALU.subtract).then_inc(gw_lo, 1)
                def split_weights(n, s, kind):
                    pat = "p c n -> p (c n)"
                    w32, w16 = ((gu32, gu16), (dn32, dn16))[kind]
                    dve.wait_ge(w_hi, 2 * (n - 1) + kind + 1)
                    dve.scalar_tensor_tensor(w16[:, s, 1].rearrange(pat), w32[:, s].rearrange(pat), WS,
                                             w16[:, s, 0].rearrange(pat), ALU.mult, ALU.subtract).then_inc(w_lo, 1)

                dve.memset(eq[:], 0.0).then_inc(hid_done, 2)
                split_weights(1, 0, 0)
                for q in range(PAIRS):
                    dve.wait_ge(f_T, q + 1)
                    dve.tensor_copy(f_xT[:, :, :, q * P:(q + 1) * P],
                                    bank16[:, q, 0:4 * P].rearrange("p (a c n) -> p a c n", a=2, c=C)).then_inc(f_Td, 1)
                split_weights(1, 0, 1)
                dve.wait_ge(lg_full, 1)
                dve.wait_ge(f_const, 2)
                link(dve.tensor_scalar(lg8[:].rearrange("p q e -> p (q e)"), bank[:, 4, 0:PAIRS * E], 1.0 / WS,
                                       None, ALU.mult))
                bc = lambda t: t.unsqueeze(2).broadcast_to([P, PAIRS, E])
                for r in range(2):
                    link(dve.reduce_max(top[:, r], lg8[:], AX_X))
                    link(dve.tensor_tensor(eq[:], lg8[:], bc(top[:, r]), ALU.is_equal))
                    link(dve.tensor_tensor(eq[:], eq[:], rank[:], ALU.mult))
                    link(dve.reduce_max(top[:, 2], eq[:], AX_X))
                    link(dve.tensor_tensor(pick[:, r], rank[:], bc(top[:, 2]), ALU.is_equal))
                    link(dve.scalar_tensor_tensor(lg8[:], pick[:, r], -3e38, lg8[:], ALU.mult, ALU.add))
                dve.tensor_tensor(top[:, 2], top[:, 1], top[:, 0], ALU.subtract).then_inc(e2_in, 1)
                dve.wait_ge(e2_out, 1)
                link(dve.tensor_scalar(top[:, 2], top[:, 3], 1.0, None, ALU.add))
                link(dve.reciprocal(top[:, 2], top[:, 2]))
                link(dve.tensor_tensor(share[:], pick[:, 1], bc(top[:, 3]), ALU.mult))
                link(dve.tensor_tensor(share[:], share[:], pick[:, 0], ALU.add))
                link(dve.scalar_tensor_tensor(share[:], share[:], 1.0 / (WS * HSC), bc(top[:, 2]),
                                              ALU.mult, ALU.mult))
                def two_experts(i, more, first=False):
                    for k in range(2 * FC):
                        m = i * 2 * FC + k + 1
                        dve.wait_ge(th_done, m)
                        dve.scalar_tensor_tensor(hid[:, k % 2], th[:, k % 2], 1.0, bank[:, 2 * (k % 2), :],
                                                 ALU.add, ALU.mult).then_inc(sg_done, 1)
                        dve.wait_ge(sg_done, m)
                        dve.scalar_tensor_tensor(hid[:, k % 2], hid[:, k % 2], HSC / (2 * WS * WS),
                                                 bank[:, 2 * (k % 2) + 1, :], ALU.mult, ALU.mult).then_inc(hid_done, 1)
                        dve.wait_ge(hid_done, m + 2)
                        dve.wait_ge(hid_hi, m)
                        dve.tensor_tensor(hid16[:, k % 4, 1], hid[:, k % 2], hid16[:, k % 4, 0],
                                          ALU.subtract).then_inc(hid_lo, 1)
                        if k in (1, 2):
                            split_weights(i * 2 + 2, 1, k - 1)
                        if k in (FC + 1, FC + 2) and more:
                            split_weights(i * 2 + 3, 0, k - FC - 1)
                        if k == 0 and not first:
                            add_expert(i * 2 - 1)
                        if k == FC:
                            add_expert(i * 2)

                def add_expert(e):
                    dve.wait_ge(ffn_done, e + 3)
                    dve.wait_ge(y3_done, e + ONE)
                    for t in range(PAIRS):
                        last = dve.scalar_tensor_tensor(x_sb[:, t], bank[:, 4 + t, 0:D],
                                                        share[:, t, bass.ds(e, 1)], x_sb[:, t],
                                                        ALU.mult, ALU.add)
                    last.then_inc(y3_done, 1)

                two_experts(0, True, True)
                with dve.Fori(1, E // 2 - 1) as i:
                    two_experts(i, True)
                two_experts(E // 2 - 1, False)
                add_expert(E - 1)

        stored = sem("stored")
        with ExitStack() as p4:
            block = p4.enter_context(nc.Block())

            @block.sync
            def _(sp):
                sp.dma_start(out.rearrange("b k d -> (b k) d").rearrange("(q p) d -> p q d", p=P),
                             x_sb[:]).then_inc(stored, 16)
                sp.wait_ge(stored, 16)


_INS = ['x', 'ctx_1024', 'L0_xattn_Wq', 'L0_xattn_Wk', 'L0_xattn_Wv', 'L0_xattn_gru_wih',
        'L0_xattn_gru_whh', 'L0_xattn_gru_bih', 'L0_xattn_gru_bhh', 'L0_xattn_slot_norm_w',
        'L0_xattn_input_norm_w', 'L0_attn_Wq', 'L0_attn_Wkv', 'L0_attn_Wout', 'L0_attn_b_out',
        'L0_attn_pos_emb', 'L0_ffn_gate_w', 'L0_ffn_gate_up_w', 'L0_ffn_down_w']


def kernel(**inputs):
    import numpy as _np
    import concourse.bacc as _bacc
    from concourse.bass_utils import run_bass_kernel_spmd as _run

    nc = _bacc.Bacc("TRN2", target_bir_lowering=False, num_devices=1)
    arrays, args = {}, []
    for name in _INS:
        a = _np.ascontiguousarray(inputs[name])
        arrays[f"in_{name}_dram"] = a
        args.append(nc.dram_tensor(f"in_{name}_dram", a.shape, mybir.dt.from_np(a.dtype), kind="ExternalInput").ap())
    shape = tuple(inputs['x'].shape)
    args.append(nc.dram_tensor("out_dram", shape, F32, kind="ExternalOutput").ap())
    perceiver_kernel(nc, *args)
    r = _run(nc, [arrays], core_ids=[0])
    return r.results[0]["out_dram"]
```
